# Optimizing a Trainium2 kernel written in Bass

```python
import numpy as np
import jax
import jax.numpy as jnp

def _softmax(x, axis=-1):
    return jax.nn.softmax(x, axis=axis)
def _gelu(x):
    return jax.nn.gelu(x, approximate=True)
def _silu(x):
    return jax.nn.silu(x)
def _sigmoid(x):
    return jax.nn.sigmoid(x)
def _layernorm(x, axis=-1, eps=1e-5):
    m = jnp.mean(x, axis=axis, keepdims=True)
    v = jnp.var(x, axis=axis, keepdims=True)
    return (x - m) / jnp.sqrt(v + eps)
def _scatter_add(tgt, idx, src, axis=0):
    return tgt.at[idx].add(src)
def _segment_sum(src, seg, n):
    return jax.ops.segment_sum(src, seg, n)

kernel_name = 'mk_conv_preact_d2_conv_nchw512_11ec51'

def setup_inputs(seed: int = 0):
    np.random.seed(seed)
    _w = jnp.asarray
    def _rec_inputs():
        import jax
        import jax.numpy as jnp
        _gk = jax.random.key(seed)
        x = 7.22e-05 + 1 * jax.random.normal(jax.random.fold_in(_gk, 1), (4, 512, 64, 64), jnp.float32)
        return x
    x = _rec_inputs()
    def _L0_conv_setup():
        import jax, jax.numpy as jnp
        from jax import lax
        import numpy as np
        INPUT_DIM = 512
        OUTPUT_DIM = 512
        D_STATE = 16
        D_CONV = 4
        EXPAND = 2
        D_MODEL = INPUT_DIM // 4
        D_INNER = EXPAND * D_MODEL
        DT_RANK = (D_MODEL + 15) // 16
        EPS = 1e-05

        def layer_norm(x, g, b):
            mu = jnp.mean(x, axis=-1, keepdims=True)
            var = jnp.mean((x - mu) ** 2, axis=-1, keepdims=True)
            return (x - mu) * lax.rsqrt(var + EPS) * g + b

        def mamba(x, in_proj_w, conv_w, conv_b, x_proj_w, dt_proj_w, dt_proj_b, A_log, D_param, out_proj_w):
            Beff, L, _ = x.shape
            xz = jnp.einsum('bld,ed->ble', x, in_proj_w)
            xi, z = jnp.split(xz, 2, axis=-1)
            xc = lax.conv_general_dilated(xi.transpose(0, 2, 1), conv_w[:, None, :], (1,), [(D_CONV - 1, 0)], feature_group_count=D_INNER)
            xc = jax.nn.silu(xc + conv_b[None, :, None]).transpose(0, 2, 1)
            dbc = jnp.einsum('bld,ed->ble', xc, x_proj_w)
            dt = dbc[..., :DT_RANK]
            Bs = dbc[..., DT_RANK:DT_RANK + D_STATE]
            Cs = dbc[..., DT_RANK + D_STATE:]
            dt = jax.nn.softplus(jnp.einsum('blr,er->ble', dt, dt_proj_w) + dt_proj_b)
            A = -jnp.exp(A_log)

            def step(h, inp):
                dt_t, B_t, C_t, x_t = inp
                dA = jnp.exp(dt_t[:, :, None] * A)
                h = dA * h + (dt_t * x_t)[:, :, None] * B_t[:, None, :]
                y = jnp.einsum('bds,bs->bd', h, C_t)
                return (h, y)
            h0 = jnp.zeros((Beff, D_INNER, D_STATE), x.dtype)
            _, ys = lax.scan(step, h0, (dt.transpose(1, 0, 2), Bs.transpose(1, 0, 2), Cs.transpose(1, 0, 2), xc.transpose(1, 0, 2)))
            y = ys.transpose(1, 0, 2) + xc * D_param
            y = y * jax.nn.silu(z)
            return jnp.einsum('bld,od->blo', y, out_proj_w)
        key = jax.random.key(seed)
        ks = jax.random.split(key, 10)
        inp = {'x': jax.random.normal(ks[0], (4, INPUT_DIM, 64, 64), jnp.float32), 'norm_g': jnp.ones((INPUT_DIM,), jnp.float32), 'norm_b': jnp.zeros((INPUT_DIM,), jnp.float32), 'in_proj_w': jax.random.normal(ks[1], (2 * D_INNER, D_MODEL), jnp.float32) * 0.02, 'conv_w': jax.random.normal(ks[2], (D_INNER, D_CONV), jnp.float32) * 0.2, 'conv_b': jnp.zeros((D_INNER,), jnp.float32), 'x_proj_w': jax.random.normal(ks[3], (DT_RANK + 2 * D_STATE, D_INNER), jnp.float32) * 0.02, 'dt_proj_w': jax.random.normal(ks[4], (D_INNER, DT_RANK), jnp.float32) * 0.1, 'dt_proj_b': jnp.full((D_INNER,), -2.0, jnp.float32), 'A_log': jnp.log(jnp.broadcast_to(jnp.arange(1, D_STATE + 1, dtype=jnp.float32), (D_INNER, D_STATE))), 'D_param': jnp.ones((D_INNER,), jnp.float32), 'out_proj_w': jax.random.normal(ks[5], (D_MODEL, D_INNER), jnp.float32) * 0.02, 'proj_w': jax.random.normal(ks[6], (OUTPUT_DIM, INPUT_DIM), jnp.float32) * 0.02, 'proj_b': jnp.zeros((OUTPUT_DIM,), jnp.float32), 'skip_scale': jnp.ones((1,), jnp.float32)}
        return inp
    _L0_conv_all = _L0_conv_setup()
    _L0_conv_in = {k: v for k, v in _L0_conv_all.items() if k in ('norm_g', 'norm_b', 'in_proj_w', 'conv_w', 'conv_b', 'x_proj_w', 'dt_proj_w', 'dt_proj_b', 'A_log', 'D_param', 'out_proj_w', 'proj_w', 'proj_b', 'skip_scale', )}
    del _L0_conv_all

    def _L1_conv_setup():
        import jax, jax.numpy as jnp
        import numpy as np
        C = 512
        G = 16
        Cg = C // G
        K = 3
        P = K * K
        PAD = 1
        STRIDE = 1
        DIL = 1
        DWK = 3
        OFFSET_SCALE = 1.0
        LN_EPS = 1e-05

        def _dcnv3_core(x, offset, mask):
            N, H, W, _ = x.shape
            Hin, Win = (H + 2 * PAD, W + 2 * PAD)
            Hout, Wout = (H, W)
            xpad = jnp.pad(x, ((0, 0), (PAD, PAD), (PAD, PAD), (0, 0)))
            base = DIL * (K - 1) // 2 + 0.5
            ref_y = (base + jnp.arange(Hout, dtype=jnp.float32) * STRIDE) / Hin
            ref_x = (base + jnp.arange(Wout, dtype=jnp.float32) * STRIDE) / Win
            ref = jnp.stack(jnp.broadcast_arrays(ref_x[None, :], ref_y[:, None]), -1)
            g1 = jnp.arange(K, dtype=jnp.float32) * DIL - DIL * (K - 1) // 2
            gxx, gyy = jnp.meshgrid(g1 / Win, g1 / Hin, indexing='ij')
            grid = jnp.stack([gxx, gyy], -1).reshape(P, 2)
            off = offset.reshape(N, Hout, Wout, G, P, 2)
            norm = jnp.array([Win, Hin], jnp.float32)
            loc = ref[None, :, :, None, None, :] + grid * OFFSET_SCALE + off * OFFSET_SCALE / norm
            px = loc[..., 0] * Win - 0.5
            py = loc[..., 1] * Hin - 0.5
            xg = xpad.reshape(N, Hin, Win, G, Cg).transpose(0, 3, 1, 2, 4).reshape(N * G, Hin, Win, Cg)
            pxg = px.transpose(0, 3, 1, 2, 4).reshape(N * G, Hout, Wout, P)
            pyg = py.transpose(0, 3, 1, 2, 4).reshape(N * G, Hout, Wout, P)
            mg = mask.transpose(0, 3, 1, 2, 4).reshape(N * G, Hout, Wout, P)

            def bilin(img, bx, by, m):
                x0 = jnp.floor(bx)
                y0 = jnp.floor(by)
                wx = (bx - x0)[..., None]
                wy = (by - y0)[..., None]
                x0i = x0.astype(jnp.int32)
                y0i = y0.astype(jnp.int32)

                def g(yy, xx):
                    valid = (yy >= 0) & (yy < Hin) & (xx >= 0) & (xx < Win)
                    v = img[jnp.clip(yy, 0, Hin - 1), jnp.clip(xx, 0, Win - 1)]
                    return v * valid[..., None]
                v00 = g(y0i, x0i)
                v01 = g(y0i, x0i + 1)
                v10 = g(y0i + 1, x0i)
                v11 = g(y0i + 1, x0i + 1)
                samp = (v00 * (1 - wx) + v01 * wx) * (1 - wy) + (v10 * (1 - wx) + v11 * wx) * wy
                return jnp.einsum('hwpc,hwp->hwc', samp, m)
            out = jax.vmap(bilin)(xg, pxg, pyg, mg)
            return out.reshape(N, G, Hout, Wout, Cg).transpose(0, 2, 3, 1, 4).reshape(N, Hout, Wout, C)
        key = jax.random.key(seed)
        ks = jax.random.split(key, 10)
        N, H, W = (2, 64, 64)
        sc = 1.0 / np.sqrt(C)
        return {'x': jax.random.normal(ks[0], (N, C, H, W), jnp.float32), 'dw_w': jax.random.normal(ks[1], (C, 1, DWK, DWK), jnp.float32) * 0.1, 'dw_b': jax.random.normal(ks[2], (C,), jnp.float32) * 0.02, 'ln_g': jnp.ones((C,), jnp.float32), 'ln_b': jnp.zeros((C,), jnp.float32), 'off_w': jax.random.normal(ks[3], (C, G * P * 2), jnp.float32) * 0.01, 'off_b': jax.random.normal(ks[4], (G * P * 2,), jnp.float32) * 0.01, 'mask_w': jax.random.normal(ks[5], (C, G * P), jnp.float32) * 0.01, 'mask_b': jnp.zeros((G * P,), jnp.float32), 'in_w': jax.random.normal(ks[6], (C, C), jnp.float32) * sc, 'in_b': jnp.zeros((C,), jnp.float32), 'out_w': jax.random.normal(ks[7], (C, C), jnp.float32) * sc, 'out_b': jnp.zeros((C,), jnp.float32)}
    _L1_conv_all = _L1_conv_setup()
    _L1_conv_in = {k: v for k, v in _L1_conv_all.items() if k in ('dw_w', 'dw_b', 'ln_g', 'ln_b', 'off_w', 'off_b', 'mask_w', 'mask_b', 'in_w', 'in_b', 'out_w', 'out_b', )}
    del _L1_conv_all

    return {
        "x": x,
        "L0_conv_norm_g": _L0_conv_in["norm_g"],
        "L0_conv_norm_b": _L0_conv_in["norm_b"],
        "L0_conv_in_proj_w": _L0_conv_in["in_proj_w"],
        "L0_conv_conv_w": _L0_conv_in["conv_w"],
        "L0_conv_conv_b": _L0_conv_in["conv_b"],
        "L0_conv_x_proj_w": _L0_conv_in["x_proj_w"],
        "L0_conv_dt_proj_w": _L0_conv_in["dt_proj_w"],
        "L0_conv_dt_proj_b": _L0_conv_in["dt_proj_b"],
        "L0_conv_A_log": _L0_conv_in["A_log"],
        "L0_conv_D_param": _L0_conv_in["D_param"],
        "L0_conv_out_proj_w": _L0_conv_in["out_proj_w"],
        "L0_conv_proj_w": _L0_conv_in["proj_w"],
        "L0_conv_proj_b": _L0_conv_in["proj_b"],
        "L0_conv_skip_scale": _L0_conv_in["skip_scale"],
        "L1_conv_dw_w": _L1_conv_in["dw_w"],
        "L1_conv_dw_b": _L1_conv_in["dw_b"],
        "L1_conv_ln_g": _L1_conv_in["ln_g"],
        "L1_conv_ln_b": _L1_conv_in["ln_b"],
        "L1_conv_off_w": _L1_conv_in["off_w"],
        "L1_conv_off_b": _L1_conv_in["off_b"],
        "L1_conv_mask_w": _L1_conv_in["mask_w"],
        "L1_conv_mask_b": _L1_conv_in["mask_b"],
        "L1_conv_in_w": _L1_conv_in["in_w"],
        "L1_conv_in_b": _L1_conv_in["in_b"],
        "L1_conv_out_w": _L1_conv_in["out_w"],
        "L1_conv_out_b": _L1_conv_in["out_b"],
    }

def reference(x, L0_conv_norm_g, L0_conv_norm_b, L0_conv_in_proj_w, L0_conv_conv_w, L0_conv_conv_b, L0_conv_x_proj_w, L0_conv_dt_proj_w, L0_conv_dt_proj_b, L0_conv_A_log, L0_conv_D_param, L0_conv_out_proj_w, L0_conv_proj_w, L0_conv_proj_b, L0_conv_skip_scale, L1_conv_dw_w, L1_conv_dw_b, L1_conv_ln_g, L1_conv_ln_b, L1_conv_off_w, L1_conv_off_b, L1_conv_mask_w, L1_conv_mask_b, L1_conv_in_w, L1_conv_in_b, L1_conv_out_w, L1_conv_out_b):
    import jax
    import jax.numpy as jnp
    def _L0_conv_ref(x, norm_g, norm_b, in_proj_w, conv_w, conv_b, x_proj_w, dt_proj_w, dt_proj_b, A_log, D_param, out_proj_w, proj_w, proj_b, skip_scale):
        import jax, jax.numpy as jnp
        from jax import lax
        import numpy as np
        INPUT_DIM = 512
        OUTPUT_DIM = 512
        D_STATE = 16
        D_CONV = 4
        EXPAND = 2
        D_MODEL = INPUT_DIM // 4
        D_INNER = EXPAND * D_MODEL
        DT_RANK = (D_MODEL + 15) // 16
        EPS = 1e-05

        def layer_norm(x, g, b):
            mu = jnp.mean(x, axis=-1, keepdims=True)
            var = jnp.mean((x - mu) ** 2, axis=-1, keepdims=True)
            return (x - mu) * lax.rsqrt(var + EPS) * g + b

        def mamba(x, in_proj_w, conv_w, conv_b, x_proj_w, dt_proj_w, dt_proj_b, A_log, D_param, out_proj_w):
            Beff, L, _ = x.shape
            xz = jnp.einsum('bld,ed->ble', x, in_proj_w)
            xi, z = jnp.split(xz, 2, axis=-1)
            xc = lax.conv_general_dilated(xi.transpose(0, 2, 1), conv_w[:, None, :], (1,), [(D_CONV - 1, 0)], feature_group_count=D_INNER)
            xc = jax.nn.silu(xc + conv_b[None, :, None]).transpose(0, 2, 1)
            dbc = jnp.einsum('bld,ed->ble', xc, x_proj_w)
            dt = dbc[..., :DT_RANK]
            Bs = dbc[..., DT_RANK:DT_RANK + D_STATE]
            Cs = dbc[..., DT_RANK + D_STATE:]
            dt = jax.nn.softplus(jnp.einsum('blr,er->ble', dt, dt_proj_w) + dt_proj_b)
            A = -jnp.exp(A_log)

            def step(h, inp):
                dt_t, B_t, C_t, x_t = inp
                dA = jnp.exp(dt_t[:, :, None] * A)
                h = dA * h + (dt_t * x_t)[:, :, None] * B_t[:, None, :]
                y = jnp.einsum('bds,bs->bd', h, C_t)
                return (h, y)
            h0 = jnp.zeros((Beff, D_INNER, D_STATE), x.dtype)
            _, ys = lax.scan(step, h0, (dt.transpose(1, 0, 2), Bs.transpose(1, 0, 2), Cs.transpose(1, 0, 2), xc.transpose(1, 0, 2)))
            y = ys.transpose(1, 0, 2) + xc * D_param
            y = y * jax.nn.silu(z)
            return jnp.einsum('bld,od->blo', y, out_proj_w)
        B, C, H, W = x.shape
        L = H * W
        xf = x.reshape(B, C, L).transpose(0, 2, 1)
        xn = layer_norm(xf, norm_g, norm_b)
        chunks = xn.reshape(B, L, 4, D_MODEL).transpose(2, 0, 1, 3).reshape(4 * B, L, D_MODEL)
        ym = mamba(chunks, in_proj_w, conv_w, conv_b, x_proj_w, dt_proj_w, dt_proj_b, A_log, D_param, out_proj_w)
        ym = ym + skip_scale * chunks
        y = ym.reshape(4, B, L, D_MODEL).transpose(1, 2, 0, 3).reshape(B, L, C)
        y = layer_norm(y, norm_g, norm_b)
        y = jnp.einsum('blc,oc->blo', y, proj_w) + proj_b
        return y.transpose(0, 2, 1).reshape(B, OUTPUT_DIM, H, W)

    def _L1_conv_ref(x, dw_w, dw_b, ln_g, ln_b, off_w, off_b, mask_w, mask_b, in_w, in_b, out_w, out_b):
        import jax, jax.numpy as jnp
        import numpy as np
        C = 512
        G = 16
        Cg = C // G
        K = 3
        P = K * K
        PAD = 1
        STRIDE = 1
        DIL = 1
        DWK = 3
        OFFSET_SCALE = 1.0
        LN_EPS = 1e-05

        def _dcnv3_core(x, offset, mask):
            N, H, W, _ = x.shape
            Hin, Win = (H + 2 * PAD, W + 2 * PAD)
            Hout, Wout = (H, W)
            xpad = jnp.pad(x, ((0, 0), (PAD, PAD), (PAD, PAD), (0, 0)))
            base = DIL * (K - 1) // 2 + 0.5
            ref_y = (base + jnp.arange(Hout, dtype=jnp.float32) * STRIDE) / Hin
            ref_x = (base + jnp.arange(Wout, dtype=jnp.float32) * STRIDE) / Win
            ref = jnp.stack(jnp.broadcast_arrays(ref_x[None, :], ref_y[:, None]), -1)
            g1 = jnp.arange(K, dtype=jnp.float32) * DIL - DIL * (K - 1) // 2
            gxx, gyy = jnp.meshgrid(g1 / Win, g1 / Hin, indexing='ij')
            grid = jnp.stack([gxx, gyy], -1).reshape(P, 2)
            off = offset.reshape(N, Hout, Wout, G, P, 2)
            norm = jnp.array([Win, Hin], jnp.float32)
            loc = ref[None, :, :, None, None, :] + grid * OFFSET_SCALE + off * OFFSET_SCALE / norm
            px = loc[..., 0] * Win - 0.5
            py = loc[..., 1] * Hin - 0.5
            xg = xpad.reshape(N, Hin, Win, G, Cg).transpose(0, 3, 1, 2, 4).reshape(N * G, Hin, Win, Cg)
            pxg = px.transpose(0, 3, 1, 2, 4).reshape(N * G, Hout, Wout, P)
            pyg = py.transpose(0, 3, 1, 2, 4).reshape(N * G, Hout, Wout, P)
            mg = mask.transpose(0, 3, 1, 2, 4).reshape(N * G, Hout, Wout, P)

            def bilin(img, bx, by, m):
                x0 = jnp.floor(bx)
                y0 = jnp.floor(by)
                wx = (bx - x0)[..., None]
                wy = (by - y0)[..., None]
                x0i = x0.astype(jnp.int32)
                y0i = y0.astype(jnp.int32)

                def g(yy, xx):
                    valid = (yy >= 0) & (yy < Hin) & (xx >= 0) & (xx < Win)
                    v = img[jnp.clip(yy, 0, Hin - 1), jnp.clip(xx, 0, Win - 1)]
                    return v * valid[..., None]
                v00 = g(y0i, x0i)
                v01 = g(y0i, x0i + 1)
                v10 = g(y0i + 1, x0i)
                v11 = g(y0i + 1, x0i + 1)
                samp = (v00 * (1 - wx) + v01 * wx) * (1 - wy) + (v10 * (1 - wx) + v11 * wx) * wy
                return jnp.einsum('hwpc,hwp->hwc', samp, m)
            out = jax.vmap(bilin)(xg, pxg, pyg, mg)
            return out.reshape(N, G, Hout, Wout, Cg).transpose(0, 2, 3, 1, 4).reshape(N, Hout, Wout, C)
        N, _, H, W = x.shape
        inp = jnp.transpose(x, (0, 2, 3, 1))
        xproj = inp @ in_w + in_b
        x1 = jax.lax.conv_general_dilated(x, dw_w, (1, 1), [((DWK - 1) // 2, (DWK - 1) // 2)] * 2, feature_group_count=C, dimension_numbers=('NCHW', 'OIHW', 'NCHW'))
        x1 = jnp.transpose(x1, (0, 2, 3, 1)) + dw_b
        mu = x1.mean(-1, keepdims=True)
        var = ((x1 - mu) ** 2).mean(-1, keepdims=True)
        x1 = (x1 - mu) / jnp.sqrt(var + LN_EPS) * ln_g + ln_b
        x1 = jax.nn.gelu(x1, approximate=False)
        offset = x1 @ off_w + off_b
        mask = jax.nn.softmax((x1 @ mask_w + mask_b).reshape(N, H, W, G, P), -1)
        out = _dcnv3_core(xproj, offset, mask)
        out = out @ out_w + out_b
        return jnp.transpose(out, (0, 3, 1, 2))

    def _gn(v, G=32, eps=1e-5):
        B_, C_, H_, W_ = v.shape
        g = v.reshape(B_, G, C_ // G, H_, W_)
        m = jnp.mean(g, axis=(2, 3, 4), keepdims=True)
        s = jnp.var(g, axis=(2, 3, 4), keepdims=True)
        return ((g - m) / jnp.sqrt(s + eps)).reshape(v.shape)

    def _ln_c(v, eps=1e-6):
        m = jnp.mean(v, axis=1, keepdims=True)
        s = jnp.var(v, axis=1, keepdims=True)
        return (v - m) / jnp.sqrt(s + eps)

    def _ln_t(v, eps=1e-5):
        m = jnp.mean(v, axis=-1, keepdims=True)
        s = jnp.var(v, axis=-1, keepdims=True)
        return (v - m) / jnp.sqrt(s + eps)

    def _to_tokens(v):
        B_, C_, H_, W_ = v.shape
        return v.reshape(B_, C_, H_ * W_).transpose(0, 2, 1)
    def _from_tokens(t, like):
        B_, C_, H_, W_ = like.shape
        return t.transpose(0, 2, 1).reshape(B_, C_, H_, W_)

    x = x + _L0_conv_ref(_gn(x), L0_conv_norm_g, L0_conv_norm_b, L0_conv_in_proj_w, L0_conv_conv_w, L0_conv_conv_b, L0_conv_x_proj_w, L0_conv_dt_proj_w, L0_conv_dt_proj_b, L0_conv_A_log, L0_conv_D_param, L0_conv_out_proj_w, L0_conv_proj_w, L0_conv_proj_b, L0_conv_skip_scale)
    x = x + _L1_conv_ref(_gn(x), L1_conv_dw_w, L1_conv_dw_b, L1_conv_ln_g, L1_conv_ln_b, L1_conv_off_w, L1_conv_off_b, L1_conv_mask_w, L1_conv_mask_b, L1_conv_in_w, L1_conv_in_b, L1_conv_out_w, L1_conv_out_b)
    return x


_drawn_inputs = setup_inputs


def setup_inputs(seed=0):
    import zlib

    import numpy as np

    out = dict(_drawn_inputs(seed))
    spreads = {'L0_conv_norm_g': (1.0, 0.2),
     'L0_conv_norm_b': (0.0, 0.1),
     'L0_conv_conv_b': (0.0, 0.8),
     'L0_conv_dt_proj_b': (-2.0, 0.6),
     'L0_conv_D_param': (1.0, 0.6),
     'L0_conv_proj_b': (0.0, 0.1),
     'L1_conv_ln_g': (1.0, 0.6),
     'L1_conv_ln_b': (0.0, 0.8),
     'L1_conv_in_b': (0.0, 0.1),
     'L1_conv_out_b': (0.0, 0.1)}
    factors = {'L0_conv_in_proj_w': 8.0,
     'L0_conv_conv_w': 8.0,
     'L0_conv_x_proj_w': 8.0,
     'L0_conv_dt_proj_w': 8.0,
     'L0_conv_A_log': 8.0,
     'L0_conv_out_proj_w': 8.0,
     'L1_conv_dw_b': 8.0,
     'L1_conv_off_b': 8.0}
    for name, (base, spread) in spreads.items():
        noise = np.random.default_rng([zlib.crc32(name.encode()), seed]).standard_normal(out[name].shape)
        drawn = base * np.exp(spread * noise) if base else spread * noise
        out[name] = jnp.asarray(drawn.astype(out[name].dtype))
    for name, factor in factors.items():
        out[name] = (out[name] * factor).astype(out[name].dtype)
    return out
```

```python
import numpy as np
import concourse.bass as bass
from concourse import mybir
from contextlib import ExitStack

F32 = mybir.dt.float32
BF16 = mybir.dt.bfloat16
I32 = mybir.dt.int32
ALU = mybir.AluOpType
ACT = mybir.ActivationFunctionType
AX = mybir.AxisListType

B, C, HW = 4, 512, 4096
IMG = 64
P = 128
K = C // P
T = 512
NT = HW // T
SEQ = B * K
GN_EPS, LN_EPS = 1e-5, 1e-5
NORM_G, NORM_B, PROJ_B, DW_B, LN_G, LN_B, IN_B, OUT_B = range(8)


def over_slabs(ap):
    return ap.unsqueeze(1).broadcast_to([P, K, T])


class LayerNorm:

    def __init__(self, nc, name, sb, pb, sem, x, ones):
        self.nc, self.x, self.ones = nc, x, ones
        self.sq = sb(name + "_sq", [P, 2, K, T], F32)
        self.stat = pb(name + "_stat", [P, 2, T], F32)
        self.rstd = sb(name + "_rstd", [P, 2, T], F32)
        self.input_ready = sem(name + "_input_ready")
        self.mean_ready = sem(name + "_mean_ready")
        self.centred = sem(name + "_centred")
        self.squared = sem(name + "_squared")
        self.var_ready = sem(name + "_var_ready")
        self.std_ready = sem(name + "_std_ready")
        self.rstd_ready = sem(name + "_rstd_ready")
        self.scaled = sem(name + "_scaled")

    def pe_mean(self, pe, u, c):
        pe.wait_ge(self.input_ready, c + 1)
        for k in range(K):
            mm = self.nc.tensor.matmul(self.stat[:, u, :], self.ones[:, :], self.x[:, u, k, :], start=k == 0, stop=k == K - 1)
        mm.then_inc(self.mean_ready, 1)

    def dve_centre(self, dve, u, c):
        dve.wait_ge(self.mean_ready, c + 1)
        self.nc.vector.tensor_tensor(self.x[:, u], self.x[:, u], over_slabs(self.stat[:, u, :]), ALU.subtract).then_inc(self.centred, 1)

    def act_square(self, act, u, c):
        act.wait_ge(self.centred, c + 1)
        self.nc.scalar.activation(self.sq[:, u], self.x[:, u], ACT.Square).then_inc(self.squared, 1)

    def pe_var(self, pe, u, c):
        pe.wait_ge(self.squared, c + 1)
        for k in range(K):
            mm = self.nc.tensor.matmul(self.stat[:, u, :], self.ones[:, :], self.sq[:, u, k, :], start=k == 0, stop=k == K - 1)
        mm.then_inc(self.var_ready, 1)

    def act_std(self, act, u, c, eps):
        act.wait_ge(self.var_ready, c + 1)
        self.nc.scalar.activation(self.rstd[:, u, :], self.stat[:, u, :], ACT.Sqrt, bias=eps).then_inc(self.std_ready, 1)

    def dve_scale(self, dve, u, c):
        dve.wait_ge(self.std_ready, c + 1)
        self.nc.vector.reciprocal(self.rstd[:, u, :], self.rstd[:, u, :]).then_inc(self.rstd_ready, 1)
        dve.wait_ge(self.rstd_ready, c + 1)
        self.nc.vector.tensor_tensor(self.x[:, u], self.x[:, u], over_slabs(self.rstd[:, u, :]), ALU.mult).then_inc(self.scaled, 1)


def finish_group_norm(nc, sb, pb, sem, block, name, stats, group_avg, ready, eps_col):
    mv = sb(name + "_mv", [P, SEQ, 2], F32)
    mom = sb(name + "_mom", [P, 2, SEQ], F32)
    grp = sb(name + "_grp", [P, 2, SEQ], F32)
    aff = sb(name + "_aff", [P, 2, SEQ], F32)
    grp_ps = pb(name + "_grp_ps", [P, 2, SEQ], F32)
    step = sem(name + "_step")
    averaged = sem(name + "_averaged")
    rooted = sem(name + "_rooted")

    def dve_part(dve):
        n = [0]

        def link(ins):
            n[0] += 1
            ins.then_inc(step, 1)
            dve.wait_ge(step, n[0])

        if ready is not None:
            dve.wait_ge(*ready)
        for r in range(SEQ):
            nc.vector.bn_aggr(mv[:, r, :], stats[:, r, :, :].rearrange("p a b -> p (a b)")).then_inc(step, 1)
        n[0] = SEQ
        dve.wait_ge(step, SEQ)
        link(nc.vector.tensor_copy(mom[:, 0, :], mv[:, :, 0]))
        link(nc.vector.tensor_tensor(mom[:, 1, :], mv[:, :, 0], mv[:, :, 0], ALU.mult))
        link(nc.vector.tensor_tensor(mom[:, 1, :], mom[:, 1, :], mv[:, :, 1], ALU.add))
        done_mom = n[0]
        dve.wait_ge(averaged, 1)
        link(nc.vector.tensor_copy(grp[:, :, :], grp_ps[:, :, :]))
        link(nc.vector.tensor_tensor(aff[:, 0, :], grp[:, 0, :], grp[:, 0, :], ALU.mult))
        link(nc.vector.tensor_tensor(aff[:, 0, :], grp[:, 1, :], aff[:, 0, :], ALU.subtract))
        done_var = n[0]
        dve.wait_ge(rooted, 1)
        link(nc.vector.reciprocal(aff[:, 0, :], aff[:, 0, :]))
        link(nc.vector.tensor_tensor(aff[:, 1, :], grp[:, 0, :], aff[:, 0, :], ALU.mult))
        link(nc.vector.tensor_scalar(aff[:, 1, :], aff[:, 1, :], -1.0, None, ALU.mult))
        return done_mom, done_var

    dones = (SEQ + 3, SEQ + 6, SEQ + 9)

    def pe_part(pe):
        pe.wait_ge(step, dones[0])
        nc.tensor.matmul(grp_ps[:, :, :].rearrange("p a b -> p (a b)"), group_avg[:, :],
                         mom[:, :, :].rearrange("p a b -> p (a b)"), start=True, stop=True).then_inc(averaged, 1)

    def act_part(act):
        act.wait_ge(step, dones[1])
        nc.scalar.activation(aff[:, 0, :], aff[:, 0, :], ACT.Sqrt, bias=eps_col[:, 0:1]).then_inc(rooted, 1)

    return aff, dve_part, pe_part, act_part


def phase_input_norm(nc, sem, x, xn, halo, vectors, ones_mat, group_mat):
    halo_next = halo[:, 1:, :].rearrange("p (r t) c -> p r t c", t=NT)
    x_in = x.rearrange("b (k p) h w -> p (b k) (h w)", p=P)
    with ExitStack() as ctx:
        sb = lambda n, s, d: ctx.enter_context(nc.sbuf_tensor(n, s, d))
        pb = lambda n, s, d: ctx.enter_context(nc.psum_tensor(n, s, d))
        xs = sb("a_xs", [P, 2, HW], F32)
        stats = sb("a_stats", [P, SEQ, NT, 6], F32)
        ones = sb("a_ones", [P, P], F32)
        gavg = sb("a_gavg", [P, P], F32)
        gb = sb("a_gb", [P, 2, K], F32)
        aff_b = sb("a_aff_b", [P, 2, K], F32)
        eps = sb("a_eps", [P, 1], F32)
        xc = sb("a_xc", [P, 2, K, T], F32)
        xo = sb("a_xo", [P, 2, K, T], F32)
        zero = sb("a_zero", [P, SEQ, 3], F32)
        consts = sem("a_consts")
        eps_set = sem("a_eps_set")
        tile_loaded = [sem("a_tile_loaded0"), sem("a_tile_loaded1")]
        tile_free = sem("a_tile_free")
        chunk_loaded = [sem("a_chunk_loaded0"), sem("a_chunk_loaded1")]
        out_ready = sem("a_out_ready")
        out_stored = sem("a_out_stored")
        out_free = sem("a_out_free")
        affine_picked = sem("a_affine_picked")
        halo_stored = sem("a_halo_stored")
        ln = LayerNorm(nc, "a_ln", sb, pb, sem, xc, ones)
        block = ctx.enter_context(nc.Block())
        aff, gn_dve, gn_pe, gn_act = finish_group_norm(
            nc, sb, pb, sem, block, "a_gn", stats, gavg, (tile_free, 2 + SEQ), eps)
        gn_done = sem("a_gn_done")

        @block.sync
        def _(sp):
            sp.dma_start(ones[:, :], ones_mat).then_inc(consts, 16)
            sp.dma_start(gavg[:, :], group_mat).then_inc(consts, 16)
            sp.dma_start(gb[:, :, :], vectors[:, NORM_G:NORM_B + 1, :]).then_inc(consts, 16)
            sp.sem_inc(tile_free, 2)
            with sp.Fori(0, SEQ // 2) as q:
                for u in range(2):
                    sp.wait_ge(tile_free, 2 * q + u + 1)
                    sp.dma_start(xs[:, u, :], x_in[:, bass.ds(2 * q + u, 1), :].rearrange("p o t -> p (o t)")).then_inc(tile_loaded[u], 16)
            sp.sem_inc(out_ready, 2)
            with sp.Fori(0, B) as b:
                with sp.Fori(0, NT // 2) as t2:
                    for u in range(2):
                        sp.wait_ge(out_ready, b * NT + t2 * 2 + u + 1)
                        sp.dma_start(xc[:, u], x_in[:, bass.ds(b * K, K), bass.ds((t2 * 2 + u) * T, T)]).then_inc(chunk_loaded[u], 16)

        @block.gpsimd
        def _(pool):
            nc.gpsimd.memset(eps[:, :], GN_EPS).then_inc(eps_set, 1)
            nc.gpsimd.memset(zero[:, :, :], 0.0).then_inc(eps_set, 1)
            pool.sem_inc(out_free, 2)
            with pool.Fori(0, B) as b:
                with pool.Fori(0, NT // 2) as t2:
                    for u in range(2):
                        n = b * NT + t2 * 2 + u
                        pool.wait_ge(out_ready, n + 3)
                        pool.dma_start(xn[:, bass.ds(b * K, K), bass.ds((t2 * 2 + u) * T, T)], xo[:, u]).then_inc(out_stored, 16)
                        pool.dma_start(halo_next[:, bass.ds(b * K, K), bass.ds(t2 * 2 + u, 1), :].rearrange("p k o c -> p k (o c)"),
                                       xo[:, u, :, T - 3:T]).then_inc(out_stored, 16)
                        pool.wait_ge(out_stored, 32 * n + 32)
                        pool.sem_inc(out_free, 1)
            pool.wait_ge(eps_set, 2)
            pool.dma_start(halo[:, 0:SEQ * NT, :].rearrange("p (r t) c -> p r t c", t=NT)[:, :, 0, :], zero[:, :, :]).then_inc(halo_stored, 16)
            pool.wait_ge(halo_stored, 16)

        @block.vector
        def _(dve):
            with dve.Fori(0, SEQ // 2) as q:
                for u in range(2):
                    dve.wait_ge(tile_loaded[u], 16 * q + 16)
                    for t in range(NT):
                        bn = nc.vector.bn_stats(stats[:, bass.ds(2 * q + u, 1), t, :].rearrange("p o s -> p (o s)"), xs[:, u, t * T:(t + 1) * T])
                    bn.then_inc(tile_free, 1)
            gn_dve(dve)
            dve.sem_inc(gn_done, 1)
            with dve.Fori(0, B * NT // 2) as q:
                for u in range(2):
                    ln.dve_centre(dve, u, 2 * q + u)
                for u in range(2):
                    ln.dve_scale(dve, u, 2 * q + u)

        @block.tensor
        def _(pe):
            pe.wait_ge(consts, 48)
            gn_pe(pe)
            with pe.Fori(0, B * NT // 2) as q:
                for u in range(2):
                    ln.pe_mean(pe, u, 2 * q + u)
                for u in range(2):
                    ln.pe_var(pe, u, 2 * q + u)

        @block.scalar
        def _(act):
            act.wait_ge(eps_set, 2)
            gn_act(act)
            act.wait_ge(gn_done, 1)
            act.wait_ge(consts, 48)
            with act.Fori(0, B) as b:
                nc.scalar.activation(aff_b[:, :, :], aff[:, :, bass.ds(b * K, K)], ACT.Identity).then_inc(affine_picked, 1)
                act.wait_ge(affine_picked, b + 1)
                with act.Fori(0, NT // 2) as t2:
                    q = b * (NT // 2) + t2
                    for u in range(2):
                        act.wait_ge(chunk_loaded[u], 16 * q + 16)
                        for k in range(K):
                            gn = nc.scalar.activation(xc[:, u, k, :], xc[:, u, k, :], ACT.Identity,
                                                      scale=aff_b[:, 0, k:k + 1], bias=aff_b[:, 1, k:k + 1])
                        gn.then_inc(ln.input_ready, 1)
                    for u in range(2):
                        ln.act_square(act, u, 2 * q + u)
                    for u in range(2):
                        ln.act_std(act, u, 2 * q + u, eps[:, 0:1])
                    for u in range(2):
                        act.wait_ge(ln.scaled, 2 * q + u + 1)
                        act.wait_ge(out_free, 2 * q + u + 1)
                        for k in range(K):
                            o = nc.scalar.activation(xo[:, u, k, :], xc[:, u, k, :], ACT.Identity, scale=gb[:, 0, k:k + 1], bias=gb[:, 1, k:k + 1])
                        o.then_inc(out_ready, 1)


NS = 16
RANK = 8
TAPS = 4
E2 = 2
UNITS = SEQ * NT
J = NS * E2
NBUF = 4


def wait(eng, sem, value):
    if not (isinstance(value, int) and value <= 0):
        eng.wait_ge(sem, value)


def phase_mamba(nc, sem, xn, halo, ym, w_in, w_conv, w_x, w_dtr, w_dt, w_out, a_log, mvec, keep_tab, sel_tab, ident_mat):
    with ExitStack() as ctx:
        sb = lambda n, s, d: ctx.enter_context(nc.sbuf_tensor(n, s, d))
        pb = lambda n, s, d: ctx.enter_context(nc.psum_tensor(n, s, d))
        win = sb("m_win", [P, 2 * E2 * P], F32)
        wcv = sb("m_wcv", [P, TAPS, E2 * P], F32)
        wx = sb("m_wx", [P, E2, 96], F32)
        wdtr = sb("m_wdtr", [P, E2, RANK], F32)
        wdt = sb("m_wdt", [RANK, E2 * P], F32)
        wout = sb("m_wout", [P, E2, P], F32)
        a = sb("m_a", [P, E2, NS], F32)
        mv = sb("m_mv", [P, 7], F32)
        keep = sb("m_keep", [P, UNITS], F32)
        sel = sb("m_sel", [96, 2 * NS, P], BF16)
        ident = sb("m_ident", [P, P], F32)
        x = sb("m_x", [P, 2, 3 + T], F32)
        xc = sb("m_xc", [P, 2, E2, T], F32)
        zs = sb("m_zs", [P, 2, E2, T], F32)
        dt = sb("m_dt", [P, 2, E2, T], F32)
        dtx = sb("m_dtx", [P, 2, E2, T], F32)
        bct = sb("m_bct", [96, 2, T], BF16)
        bcf = sb("m_bcf", [96, T], F32)
        bcr = sb("m_bcr", [64, T], F32)
        dtr = sb("m_dtr", [RANK, T], F32)
        v = sb("m_v", [P, E2, T], F32)
        ea = sb("m_ea", [P, E2, T], F32)
        eb = sb("m_eb", [P, E2, T], F32)
        ec = sb("m_ec", [P, E2, T], F32)
        h = sb("m_h", [P, J, T], F32)
        carry = sb("m_carry", [P, J], F32)
        da = sb("m_da", [P, NBUF, T], F32)
        dbx = sb("m_dbx", [P, NBUF, T], F32)
        hc = sb("m_hc", [P, NBUF, T], F32)
        b_all = sb("m_b_all", [P, NBUF, T], F32)
        yd = sb("m_yd", [P, E2, T], F32)
        yo = sb("m_yo", [P, T], F32)
        y_ps = pb("m_y_ps", [P, E2, T], F32)
        b_ps = pb("m_b_ps", [P, 2, T], F32)
        c_ps = pb("m_c_ps", [P, 2, T], F32)
        pre = pb("m_pre", [P, 2, T], F32)

        consts = sem("m_consts")
        a_exped = sem("m_a_exped")
        a_ready = sem("m_a_ready")
        sel_ready = sem("m_sel_ready")
        carry_zeroed = sem("m_carry_zeroed")
        taps_folded = sem("m_taps_folded")
        x_loaded = [sem("m_x_loaded0"), sem("m_x_loaded1")]
        pre_filled = sem("m_pre_filled")
        out_filled = sem("m_out_filled")
        pre_used = sem("m_pre_used")
        act_chain = sem("m_act_chain")
        bc_rest = sem("m_bc_rest")
        bct_ready = sem("m_bct_ready")
        log_parts = sem("m_log_parts")
        softplus_tail = sem("m_softplus_tail")
        pool_chain = sem("m_pool_chain")
        dt_ready = sem("m_dt_ready")
        dtx_ready = sem("m_dtx_ready")
        carried = sem("m_carried")
        b_filled = sem("m_b_filled")
        c_filled = sem("m_c_filled")
        b_copied = sem("m_b_copied")
        decays = sem("m_decays")
        inputs = sem("m_inputs")
        scanned = sem("m_scanned")
        products = sem("m_products")
        summed = sem("m_summed")
        y_read = sem("m_y_read")
        yz_ready = sem("m_yz_ready")
        out_ready = sem("m_out_ready")
        out_stored = sem("m_out_stored")
        block = ctx.enter_context(nc.Block())

        def units(eng, run):
            run(0, 0, 0, False, True)
            with eng.Fori(0, UNITS // 2 - 1) as i:
                run(2 * i + 1, i, 1, True, True)
                run(2 * i + 2, i + 1, 0, True, True)
            run(UNITS - 1, UNITS // 2 - 1, 1, True, False)

        @block.sync
        def _(sp):
            sel_f = h[0:96, 0:8, :].rearrange("p a b -> p (a b)")
            for dst, src in ((win[:, :], w_in), (wcv[:, :, :].rearrange("p a b -> p (a b)"), w_conv.partition_broadcast(P)),
                             (wx[:, :, :], w_x), (wdtr[:, :, :], w_dtr), (wdt[:, :], w_dt), (wout[:, :, :], w_out), (a[:, :, :], a_log),
                             (mv[:, :], mvec), (keep[:, :], keep_tab), (sel_f, sel_tab), (ident[:, :], ident_mat)):
                sp.dma_start(dst, src).then_inc(consts, 16)

            def load(n, u):
                sp.dma_start(x[:, u, 3:3 + T], xn[:, bass.ds(n, 1), :].rearrange("p o t -> p (o t)")).then_inc(x_loaded[u], 16)
                sp.dma_start(x[:, u, 0:3], halo[:, bass.ds(n, 1), :].rearrange("p o t -> p (o t)")).then_inc(x_loaded[u], 16)

            def run(n, m, u, has_prev, has_next):
                if has_prev:
                    sp.wait_ge(out_ready, n)
                    sp.dma_start(ym[:, bass.ds(n - 1, 1), :].rearrange("p o t -> p (o t)"), yo[:, :]).then_inc(out_stored, 16)
                if has_next:
                    load(n + 1, 1 - u)

            load(0, 0)
            units(sp, run)
            sp.wait_ge(out_ready, UNITS)
            sp.dma_start(ym[:, UNITS - 1, :], yo[:, :]).then_inc(out_stored, 16)
            sp.wait_ge(out_stored, 16 * UNITS)

        @block.tensor
        def _(pe):
            def project(out, terms, filled):
                for i, (lhs, rhs) in enumerate(terms):
                    mm = nc.tensor.matmul(out, lhs, rhs, start=i == 0, stop=i == len(terms) - 1)
                mm.then_inc(filled, 1)

            def pre_step(g, n, m, u):
                if g == 0:
                    pe.wait_ge(x_loaded[u], 32 * m + 32)
                    wait(pe, out_ready, n - 1)
                else:
                    wait(pe, pre_used, 8 * n + g - 1)
                if g < 2:
                    project(pre[:, g % 2, :], [(wcv[:, tap, g * P:(g + 1) * P], x[:, u, tap:tap + T]) for tap in range(TAPS)], pre_filled)
                elif g < 4:
                    project(pre[:, g % 2, :], [(win[:, g * P:(g + 1) * P], x[:, u, 3:3 + T])], pre_filled)
                elif g == 4:
                    project(pre[0:96, 0, :], [(wx[:, e, :], xc[:, u, e, :]) for e in range(E2)], pre_filled)
                elif g == 5:
                    project(pre[0:RANK, 1, :], [(wdtr[:, e, :], xc[:, u, e, :]) for e in range(E2)], pre_filled)
                else:
                    if g == 6:
                        pe.wait_ge(pre_used, 8 * n + 6)
                    project(pre[:, g % 2, :], [(wdt[:, (g - 6) * P:(g - 5) * P], dtr[:, :])], pre_filled)

            def out_step(n, pre_before):
                pe.wait_ge(yz_ready, n + 1)
                wait(pe, pre_used, pre_before)
                project(pre[:, 0, :], [(wout[:, e, :], yd[:, e, :]) for e in range(E2)], out_filled)

            def spread_b(n, u, s):
                if s == 0:
                    pe.wait_ge(bct_ready, n + 1)
                wait(pe, b_copied, NS * n + s - 1)
                nc.tensor.matmul(b_ps[:, s % 2, :], sel[:, s, :], bct[:, u, :], start=True, stop=True).then_inc(b_filled, 1)

            def spread_c(n, u, s):
                wait(pe, products, J * n + E2 * (s - 1))
                nc.tensor.matmul(c_ps[:, s % 2, :], sel[:, NS + s, :], bct[:, u, :], start=True, stop=True).then_inc(c_filled, 1)

            def run(n, m, u, has_prev, has_next):
                nm = m + u
                for s in range(NS):
                    if s + 2 < NS:
                        spread_b(n, u, s + 2)
                    elif has_next:
                        spread_b(n + 1, 1 - u, s + 2 - NS)
                    if s + 1 < NS:
                        spread_c(n, u, s + 1)
                    elif has_next:
                        spread_c(n + 1, 1 - u, 0)
                    for e in range(E2):
                        j = E2 * s + e
                        pe.wait_ge(products, J * n + j + 1)
                        if j == 0:
                            wait(pe, y_read, n)
                        nc.tensor.matmul(y_ps[:, e, :], ident[:, :], hc[:, j % NBUF, :], start=s == 0, stop=s == NS - 1).then_inc(summed, 1)
                        if has_prev and j == 4:
                            out_step(n - 1, 8 * n + 8)
                        if has_next and j in PRE_AT:
                            for g in PRE_AT[j]:
                                pre_step(g, n + 1, nm, 1 - u)

            PRE_AT = {5: (0,), 7: (1,), 9: (2, 3), 12: (4, 5), 15: (6, 7)}
            pe.wait_ge(consts, 16 * 11)
            pe.wait_ge(sel_ready, 1)
            pe.wait_ge(taps_folded, TAPS)
            for g in range(8):
                pre_step(g, 0, 0, 0)
            spread_b(0, 0, 0)
            spread_b(0, 0, 1)
            spread_c(0, 0, 0)
            units(pe, run)
            out_step(UNITS - 1, 8 * UNITS)

        @block.scalar
        def _(act):
            act.wait_ge(consts, 16 * 11)
            nc.scalar.activation(a[:, :, :], a[:, :, :], ACT.Exp).then_inc(a_exped, 1)
            nc.scalar.activation(sel[:, :, :].rearrange("p a b -> p (a b)"), h[0:96, 0:8, :].rearrange("p a b -> p (a b)"), ACT.Copy).then_inc(sel_ready, 1)

            def silus(n, u):
                for g in range(4):
                    act.wait_ge(pre_filled, 8 * n + g + 1)
                    if g < 2:
                        nc.scalar.activation(xc[:, u, g, :], pre[:, g % 2, :], ACT.Silu, bias=mv[:, g:g + 1]).then_inc(pre_used, 1)
                    else:
                        nc.scalar.activation(zs[:, u, g - 2, :], pre[:, g % 2, :], ACT.Silu).then_inc(pre_used, 1)

            def projections(n, u):
                act.wait_ge(pre_filled, 8 * n + 5)
                nc.scalar.activation(bcf[:, :], pre[0:96, 0, :], ACT.Copy).then_inc(pre_used, 1)
                act.wait_ge(pre_filled, 8 * n + 6)
                nc.scalar.activation(dtr[:, :], pre[0:RANK, 1, :], ACT.Copy).then_inc(pre_used, 1)
                act.wait_ge(pre_used, 8 * n + 5)
                nc.scalar.activation(bct[:, u, :], bcf[:, :], ACT.Copy).then_inc(act_chain, 1)
                for e in range(E2):
                    act.wait_ge(pre_filled, 8 * n + 7 + e)
                    nc.scalar.activation(v[:, e, :], pre[:, e, :], ACT.Identity, bias=mv[:, 2 + e:3 + e]).then_inc(pre_used, 1)

            def mid_part(n, u):
                act.wait_ge(bc_rest, n + 1)
                nc.scalar.activation(bct[0:64, u, :], bcr[:, :], ACT.Copy).then_inc(act_chain, 1)

            def softplus(n):
                act.wait_ge(pre_used, 8 * n + 8)
                nc.scalar.activation(ea[:, :, :], v[:, :, :], ACT.Abs).then_inc(act_chain, 1)
                act.wait_ge(act_chain, 6 * n + 3)
                nc.scalar.activation(ea[:, :, :], ea[:, :, :], ACT.Exp, scale=-1.0).then_inc(act_chain, 1)
                act.wait_ge(act_chain, 6 * n + 4)
                nc.scalar.activation(eb[:, :, :], ea[:, :, :], ACT.Identity, bias=1.0).then_inc(act_chain, 1)
                act.wait_ge(act_chain, 6 * n + 5)
                nc.scalar.activation(ec[:, :, :], eb[:, :, :], ACT.Ln).then_inc(act_chain, 1)
                nc.scalar.activation(eb[:, :, :], eb[:, :, :], ACT.Identity, bias=-1.0).then_inc(log_parts, 1)

            def copy_b(n, s):
                act.wait_ge(b_filled, NS * n + s + 1)
                wait(act, inputs, J * n + E2 * (s - NBUF + 1))
                nc.scalar.activation(b_all[:, s % NBUF, :], b_ps[:, s % 2, :], ACT.Copy).then_inc(b_copied, 1)

            def run(n, m, u, has_prev, has_next):
                act.wait_ge(dt_ready, n + 1)
                for s in range(NS):
                    if s + 1 < NS:
                        copy_b(n, s + 1)
                    elif has_next:
                        copy_b(n + 1, 0)
                    for e in range(E2):
                        j = E2 * s + e
                        wait(act, scanned, J * n + j - NBUF + 1)
                        nc.scalar.activation(da[:, j % NBUF, :], dt[:, u, e, :], ACT.Exp, scale=a[:, e, s:s + 1]).then_inc(decays, 1)
                        if has_next:
                            if j == 11:
                                silus(n + 1, 1 - u)
                            elif j == 17:
                                projections(n + 1, 1 - u)
                            elif j == 19:
                                mid_part(n + 1, 1 - u)
                            elif j == 20:
                                softplus(n + 1)

            act.wait_ge(a_ready, 1)
            silus(0, 0)
            projections(0, 0)
            mid_part(0, 0)
            softplus(0)
            copy_b(0, 0)
            units(act, run)

        @block.gpsimd
        def _(pool):
            def split(n, u, part):
                if part == 0:
                    pool.wait_ge(act_chain, 6 * n + 1)
                    nc.gpsimd.tensor_tensor(bcr[:, :], bcf[0:64, :], bct[0:64, u, :], ALU.subtract).then_inc(bc_rest, 1)
                else:
                    pool.wait_ge(act_chain, 6 * n + 2)
                    nc.gpsimd.tensor_tensor(bct[0:32, u, :], bcr[0:32, :], bct[0:32, u, :], ALU.subtract).then_inc(bct_ready, 1)

            def tail(n):
                pool.wait_ge(log_parts, n + 1)
                nc.gpsimd.tensor_tensor(ea[:, :, :], ea[:, :, :], eb[:, :, :], ALU.subtract).then_inc(pool_chain, 1)
                pool.wait_ge(pool_chain, n + 1)
                nc.gpsimd.tensor_tensor(ec[:, :, :], ec[:, :, :], ea[:, :, :], ALU.add).then_inc(softplus_tail, 1)

            def dt_times_x(n, u):
                pool.wait_ge(dt_ready, n + 1)
                nc.gpsimd.tensor_tensor(dtx[:, u], dt[:, u], xc[:, u], ALU.mult).then_inc(dtx_ready, 1)

            def gate(n, u):
                pool.wait_ge(y_read, n + 1)
                nc.gpsimd.tensor_tensor(yd[:, :, :], yd[:, :, :], zs[:, u], ALU.mult).then_inc(yz_ready, 1)

            def run(n, m, u, has_prev, has_next):
                for s in range(NS):
                    pool.wait_ge(b_copied, NS * n + s + 1)
                    for e in range(E2):
                        j = E2 * s + e
                        wait(pool, scanned, J * n + j - NBUF + 1)
                        if j == 0:
                            pool.wait_ge(dtx_ready, n + 1)
                        nc.gpsimd.tensor_tensor(dbx[:, j % NBUF, :], dtx[:, u, e, :], b_all[:, s % NBUF, :], ALU.mult).then_inc(inputs, 1)
                        if has_prev and j == 4:
                            gate(n - 1, 1 - u)
                        if has_next:
                            if j == 18:
                                split(n + 1, 1 - u, 0)
                            elif j == 20:
                                split(n + 1, 1 - u, 1)
                            elif j == 22:
                                tail(n + 1)
                            elif j == 26:
                                dt_times_x(n + 1, 1 - u)

            nc.gpsimd.memset(carry[:, :], 0.0).then_inc(carry_zeroed, 1)
            split(0, 0, 0)
            split(0, 0, 1)
            tail(0)
            dt_times_x(0, 0)
            units(pool, run)
            gate(UNITS - 1, 1)

        @block.vector
        def _(dve):
            dve.wait_ge(consts, 16 * 11)
            for tap in range(TAPS):
                nc.vector.tensor_tensor(wcv[:, tap, :], wcv[:, tap, :], win[:, 0:E2 * P], ALU.mult).then_inc(taps_folded, 1)
            dve.wait_ge(a_exped, 1)
            nc.vector.tensor_scalar(a[:, :, :], a[:, :, :], -1.0, None, ALU.mult).then_inc(a_ready, 1)
            dve.wait_ge(carry_zeroed, 1)

            def softplus_head(n, u):
                dve.wait_ge(softplus_tail, n + 1)
                nc.vector.scalar_tensor_tensor(dt[:, u].rearrange("p a b -> p (a b)"), v[:, :, :].rearrange("p a b -> p (a b)"), 0.0,
                                               ec[:, :, :].rearrange("p a b -> p (a b)"), ALU.max, ALU.add).then_inc(dt_ready, 1)

            def read_y(n, u):
                dve.wait_ge(summed, J * n + J)
                wait(dve, out_filled, n)
                for e in range(E2):
                    y = nc.vector.scalar_tensor_tensor(yd[:, e, :], xc[:, u, e, :], mv[:, 4 + e:5 + e], y_ps[:, e, :], ALU.mult, ALU.add)
                y.then_inc(y_read, 1)

            def output(n, u):
                dve.wait_ge(out_filled, n + 1)
                wait(dve, out_stored, 16 * n)
                nc.vector.scalar_tensor_tensor(yo[:, :], x[:, u, 3:3 + T], mv[:, 6:7], pre[:, 0, :], ALU.mult, ALU.add).then_inc(out_ready, 1)

            def product(n, j):
                s, e = divmod(j, E2)
                dve.wait_ge(scanned, J * n + j + 1)
                dve.wait_ge(c_filled, NS * n + s + 1)
                wait(dve, summed, J * n + j - NBUF + 1)
                nc.vector.tensor_tensor(hc[:, j % NBUF, :], h[:, j, :], c_ps[:, s % 2, :], ALU.mult).then_inc(products, 1)

            def run(n, m, u, has_prev, has_next):
                if has_prev:
                    dve.wait_ge(scanned, J * n)
                    nc.vector.tensor_tensor(carry[:, :], h[:, :, T - 1], keep[:, bass.ds(n, 1)].broadcast_to([P, J]), ALU.mult).then_inc(carried, 1)
                    dve.wait_ge(carried, n)
                for j in range(J):
                    dve.wait_ge(decays, J * n + j + 1)
                    dve.wait_ge(inputs, J * n + j + 1)
                    nc.vector.tensor_tensor_scan(h[:, j, :], da[:, j % NBUF, :], dbx[:, j % NBUF, :], carry[:, j:j + 1],
                                                 ALU.mult, ALU.add).then_inc(scanned, 1)
                    if j:
                        product(n, j - 1)
                    if has_prev:
                        if j == 1:
                            read_y(n - 1, 1 - u)
                        elif j == 7:
                            output(n - 1, 1 - u)
                    if has_next and j == 25:
                        softplus_head(n + 1, 1 - u)
                product(n, J - 1)

            softplus_head(0, 0)
            units(dve, run)
            read_y(UNITS - 1, 1)
            output(UNITS - 1, 1)


def phase_project(nc, sem, ym, x, x2, stats_out, vectors, w_proj, ones_mat):
    x_in = x.rearrange("b (k p) h w -> p (b k) (h w)", p=P)
    y_in = ym.rearrange("p (r t) c -> p r (t c)", t=NT)
    with ExitStack() as ctx:
        sb = lambda n, s, d: ctx.enter_context(nc.sbuf_tensor(n, s, d))
        pb = lambda n, s, d: ctx.enter_context(nc.psum_tensor(n, s, d))
        ones = sb("p_ones", [P, P], F32)
        vec = sb("p_vec", [P, 3, K], F32)
        w = sb("p_w", [P, K, C], F32)
        eps = sb("p_eps", [P, 1], F32)
        y = sb("p_y", [P, 2, K, T], F32)
        yn = sb("p_yn", [P, 2, K, T], F32)
        res = sb("p_res", [P, 2, K, T], F32)
        stats = sb("p_stats", [P, SEQ, NT, 6], F32)
        out_ps = pb("p_out_ps", [P, 4, T], F32)
        consts = sem("p_consts")
        eps_set = sem("p_eps_set")
        y_loaded = [sem("p_y_loaded0"), sem("p_y_loaded1")]
        x_loaded = [sem("p_x_loaded0"), sem("p_x_loaded1")]
        res_free = sem("p_res_free")
        yn_ready = sem("p_yn_ready")
        bank_filled = sem("p_bank_filled")
        bank_read = sem("p_bank_read")
        stats_done = sem("p_stats_done")
        stored = sem("p_stored")
        ln = LayerNorm(nc, "p_ln", sb, pb, sem, y, ones)
        block = ctx.enter_context(nc.Block())
        CHUNKS = B * NT

        @block.sync
        def _(sp):
            sp.dma_start(ones[:, :], ones_mat).then_inc(consts, 16)
            sp.dma_start(vec[:, :, :], vectors[:, NORM_G:PROJ_B + 1, :]).then_inc(consts, 16)
            sp.dma_start(w[:, :, :], w_proj).then_inc(consts, 16)
            sp.sem_inc(yn_ready, 2)
            with sp.Fori(0, B) as b:
                with sp.Fori(0, NT // 2) as t2:
                    q = b * (NT // 2) + t2
                    for u in range(2):
                        sp.wait_ge(yn_ready, 2 * q + u + 1)
                        sp.dma_start(y[:, u], y_in[:, bass.ds(b * K, K), bass.ds((t2 * 2 + u) * T, T)]).then_inc(y_loaded[u], 16)
                        sp.wait_ge(res_free, 2 * q + u + 1)
                        sp.dma_start(res[:, u], x_in[:, bass.ds(b * K, K), bass.ds((t2 * 2 + u) * T, T)]).then_inc(x_loaded[u], 16)

        @block.gpsimd
        def _(pool):
            nc.gpsimd.memset(eps[:, :], LN_EPS).then_inc(eps_set, 1)
            pool.sem_inc(res_free, 2)
            with pool.Fori(0, B) as b:
                with pool.Fori(0, NT // 2) as t2:
                    for u in range(2):
                        n = b * NT + t2 * 2 + u
                        pool.wait_ge(stats_done, n + 1)
                        pool.dma_start(x2[:, bass.ds(b * K, K), bass.ds((t2 * 2 + u) * T, T)], res[:, u]).then_inc(stored, 16)
                        pool.wait_ge(stored, 16 * n + 16)
                        pool.sem_inc(res_free, 1)
            pool.dma_start(stats_out, stats[:, :, :, :]).then_inc(stored, 16)
            pool.wait_ge(stored, 16 * CHUNKS + 16)

        @block.tensor
        def _(pe):
            pe.wait_ge(consts, 48)
            with pe.Fori(0, CHUNKS // 2) as q:
                for u in range(2):
                    ln.pe_mean(pe, u, 2 * q + u)
                for u in range(2):
                    ln.pe_var(pe, u, 2 * q + u)
                for u in range(2):
                    c = 2 * q + u
                    pe.wait_ge(yn_ready, c + 3)
                    for o in range(K):
                        pe.wait_ge(bank_read, 4 * c + o + 1)
                        for k in range(K):
                            mm = nc.tensor.matmul(out_ps[:, o, :], w[:, k, o * P:(o + 1) * P], yn[:, u, k, :], start=k == 0, stop=k == K - 1)
                        mm.then_inc(bank_filled, 1)

        @block.scalar
        def _(act):
            act.sem_inc(bank_read, 4)
            act.wait_ge(eps_set, 1)
            act.wait_ge(consts, 48)
            with act.Fori(0, CHUNKS // 2) as q:
                for u in range(2):
                    act.wait_ge(y_loaded[u], 16 * q + 16)
                    act.sem_inc(ln.input_ready, 1)
                for u in range(2):
                    ln.act_square(act, u, 2 * q + u)
                for u in range(2):
                    ln.act_std(act, u, 2 * q + u, eps[:, 0:1])
                for u in range(2):
                    c = 2 * q + u
                    act.wait_ge(ln.scaled, c + 1)
                    for k in range(K):
                        o = nc.scalar.activation(yn[:, u, k, :], y[:, u, k, :], ACT.Identity, scale=vec[:, 0, k:k + 1], bias=vec[:, 1, k:k + 1])
                    o.then_inc(yn_ready, 1)

        @block.vector
        def _(dve):
            with dve.Fori(0, B) as b:
                with dve.Fori(0, NT // 2) as t2:
                    q = b * (NT // 2) + t2
                    for u in range(2):
                        ln.dve_centre(dve, u, 2 * q + u)
                    for u in range(2):
                        ln.dve_scale(dve, u, 2 * q + u)
                    for u in range(2):
                        c = 2 * q + u
                        dve.wait_ge(x_loaded[u], 16 * q + 16)
                        for k in range(K):
                            dve.wait_ge(bank_filled, 4 * c + k + 1)
                            nc.vector.scalar_tensor_tensor(res[:, u, k, :], out_ps[:, k, :], vec[:, 2, k:k + 1], res[:, u, k, :],
                                                           ALU.add, ALU.add).then_inc(bank_read, 1)
                        dve.wait_ge(bank_read, 4 * c + 8)
                        for k in range(K):
                            bn = nc.vector.bn_stats(stats[:, bass.ds(b * K + k, 1), bass.ds(t2 * 2 + u, 1), :].rearrange("p o n s -> p (o n s)"),
                                                    res[:, u, k, :])
                        bn.then_inc(stats_done, 1)


G = 16
PTS = 9
NOFF = G * PTS * 2
NMASK = G * PTS
ROWS = T // IMG
TT = T // P
PADI = IMG + 2
NCOL = NOFF + NMASK
REACH = 3
PADW = IMG + 2 * REACH


def phase_offsets(nc, sem, x2, stats_in, xproj, offsets, masks, peak, vectors, w_in, dw_w, w_om, b_om, ones_mat, group_mat):
    with ExitStack() as ctx:
        sb = lambda n, s, d: ctx.enter_context(nc.sbuf_tensor(n, s, d))
        pb = lambda n, s, d: ctx.enter_context(nc.psum_tensor(n, s, d))
        ones = sb("o_ones", [P, P], F32)
        gavg = sb("o_gavg", [P, P], F32)
        vec = sb("o_vec", [P, 4, K], F32)
        w = sb("o_w", [P, K, C], F32)
        wom = sb("o_wom", [P, K, NCOL], F32)
        bom = sb("o_bom", [P, NCOL], F32)
        dw = sb("o_dw", [P, K, 9], F32)
        eps = sb("o_eps", [P, 1], F32)
        stats = sb("o_stats", [P, SEQ, NT, 6], F32)
        aff_b = sb("o_aff_b", [P, 2, K], F32)
        raw = sb("o_raw", [P, 2, K, T], F32)
        g = sb("o_g", [P, K, PADI, PADI], F32)
        d = sb("o_d", [P, 2, K, T], F32)
        xp = sb("o_xp", [P, K, ROWS, PADW], F32)
        zero = sb("o_zero", [P, K, REACH * PADW], F32)
        om = sb("o_om", [P, TT, NCOL], F32)
        small = sb("o_small", [P, 2, TT, G], F32)
        peaks = sb("o_peaks", [P, B * NT], F32)
        out_ps = pb("o_out_ps", [P, 4, T], F32)
        consts = sem("o_consts")
        eps_set = sem("o_eps_set")
        border_set = sem("o_border_set")
        xp_border_set = sem("o_xp_border_set")
        zeros_set = sem("o_zeros_set")
        rows_stored = sem("o_rows_stored")
        affine_picked = sem("o_affine_picked")
        raw_loaded = [sem("o_raw_loaded0"), sem("o_raw_loaded1")]
        normed = sem("o_normed")
        convolved = sem("o_convolved")
        geluded = sem("o_geluded")
        bank_filled = sem("o_bank_filled")
        bank_read_act = sem("o_bank_read_act")
        bank_read_dve = sem("o_bank_read_dve")
        xp_ready = sem("o_xp_ready")
        xp_stored = sem("o_xp_stored")
        om_step = sem("o_om_step")
        exp_done = sem("o_exp_done")
        om_ready = sem("o_om_ready")
        om_stored = sem("o_om_stored")
        chunk_done = sem("o_chunk_done")
        ln = LayerNorm(nc, "o_ln", sb, pb, sem, d, ones)
        block = ctx.enter_context(nc.Block())
        aff, gn_dve, gn_pe, gn_act = finish_group_norm(
            nc, sb, pb, sem, block, "o_gn", stats, gavg, (consts, 16 * 8), eps)
        CH = B * NT
        OM = 7

        @block.sync
        def _(sp):
            for dst, src in ((ones[:, :], ones_mat), (gavg[:, :], group_mat), (vec[:, :, :], vectors[:, DW_B:IN_B + 1, :]),
                             (w[:, :, :], w_in), (wom[:, :, :], w_om), (bom[:, :], b_om.partition_broadcast(P)),
                             (dw[:, :, :], dw_w), (stats[:, :, :, :], stats_in)):
                sp.dma_start(dst, src).then_inc(consts, 16)
            sp.sem_inc(normed, 2)
            with sp.Fori(0, B) as b:
                with sp.Fori(0, NT // 2) as t2:
                    for u in range(2):
                        sp.wait_ge(normed, b * NT + t2 * 2 + u + 1)
                        sp.dma_start(raw[:, u], x2[:, bass.ds(b * K, K), bass.ds((t2 * 2 + u) * T, T)]).then_inc(raw_loaded[u], 16)

        @block.gpsimd
        def _(pool):
            nc.gpsimd.memset(eps[:, :], LN_EPS).then_inc(eps_set, 1)
            nc.gpsimd.memset(g[:, :, :, :].rearrange("p k a b -> p (k a b)"), 0.0).then_inc(border_set, 1)
            nc.gpsimd.memset(xp[:, :, :, :].rearrange("p k a b -> p (k a b)"), 0.0).then_inc(xp_border_set, 1)
            nc.gpsimd.memset(zero[:, :, :].rearrange("p k a -> p (k a)"), 0.0).then_inc(zeros_set, 1)
            pool.wait_ge(zeros_set, 1)
            for b in range(B):
                for r in (0, PADW - REACH):
                    pool.dma_start(xproj[:, b * K:(b + 1) * K, r * PADW:(r + REACH) * PADW], zero[:, :, :]).then_inc(rows_stored, 16)
            with pool.Fori(0, B) as b:
                with pool.Fori(0, NT) as t:
                    n = b * NT + t
                    pool.wait_ge(xp_ready, n + 1)
                    pool.dma_start(xproj[:, bass.ds(b * K, K), bass.ds((t * ROWS + REACH) * PADW, ROWS * PADW)],
                                   xp[:, :, :, :].rearrange("p k a b -> p k (a b)")).then_inc(xp_stored, 16)
                    pool.wait_ge(om_ready, n + 1)
                    pool.dma_start(offsets[:, bass.ds(n * TT, TT), :], om[:, :, 0:NOFF]).then_inc(om_stored, 16)
                    pool.dma_start(masks[:, bass.ds(n * TT, TT), :], om[:, :, NOFF:NCOL]).then_inc(om_stored, 16)
                    pool.wait_ge(xp_stored, 16 * n + 16)
                    pool.wait_ge(om_stored, 32 * n + 32)
                    pool.sem_inc(chunk_done, 1)
            pool.dma_start(peak, peaks[:, :]).then_inc(om_stored, 16)
            pool.wait_ge(om_stored, 32 * CH + 16)
            pool.wait_ge(rows_stored, 16 * 2 * B)

        @block.tensor
        def _(pe):
            pe.wait_ge(consts, 16 * 8)
            gn_pe(pe)
            with pe.Fori(0, B) as b:
                with pe.Fori(0, NT // 2) as t2:
                    for u in range(2):
                        c = b * NT + t2 * 2 + u
                        pe.wait_ge(normed, (b + 1) * NT + 2)
                        for o in range(K):
                            wait(pe, bank_read_act, 4 * c + o + 1)
                            if o == 0:
                                wait(pe, bank_read_dve, c + 1)
                            for k in range(K):
                                mm = nc.tensor.matmul(out_ps[:, o, :], w[:, k, o * P:(o + 1) * P],
                                                      g[:, k, bass.ds((t2 * 2 + u) * ROWS + 1, ROWS), 1:1 + IMG], start=k == 0, stop=k == K - 1)
                            mm.then_inc(bank_filled, 1)
                        if u == 0:
                            for v in range(2):
                                ln.pe_mean(pe, v, b * NT + t2 * 2 + v)
                            for v in range(2):
                                ln.pe_var(pe, v, b * NT + t2 * 2 + v)
                        pe.wait_ge(geluded, c + 1)
                        pe.wait_ge(bank_read_act, 4 * c + 8)
                        for t in range(TT):
                            for k in range(K):
                                mm = nc.tensor.matmul(out_ps[:, t, 0:NCOL], d[:, u, k, t * P:(t + 1) * P], wom[:, k, :], start=k == 0, stop=k == K - 1)
                        mm.then_inc(bank_filled, 1)

        @block.scalar
        def _(act):
            act.sem_inc(bank_read_act, 4)
            act.wait_ge(eps_set, 1)
            gn_act(act)
            act.wait_ge(xp_border_set, 1)
            act.wait_ge(consts, 16 * 8)
            with act.Fori(0, B) as b:
                with act.Fori(0, NT // 2) as t2:
                    for u in range(2):
                        c = b * NT + t2 * 2 + u
                        act.wait_ge(chunk_done, c + 1)
                        for k in range(K):
                            act.wait_ge(bank_filled, 5 * c + k + 1)
                            nc.scalar.activation(xp[:, k, :, REACH:REACH + IMG], out_ps[:, k, :].rearrange("p (r c) -> p r c", c=IMG), ACT.Identity, bias=vec[:, 3, k:k + 1]).then_inc(bank_read_act, 1)
                        act.wait_ge(bank_read_act, 4 * c + 8)
                        act.sem_inc(xp_ready, 1)
                        if u == 0:
                            for v in range(2):
                                ln.act_square(act, v, b * NT + t2 * 2 + v)
                            for v in range(2):
                                ln.act_std(act, v, b * NT + t2 * 2 + v, eps[:, 0:1])
                        act.wait_ge(ln.scaled, c + 1)
                        for k in range(K):
                            a = nc.scalar.activation(d[:, u, k, :], d[:, u, k, :], ACT.Gelu, scale=vec[:, 1, k:k + 1], bias=vec[:, 2, k:k + 1])
                        a.then_inc(geluded, 1)
                        act.wait_ge(om_step, OM * c + 3)
                        nc.scalar.activation(om[:, :, NOFF:NCOL], om[:, :, NOFF:NCOL], ACT.Exp).then_inc(exp_done, 1)

        @block.vector
        def _(dve):
            dve.sem_inc(bank_read_dve, 1)
            dve.sem_inc(chunk_done, 1)
            gn_dve(dve)
            dve.wait_ge(border_set, 1)
            lg = om[:, :, NOFF:NCOL].rearrange("p t (g q) -> p t g q", q=PTS)
            per_point = lambda s: s.unsqueeze(3).broadcast_to([P, TT, G, PTS])
            with dve.Fori(0, B) as b:
                dve.wait_ge(bank_filled, 5 * NT * b)
                nc.vector.tensor_scalar(aff_b[:, :, :], aff[:, :, bass.ds(b * K, K)], 1.0, None, ALU.mult).then_inc(affine_picked, 1)
                with dve.Fori(0, NT // 2) as t2:
                    for u in range(2):
                        dve.wait_ge(affine_picked, b + 1)
                        dve.wait_ge(raw_loaded[u], 16 * (b * (NT // 2) + t2) + 16)
                        for k in range(K):
                            a = nc.vector.tensor_scalar(g[:, k, bass.ds((t2 * 2 + u) * ROWS + 1, ROWS), 1:1 + IMG],
                                                        raw[:, u, k, :].rearrange("p (r c) -> p r c", c=IMG),
                                                        aff_b[:, 0, k:k + 1], aff_b[:, 1, k:k + 1], ALU.mult, ALU.add)
                        a.then_inc(normed, 1)
                with dve.Fori(0, NT // 2) as t2:
                    for u in range(2):
                        c = b * NT + t2 * 2 + u
                        dve.wait_ge(normed, (b + 1) * NT + 2)
                        dve.wait_ge(bank_read_dve, c)
                        for k in range(K):
                            for tap in range(9):
                                r, s = divmod(tap, 3)
                                src = g[:, k, bass.ds((t2 * 2 + u) * ROWS + r, ROWS), s:s + IMG]
                                dst = d[:, u, k, :].rearrange("p (r c) -> p r c", c=IMG)
                                if tap == 0:
                                    i = nc.vector.tensor_scalar(dst, src, dw[:, k, 0:1], vec[:, 0, k:k + 1], ALU.mult, ALU.add)
                                else:
                                    i = nc.vector.scalar_tensor_tensor(dst, src, dw[:, k, tap:tap + 1], dst, ALU.mult, ALU.add)
                                i.then_inc(convolved, 1)
                                dve.wait_ge(convolved, 36 * c + 9 * k + tap + 1)
                        dve.sem_inc(ln.input_ready, 1)
                    for u in range(2):
                        ln.dve_centre(dve, u, b * NT + t2 * 2 + u)
                    for u in range(2):
                        ln.dve_scale(dve, u, b * NT + t2 * 2 + u)
                    for u in range(2):
                        c = b * NT + t2 * 2 + u
                        dve.wait_ge(bank_filled, 5 * c + 5)
                        dve.wait_ge(chunk_done, c + 1)
                        nc.vector.tensor_tensor(om[:, :, :], out_ps[:, :, 0:NCOL], bom[:, :].unsqueeze(1).broadcast_to([P, TT, NCOL]),
                                                ALU.add).then_inc(om_step, 1)
                        dve.wait_ge(om_step, OM * c + 1)
                        dve.sem_inc(bank_read_dve, 1)
                        nc.vector.tensor_reduce(small[:, 0], lg, AX.X, ALU.max).then_inc(om_step, 1)
                        dve.wait_ge(om_step, OM * c + 2)
                        nc.vector.tensor_tensor(lg, lg, per_point(small[:, 0]), ALU.subtract).then_inc(om_step, 1)
                        nc.vector.tensor_reduce(peaks[:, bass.ds(c, 1)], om[:, :, 0:NOFF], AX.XY, ALU.max, apply_absolute_value=True).then_inc(om_step, 1)
                        dve.wait_ge(exp_done, c + 1)
                        nc.vector.tensor_reduce(small[:, 1], lg, AX.X, ALU.add).then_inc(om_step, 1)
                        dve.wait_ge(om_step, OM * c + 5)
                        nc.vector.reciprocal(small[:, 1], small[:, 1]).then_inc(om_step, 1)
                        dve.wait_ge(om_step, OM * c + 6)
                        nc.vector.tensor_tensor(lg, lg, per_point(small[:, 1]), ALU.mult).then_inc(om_step, 1)
                        dve.wait_ge(om_step, OM * c + 7)
                        dve.sem_inc(om_ready, 1)


WIN = 2 * REACH + 1
D = WIN * WIN
HATS = 5
PARTS = 3
GK = G // K
ROWD = PARTS * GK
PER_BLOCK = 10
BLOCKS = -(-D // PER_BLOCK)
PAIRS = (D + 1) // 2


def phase_sample(nc, sem, x2, xproj, offsets, masks, out, vectors, w_out, sel_tab, ident_mat):
    with ExitStack() as ctx:
        sb = lambda n, s, d: ctx.enter_context(nc.sbuf_tensor(n, s, d))
        pb = lambda n, s, d: ctx.enter_context(nc.psum_tensor(n, s, d))
        vec = sb("s_vec", [P, 1, K], F32)
        w = sb("s_w", [P, K, C], F32)
        sel = sb("s_sel", [PER_BLOCK * ROWD, PER_BLOCK, P], BF16)
        ident = sb("s_ident", [P, P], F32)
        identb = sb("s_identb", [P, P], BF16)
        img = sb("s_img", [P, 2, K, (ROWS + 2 * REACH) * PADW], F32)
        off = sb("s_off", [P, TT, NOFF], F32)
        msk = sb("s_msk", [P, TT, NMASK], F32)
        hx = sb("s_hx", [P, TT * G, PTS, HATS], F32)
        hy = sb("s_hy", [P, TT * G, PTS, HATS], F32)
        outer = sb("s_outer", [P, 2, TT * G, HATS, HATS], F32)
        wts = sb("s_wts", [P, TT * G, WIN, WIN], F32)
        wtp = sb("s_wtp", [P, TT, K, D * ROWD], BF16)
        wtt = sb("s_wtt", [PER_BLOCK * ROWD, K, BLOCKS, T], BF16)
        dist = sb("s_dist", [P, HATS], F32)
        prod = sb("s_prod", [P, 2, 2, T], F32)
        dcn = sb("s_dcn", [P, K, T], F32)
        res = sb("s_res", [P, K, T], F32)
        spread = pb("s_spread", [P, 2, 2, T], F32)
        acc = pb("s_acc", [P, 2, T], F32)
        tps = pb("s_tps", [P, 2 * T], BF16)
        out_ps = pb("s_out_ps", [P, T], F32)
        consts = sem("s_consts")
        sel_ready = sem("s_sel_ready")
        img_loaded = [sem("s_img_loaded0"), sem("s_img_loaded1")]
        off_loaded = sem("s_off_loaded")
        res_loaded = sem("s_res_loaded")
        stored = sem("s_stored")
        dist_ready = sem("s_dist_ready")
        hat_step = sem("s_hat_step")
        masked = sem("s_masked")
        outer_ready = sem("s_outer_ready")
        added = sem("s_added")
        part_cast = sem("s_part_cast")
        part_left = sem("s_part_left")
        transposed = sem("s_transposed")
        wtt_ready = sem("s_wtt_ready")
        spread_ready = sem("s_spread_ready")
        multiplied = sem("s_multiplied")
        summed = sem("s_summed")
        acc_read = sem("s_acc_read")
        out_filled = sem("s_out_filled")
        out_ready = sem("s_out_ready")
        block = ctx.enter_context(nc.Block())
        CH = B * NT
        NB = K * BLOCKS
        NP = K * PAIRS
        OUT_AT = (3, 6, 9, 12)

        def units(eng, run):
            run(0, 0, False, True, True)
            run(1, 1, True, True, True)
            with eng.Fori(1, CH // 2 - 1) as i:
                run(2 * i, 0, True, True, True)
                run(2 * i + 1, 1, True, True, True)
            run(CH - 2, 0, True, True, False)
            run(CH - 1, 1, True, False, False)

        def block_rows(blk):
            return min(PER_BLOCK, D - blk * PER_BLOCK) * ROWD

        def part_view(i):
            return wtp[:, :, :, :].rearrange("p t k (d q g) -> p (t k) d q g", q=PARTS, g=GK)[:, :, :, i, :]

        def weight_view():
            return wts[:, :, :, :].rearrange("p (a g) y x -> p a (y x) g", g=GK)

        @block.sync
        def _(sp):
            sel_f = wts[0:PER_BLOCK * ROWD, 0:27, :, :].rearrange("p a b c -> p (a b c)")[:, 0:PER_BLOCK * P]
            for dst, src in ((vec[:, :, :], vectors[:, OUT_B:OUT_B + 1, :]), (w[:, :, :], w_out), (sel_f, sel_tab), (ident[:, :], ident_mat)):
                sp.dma_start(dst, src).then_inc(consts, 16)

            def load_image(n, u):
                sp.dma_start(img[:, u], xproj[:, bass.ds((n // NT) * K, K), bass.ds((n % NT) * (ROWS * PADW), (ROWS + 2 * REACH) * PADW)]).then_inc(img_loaded[u], 16)

            def load_offsets(n):
                sp.dma_start(off[:, :, :], offsets[:, bass.ds(n * TT, TT), :]).then_inc(off_loaded, 16)
                sp.dma_start(msk[:, :, :], masks[:, bass.ds(n * TT, TT), :]).then_inc(off_loaded, 16)

            def run(n, u, has_prev, has_1, has_2):
                if has_1:
                    wait(sp, multiplied, NP * n)
                    load_image(n + 1, 1 - u)
                if has_2:
                    sp.wait_ge(masked, n + 2)
                    load_offsets(n + 2)
                if has_prev:
                    sp.wait_ge(out_ready, K * n)
                    sp.dma_start(outv[:, bass.ds(((n - 1) // NT) * K, K), bass.ds(((n - 1) % NT) * T, T)], res[:, :, :]).then_inc(stored, 16)
                    sp.wait_ge(stored, 16 * n)
                sp.dma_start(res[:, :, :], x2[:, bass.ds((n // NT) * K, K), bass.ds((n % NT) * T, T)]).then_inc(res_loaded, 16)

            outv = out.rearrange("b (k p) h w -> p (b k) (h w)", p=P)
            load_image(0, 0)
            load_offsets(0)
            sp.wait_ge(masked, 1)
            load_offsets(1)
            units(sp, run)
            sp.wait_ge(out_ready, K * CH)
            sp.dma_start(outv[:, SEQ - K:SEQ, HW - T:HW], res[:, :, :]).then_inc(stored, 16)
            sp.wait_ge(stored, 16 * CH)

        @block.scalar
        def _(act):
            act.wait_ge(consts, 64)
            sel_f = wts[0:PER_BLOCK * ROWD, 0:27, :, :].rearrange("p a b c -> p (a b c)")[:, 0:PER_BLOCK * P]
            nc.scalar.activation(sel[:, :, :].rearrange("p a b -> p (a b)"), sel_f, ACT.Copy).then_inc(sel_ready, 1)
            nc.scalar.activation(identb[:, :], ident[:, :], ACT.Copy).then_inc(sel_ready, 1)

            def hats(n):
                act.wait_ge(off_loaded, 32 * n + 32)
                wait(act, outer_ready, PTS * n)
                o = off[:, :, :].rearrange("p t (q c) -> p (t q) c", c=2)
                for c, dst in ((0, hx), (1, hy)):
                    for r in range(HATS):
                        a = nc.scalar.activation(dst[:, :, :, r].rearrange("p a b -> p (a b)"), o[:, :, c], ACT.Abs, bias=dist[:, r:r + 1])
                a.then_inc(hat_step, 1)
                act.wait_ge(hat_step, 2 * n + 1)
                for dst in (hx, hy):
                    d = dst[:, :, :, :].rearrange("p a b c -> p (a b c)")
                    a = nc.scalar.activation(d, d, ACT.Relu, scale=-1.0, bias=1.0)
                a.then_inc(hat_step, 1)

            def cast_part(n, i):
                if i == 0:
                    act.wait_ge(added, 10 * n + 10)
                    wait(act, transposed, NB * n)
                else:
                    act.wait_ge(part_left, 2 * n + 1)
                nc.scalar.activation(part_view(i), weight_view(), ACT.Copy).then_inc(part_cast, 1)

            def copy_block(n, i):
                k, blk = divmod(i, BLOCKS)
                rows = block_rows(blk)
                act.wait_ge(transposed, NB * n + i + 1)
                nc.scalar.activation(wtt[0:rows, k, blk, :], tps[0:rows, 0:T], ACT.Copy).then_inc(wtt_ready, 1)

            def run(n, u, has_prev, has_1, has_2):
                if has_1:
                    cast_part(n + 1, 0)
                    cast_part(n + 1, 1)
                for k in range(K):
                    for blk in range(BLOCKS):
                        if has_1:
                            copy_block(n + 1, k * BLOCKS + blk)
                        if has_2 and (k, blk) == (0, 0):
                            hats(n + 2)
                    act.wait_ge(summed, NP * n + PAIRS * (k + 1))
                    wait(act, out_filled, K * n)
                    nc.scalar.activation(dcn[:, k, :], acc[:, k % 2, :], ACT.Copy).then_inc(acc_read, 1)

            act.wait_ge(dist_ready, HATS)
            hats(0)
            cast_part(0, 0)
            cast_part(0, 1)
            for i in range(NB):
                copy_block(0, i)
            hats(1)
            units(act, run)

        @block.gpsimd
        def _(pool):
            for r in range(HATS):
                nc.gpsimd.memset(dist[:, r:r + 1], float(HATS // 2 - r)).then_inc(dist_ready, 1)

            def masked_hats(n):
                pool.wait_ge(hat_step, 2 * n + 2)
                nc.gpsimd.tensor_tensor(hy[:, :, :, :].rearrange("p a b c -> p (a b) c"), hy[:, :, :, :].rearrange("p a b c -> p (a b) c"),
                                        msk[:, :, :].rearrange("p a b -> p (a b)").unsqueeze(2).broadcast_to([P, TT * G * PTS, HATS]),
                                        ALU.mult).then_inc(masked, 1)
                pool.wait_ge(masked, n + 1)

            def outer_product(n, q):
                wait(pool, added, 10 * n + q)
                nc.gpsimd.tensor_tensor(outer[:, q % 2], hy[:, :, q, :].unsqueeze(3).broadcast_to([P, TT * G, HATS, HATS]),
                                        hx[:, :, q, :].unsqueeze(2).broadcast_to([P, TT * G, HATS, HATS]), ALU.mult).then_inc(outer_ready, 1)

            def weights(n):
                masked_hats(n)
                for q in range(PTS):
                    outer_product(n, q)

            def run(n, u, has_prev, has_1, has_2):
                if has_2:
                    weights(n + 2)

            weights(0)
            weights(1)
            units(pool, run)

        @block.vector
        def _(dve):
            def clear_window(n):
                wait(dve, part_left, 2 * n)
                nc.vector.memset(wts[:, :, :, :].rearrange("p a b c -> p (a b c)"), 0.0).then_inc(added, 1)

            def add_point(n, q):
                ix, iy = divmod(q, 3)
                dve.wait_ge(outer_ready, PTS * n + q + 1)
                dve.wait_ge(added, 10 * n + q + 1)
                v = wts[:, :, iy:iy + HATS, ix:ix + HATS]
                nc.vector.tensor_tensor(v, v, outer[:, q % 2], ALU.add).then_inc(added, 1)

            def leave_part(n, i):
                dve.wait_ge(part_cast, 2 * n + i + 1)
                nc.vector.tensor_tensor(weight_view() if i == 0 else part_view(2), weight_view(), part_view(i), ALU.subtract).then_inc(part_left, 1)

            def finish_output(n, o):
                dve.wait_ge(out_filled, K * n + o + 1)
                dve.wait_ge(res_loaded, 16 * n + 16)
                nc.vector.scalar_tensor_tensor(res[:, o, :], out_ps[:, :], vec[:, 0, o:o + 1], res[:, o, :], ALU.add, ALU.add).then_inc(out_ready, 1)

            def run(n, u, has_prev, has_1, has_2):
                dve.wait_ge(img_loaded[u], 16 * ((n + 2) // 2) if isinstance(n, int) else 8 * (n - u) + 16)
                for i in range(NP):
                    k, pair = divmod(i, PAIRS)
                    d0 = 2 * pair
                    ds = [d for d in (d0, d0 + 1) if d < D]
                    at = [(d // WIN) * PADW + d % WIN for d in ds]
                    dve.wait_ge(spread_ready, NP * n + i + 1)
                    wait(dve, summed, NP * n + i - 1)
                    nc.vector.tensor_tensor(
                        prod[:, i % 2, 0:len(ds), :].rearrange("p a (r c) -> p a r c", c=IMG),
                        spread[:, i % 2, 0:len(ds), :].rearrange("p a (r c) -> p a r c", c=IMG),
                        window(u, k, at), ALU.mult).then_inc(multiplied, 1)
                    if has_1 and i in (0, 2):
                        leave_part(n + 1, i // 2)
                    if has_prev and i in OUT_AT:
                        finish_output(n - 1, OUT_AT.index(i))
                    if has_2 and i >= 20 and i % 6 == 2 and (i - 20) // 6 < 10:
                        q = (i - 20) // 6
                        if q == 0:
                            clear_window(n + 2)
                        else:
                            add_point(n + 2, q - 1)

            def window(u, k, at):
                base = img[:, u, k, at[0]:at[0] + 1]
                steps = [[at[1] - at[0], 2]] if len(at) == 2 else [[1, 1]]
                return bass.AP(tensor=base.tensor, offset=base.offset, ap=[list(base.ap[0])] + steps + [[PADW, ROWS], [1, IMG]])

            def weights(n):
                clear_window(n)
                for q in range(PTS):
                    add_point(n, q)

            dve.wait_ge(sel_ready, 2)
            weights(0)
            leave_part(0, 0)
            leave_part(0, 1)
            weights(1)
            units(dve, run)
            for o in range(K):
                finish_output(CH - 1, o)

        @block.tensor
        def _(pe):
            def transpose_block(n, i):
                k, blk = divmod(i, BLOCKS)
                rows = block_rows(blk)
                if i == 0:
                    pe.wait_ge(part_left, 2 * n + 2)
                wait(pe, wtt_ready, NB * n + i)
                for t in range(TT):
                    mm = nc.tensor.transpose(tps[0:rows, t * P:(t + 1) * P], wtp[:, t, k, blk * PER_BLOCK * ROWD:blk * PER_BLOCK * ROWD + rows], identb[:, :])
                mm.then_inc(transposed, 1)

            def spread_pair(n, i):
                k, pair = divmod(i, PAIRS)
                blk = 2 * pair // PER_BLOCK
                rows = block_rows(blk)
                pe.wait_ge(wtt_ready, NB * n + k * BLOCKS + blk + 1)
                wait(pe, multiplied, NP * n + i - 1)
                for a, d in enumerate(d for d in (2 * pair, 2 * pair + 1) if d < D):
                    mm = nc.tensor.matmul(spread[:, i % 2, a, :], sel[0:rows, d % PER_BLOCK, :], wtt[0:rows, k, blk, :], start=True, stop=True)
                mm.then_inc(spread_ready, 1)

            def sum_pair(n, i):
                k, pair = divmod(i, PAIRS)
                pe.wait_ge(multiplied, NP * n + i + 1)
                if pair == 0:
                    wait(pe, acc_read, K * n + k - 1)
                ds = [d for d in (2 * pair, 2 * pair + 1) if d < D]
                for a, d in enumerate(ds):
                    mm = nc.tensor.matmul(acc[:, k % 2, :], ident[:, :], prod[:, i % 2, a, :], start=d == 0, stop=d == D - 1)
                mm.then_inc(summed, 1)

            def project_out(n, o):
                pe.wait_ge(acc_read, K * n + K)
                wait(pe, out_ready, K * n + o)
                for k in range(K):
                    mm = nc.tensor.matmul(out_ps[:, :], w[:, k, o * P:(o + 1) * P], dcn[:, k, :], start=k == 0, stop=k == K - 1)
                mm.then_inc(out_filled, 1)

            def run(n, u, has_prev, has_1, has_2):
                for i in range(NP):
                    if i == 0:
                        spread_pair(n, 0)
                    if i + 1 < NP:
                        spread_pair(n, i + 1)
                    sum_pair(n, i)
                    if has_prev and i + 1 in OUT_AT:
                        project_out(n - 1, OUT_AT.index(i + 1))
                    k, pair = divmod(i, PAIRS)
                    if has_1 and (pair % (PER_BLOCK // 2) == PER_BLOCK // 2 - 1 or pair == PAIRS - 1):
                        transpose_block(n + 1, k * BLOCKS + pair // (PER_BLOCK // 2))

            pe.wait_ge(consts, 64)
            pe.wait_ge(sel_ready, 2)
            for i in range(NB):
                transpose_block(0, i)
            units(pe, run)
            for o in range(K):
                project_out(CH - 1, o)


CORNERS = 4
CG = C // G
PIX = PADW * PADW


def phase_sample_any(nc, sem, x2, xproj, offsets, masks, peak, table, out, vectors, w_out, ident_mat, grid_tab):
    with ExitStack() as ctx:
        sb = lambda n, s, d: ctx.enter_context(nc.sbuf_tensor(n, s, d))
        pb = lambda n, s, d: ctx.enter_context(nc.psum_tensor(n, s, d))
        TILES = B * HW // P
        PX = 100
        GRID = 2 * PTS + G + 2 * TILES
        peaks = sb("g_peaks", [P, B * NT], F32)
        top = sb("g_top", [P, 2], F32)
        flag = sb("g_flag", [P, 1], I32)
        peak_loaded = sem("g_peak_loaded")
        peak_step = sem("g_peak_step")

        with nc.Block() as block:
            @block.sync
            def _(sp):
                sp.dma_start(peaks[:, :], peak).then_inc(peak_loaded, 16)

            @block.vector
            def _(dve):
                dve.wait_ge(peak_loaded, 16)
                nc.vector.tensor_reduce(top[:, 0:1], peaks[:, :], AX.X, ALU.max).then_inc(peak_step, 1)
                dve.wait_ge(peak_step, 2)
                nc.vector.tensor_scalar(flag[:, :], top[:, 1:2], 2.0, None, ALU.is_gt).then_inc(peak_step, 1)

            @block.gpsimd
            def _(pool):
                pool.wait_ge(peak_step, 1)
                nc.gpsimd.partition_all_reduce(top[:, 1:2], top[:, 0:1], P, bass.bass_isa.ReduceOp.max).then_inc(peak_step, 1)

        vec = sb("g_vec", [P, 1, K], F32)
        w = sb("g_w", [P, K, C], F32)
        ident = sb("g_ident", [P, P], F32)
        grid = sb("g_grid", [P, GRID], F32)
        img = sb("g_img", [P, PIX], F32)
        tr = sb("g_tr", [PX, P], F32)
        off = sb("g_off", [P, NOFF], F32)
        msk = sb("g_msk", [P, NMASK], F32)
        pos = sb("g_pos", [P, 2, NMASK], F32)
        low = sb("g_low", [P, 2, NMASK], F32)
        lowi = sb("g_lowi", [P, 2, NMASK], I32)
        over = sb("g_over", [P, 2, NMASK], F32)
        cw = sb("g_cw", [P, CORNERS, NMASK], F32)
        row = sb("g_row", [P, NMASK], F32)
        cwg = sb("g_cwg", [P, CORNERS, PTS], F32)
        rowg = sb("g_rowg", [P, CORNERS, PTS], I32)
        got = sb("g_got", [P, CORNERS * PTS, CG], F32)
        sampled = sb("g_sampled", [P, C], F32)
        dcn = sb("g_dcn", [P, K, P], F32)
        res = sb("g_res", [P, K, P], F32)
        ps = pb("g_ps", [P, T], F32)
        consts = sem("g_consts")
        img_loaded = sem("g_img_loaded")
        tr_ready = sem("g_tr_ready")
        tr_copied = sem("g_tr_copied")
        table_stored = sem("g_table_stored")
        table_done = sem("g_table_done")
        tile_loaded = sem("g_tile_loaded")
        step = sem("g_step")
        rows_ready = sem("g_rows_ready")
        gathered = sem("g_gathered")
        group_started = sem("g_group_started")
        group_gathered = sem("g_group_gathered")
        cwg_ready = sem("g_cwg_ready")
        products = sem("g_products")
        group_done = sem("g_group_done")
        flipped = sem("g_flipped")
        flip_copied = sem("g_flip_copied")
        out_filled = sem("g_out_filled")
        out_ready = sem("g_out_ready")
        stored = sem("g_stored")
        tile_stored = sem("g_tile_stored")
        block = ctx.enter_context(nc.Block())
        STEPS = 16
        outv = out.rearrange("b (k p) h w -> p (b k) (h w)", p=P)

        table_v = table.rearrange("(g q) c -> q g c", q=PIX)

        @block.sync
        def _(sp):
            with sp.If(sp.value_load(flag[0:1, 0:1], min_val=0, max_val=1) > 0):
                for dst, src in ((vec[:, :, :], vectors[:, OUT_B:OUT_B + 1, :]), (w[:, :, :], w_out), (ident[:, :], ident_mat), (grid[:, :], grid_tab)):
                    sp.dma_start(dst, src).then_inc(consts, 16)
                with sp.Fori(0, SEQ) as r:
                    sp.wait_ge(tr_ready, (PIX // PX) * r)
                    sp.dma_start(img[:, :], xproj[:, bass.ds(r, 1), :].rearrange("p o t -> p (o t)")).then_inc(img_loaded, 16)
                    with sp.Fori(0, PIX // PX) as i:
                        sp.wait_ge(tr_copied, r * (PIX // PX) + i + 1)
                        sp.dma_start(table_v[bass.ds(i * PX, PX), bass.ds(r * GK, GK), :], tr[:, :].rearrange("q (g c) -> q g c", c=CG)).then_inc(table_stored, 16)
                        sp.wait_ge(table_stored, (r * (PIX // PX) + i) * 16 + 16)
                        sp.sem_inc(table_done, 1)
                with sp.Fori(0, TILES) as n:
                    slabs = sp.snap((n // (HW // P)) * K)
                    pixels = sp.snap((n % (HW // P)) * P)
                    sp.wait_ge(out_ready, K * n)
                    sp.dma_start(off[:, :], offsets[:, bass.ds(n, 1), :].rearrange("p o q -> p (o q)")).then_inc(tile_loaded, 16)
                    sp.dma_start(msk[:, :], masks[:, bass.ds(n, 1), :].rearrange("p o q -> p (o q)")).then_inc(tile_loaded, 16)
                    sp.dma_start(res[:, :, :], x2[:, bass.ds(slabs, K), bass.ds(pixels, P)]).then_inc(tile_loaded, 16)
                    sp.wait_ge(out_ready, K * n + K)
                    sp.dma_start(outv[:, bass.ds(slabs, K), bass.ds(pixels, P)], res[:, :, :]).then_inc(stored, 16)
                    sp.wait_ge(stored, 16 * n + 16)
                    sp.sem_inc(tile_stored, 1)

        @block.tensor
        def _(pe):
            with pe.If(pe.value_load(flag[0:1, 0:1], min_val=0, max_val=1) > 0):
                pe.wait_ge(consts, 64)
                with pe.Fori(0, SEQ) as r:
                    pe.wait_ge(img_loaded, 16 * r + 16)
                    for i in range(PIX // PX):
                        pe.wait_ge(tr_copied, r * (PIX // PX) + i)
                        nc.tensor.transpose(ps[0:PX, 0:P], img[:, i * PX:(i + 1) * PX], ident[:, :]).then_inc(tr_ready, 1)
                with pe.Fori(0, TILES) as n:
                    pe.wait_ge(group_done, G * n + G)
                    for k in range(K):
                        pe.wait_ge(flip_copied, K * n + k)
                        if k == 0:
                            pe.wait_ge(out_ready, K * n)
                        nc.tensor.transpose(ps[:, 0:P], sampled[:, k * P:(k + 1) * P], ident[:, :]).then_inc(flipped, 1)
                    pe.wait_ge(flip_copied, K * n + K)
                    for o in range(K):
                        pe.wait_ge(out_ready, K * n + o)
                        for k in range(K):
                            mm = nc.tensor.matmul(ps[:, 0:P], w[:, k, o * P:(o + 1) * P], dcn[:, k, :], start=k == 0, stop=k == K - 1)
                        mm.then_inc(out_filled, 1)

        @block.scalar
        def _(act):
            with act.If(act.value_load(flag[0:1, 0:1], min_val=0, max_val=1) > 0):
                with act.Fori(0, SEQ * PIX // PX) as i:
                    act.wait_ge(tr_ready, i + 1)
                    act.wait_ge(table_done, i)
                    nc.scalar.activation(tr[:, :], ps[0:PX, 0:P], ACT.Copy).then_inc(tr_copied, 1)
                with act.Fori(0, TILES) as n:
                    for k in range(K):
                        act.wait_ge(flipped, K * n + k + 1)
                        nc.scalar.activation(dcn[:, k, :], ps[:, 0:P], ACT.Copy).then_inc(flip_copied, 1)

        @block.gpsimd
        def _(pool):
            with pool.If(pool.value_load(flag[0:1, 0:1], min_val=0, max_val=1) > 0):
                pool.wait_ge(table_done, SEQ * PIX // PX)
                with pool.Fori(0, TILES) as n:
                    with pool.Fori(0, G) as g:
                        pool.wait_ge(rows_ready, n * G + g + 1)
                        pool.sem_inc(group_started, 1)
                        for q in range(CORNERS * PTS):
                            nc.gpsimd.indirect_dma_start(
                                out=got[:, q, :], out_offset=None, in_=table,
                                in_offset=bass.IndirectOffsetOnAxis(ap=rowg[:, q // PTS, q % PTS:q % PTS + 1], axis=0),
                            ).then_inc(gathered, 16)
                        pool.wait_ge(gathered, 16 * CORNERS * PTS)
                        pool.dma_reset(range(gathered.num, gathered.num + 1))
                        pool.sem_clear(gathered)
                        pool.sem_inc(group_gathered, 1)

        @block.vector
        def _(dve):
            with dve.If(dve.value_load(flag[0:1, 0:1], min_val=0, max_val=1) > 0):
                v = nc.vector
                dve.wait_ge(consts, 64)
                with dve.Fori(0, TILES) as n:
                    done = [0]

                    def link(ins):
                        done[0] += 1
                        ins.then_inc(step, 1)
                        dve.wait_ge(step, STEPS * n + done[0])

                    dve.wait_ge(tile_loaded, 48 * n + 48)
                    for c in range(2):
                        o = off[:, :].rearrange("p (g q c) -> p g q c", q=PTS, c=2)[:, :, :, c]
                        at = grid[:, c * PTS:(c + 1) * PTS].unsqueeze(1).broadcast_to([P, G, PTS])
                        link(v.tensor_tensor(pos[:, c, :].rearrange("p (g q) -> p g q", q=PTS), o, at, ALU.add))
                    tile_y = grid[:, bass.ds(2 * PTS + G + n, 1)].broadcast_to([P, NMASK])
                    link(v.tensor_tensor(pos[:, 1, :], pos[:, 1, :], tile_y, ALU.add))
                    link(v.tensor_scalar(pos[:, :, :], pos[:, :, :], float(REACH - 1), float(REACH + IMG), ALU.max, ALU.min))
                    link(v.tensor_copy(lowi[:, :, :], pos[:, :, :]))
                    link(v.tensor_copy(low[:, :, :], lowi[:, :, :]))
                    link(v.tensor_tensor(over[:, :, :], low[:, :, :], pos[:, :, :], ALU.is_gt))
                    link(v.tensor_tensor(low[:, :, :], low[:, :, :], over[:, :, :], ALU.subtract))
                    link(v.tensor_tensor(pos[:, :, :], pos[:, :, :], low[:, :, :], ALU.subtract))
                    link(v.tensor_tensor(over[:, 1, :], msk[:, :], pos[:, 1, :], ALU.mult))
                    link(v.tensor_tensor(over[:, 0, :], msk[:, :], over[:, 1, :], ALU.subtract))
                    fx = pos[:, 0, :].unsqueeze(1).broadcast_to([P, 2, NMASK])
                    link(v.tensor_tensor(cw[:, 1:4:2, :], over[:, :, :], fx, ALU.mult))
                    link(v.tensor_tensor(cw[:, 0:4:2, :], over[:, :, :], cw[:, 1:4:2, :], ALU.subtract))
                    link(v.scalar_tensor_tensor(row[:, :], low[:, 1, :], float(PADW), low[:, 0, :], ALU.mult, ALU.add))
                    link(v.tensor_tensor(row[:, :].rearrange("p (g q) -> p g q", q=PTS), row[:, :].rearrange("p (g q) -> p g q", q=PTS),
                                         grid[:, 2 * PTS:2 * PTS + G].unsqueeze(2).broadcast_to([P, G, PTS]), ALU.add))
                    tile_row = grid[:, bass.ds(2 * PTS + G + TILES + n, 1)].broadcast_to([P, NMASK])
                    v.tensor_tensor(row[:, :], row[:, :], tile_row, ALU.add).then_inc(step, 1)
                    assert done[0] + 1 == STEPS
                    with dve.Fori(0, G) as g:
                        dve.wait_ge(step, STEPS * n + STEPS)
                        dve.wait_ge(group_gathered, n * G + g)
                        for c, move in enumerate((0, 1, PADW, PADW + 1)):
                            i = v.tensor_scalar(rowg[:, c, :], row[:, bass.ds(g * PTS, PTS)], float(move), None, ALU.add)
                        i.then_inc(rows_ready, 1)
                        i = v.tensor_scalar(cwg[:, :, :], cw[:, :, bass.ds(g * PTS, PTS)], 1.0, None, ALU.mult).then_inc(cwg_ready, 1)
                        dve.wait_ge(cwg_ready, n * G + g + 1)
                        dve.wait_ge(group_gathered, n * G + g + 1)
                        v.tensor_tensor(got[:, :, :], got[:, :, :], cwg[:, :, :].rearrange("p a b -> p (a b)").unsqueeze(2).broadcast_to([P, CORNERS * PTS, CG]),
                                        ALU.mult).then_inc(products, 1)
                        dve.wait_ge(products, n * G + g + 1)
                        v.tensor_reduce(sampled[:, bass.ds(g * CG, CG)], got[:, :, :].rearrange("p a b -> p b a"), AX.X, ALU.add).then_inc(group_done, 1)
                    for o in range(K):
                        dve.wait_ge(out_filled, K * n + o + 1)
                        v.scalar_tensor_tensor(res[:, o, :], ps[:, 0:P], vec[:, 0, o:o + 1], res[:, o, :], ALU.add, ALU.add).then_inc(out_ready, 1)


def build(nc, x, vectors, mvec, w_in, w_conv, w_x, w_dtr, w_dt, w_out, a_log, w_proj, l1_in_w, dw_w, w_om, b_om, l1_out_w,
          ones_mat, group_mat, ident_mat, keep_tab, bc_sel, point_sel, grid_tab, out):
    dram = lambda name, shape: nc.dram_tensor(name, shape, F32, kind="Internal").ap()
    xn = dram("xn_scratch", (P, UNITS, T))
    halo = dram("halo_scratch", (P, UNITS + 1, 3))
    ym = dram("ym_scratch", (P, UNITS, T))
    x2 = dram("x2_scratch", (P, SEQ, HW))
    stats = dram("stats_scratch", (P, SEQ, NT, 6))
    xproj = dram("xproj_scratch", (P, SEQ, PADW * PADW))
    offsets = dram("offsets_scratch", (P, B * HW // P, NOFF))
    masks = dram("masks_scratch", (P, B * HW // P, NMASK))
    peak = dram("peak_scratch", (P, B * NT))
    table = dram("table_scratch", (B * G * PADW * PADW, CG))
    with ExitStack() as ctx:
        sem = lambda name: ctx.enter_context(nc.semaphore(name))
        phase_input_norm(nc, sem, x, xn.rearrange("p (r t) c -> p r (t c)", t=NT), halo, vectors, ones_mat, group_mat)
        phase_mamba(nc, sem, xn, halo, ym, w_in, w_conv, w_x, w_dtr, w_dt, w_out, a_log, mvec, keep_tab, bc_sel, ident_mat)
        phase_project(nc, sem, ym, x, x2, stats, vectors, w_proj, ones_mat)
        phase_offsets(nc, sem, x2, stats, xproj, offsets, masks, peak, vectors, l1_in_w, dw_w, w_om, b_om, ones_mat, group_mat)
        phase_sample(nc, sem, x2, xproj, offsets, masks, out, vectors, l1_out_w, point_sel, ident_mat)
        phase_sample_any(nc, sem, x2, xproj, offsets, masks, peak, table, out, vectors, l1_out_w, ident_mat, grid_tab)


def laid_out(inputs):
    at = np.ascontiguousarray
    l0 = lambda name: np.asarray(inputs["L0_conv_" + name])
    l1 = lambda name: np.asarray(inputs["L1_conv_" + name])
    columns = lambda v: v.reshape(-1, P).T
    rows = lambda m: at(m.reshape(-1, P, m.shape[1]).transpose(1, 0, 2))
    f32 = np.float32
    x_proj = l0("x_proj_w")
    bc_sel = np.zeros((PARTS * 2 * NS, 2 * NS, P), f32)
    for r in range(2 * NS):
        for part in range(PARTS):
            bc_sel[part * 2 * NS + r, r] = 1
    point_sel = np.zeros((PER_BLOCK * ROWD, PER_BLOCK, P), f32)
    for d in range(PER_BLOCK):
        for part in range(PARTS):
            for g in range(GK):
                point_sel[d * ROWD + part * GK + g, d, g * CG:(g + 1) * CG] = 1
    keep = np.ones((P, UNITS), f32)
    keep[:, ::NT] = 0
    group = np.zeros((P, P), f32)
    per = C // 32
    for g in range(P // per):
        group[g * per:(g + 1) * per, g * per:(g + 1) * per] = 1.0 / per
    pixel, point, tile = np.arange(P), np.arange(PTS), np.arange(B * HW // P)
    per_image = HW // P
    grid = np.concatenate([
        (pixel % IMG)[:, None] + (point // 3 - 1)[None] + REACH,
        (pixel // IMG)[:, None] + (point % 3 - 1)[None] + REACH,
        np.broadcast_to(np.arange(G) * PADW * PADW, (P, G)),
        np.broadcast_to((P // IMG) * (tile % per_image), (P, tile.size)),
        np.broadcast_to((tile // per_image) * G * PADW * PADW, (P, tile.size)),
    ], 1).astype(f32)
    return {
        "x": at(np.asarray(inputs["x"])),
        "vectors": at(np.stack([columns(v) for v in (l0("norm_g"), l0("norm_b"), l0("proj_b"), l1("dw_b"), l1("ln_g"), l1("ln_b"), l1("in_b"), l1("out_b"))], 1)),
        "mvec": at(np.concatenate([columns(l0("conv_b")), columns(l0("dt_proj_b")), columns(l0("D_param")), np.broadcast_to(l0("skip_scale")[None], (P, 1))], 1)),
        "w_in": at(l0("in_proj_w").T),
        "w_conv": at(l0("conv_w").T).reshape(-1),
        "w_x": at(np.tile(rows(x_proj[RANK:].T), (1, 1, PARTS))),
        "w_dtr": rows(x_proj[:RANK].T),
        "w_dt": at(l0("dt_proj_w").T),
        "w_out": rows(l0("out_proj_w").T),
        "a_log": rows(l0("A_log")),
        "w_proj": rows(l0("proj_w").T),
        "l1_in_w": rows(l1("in_w")),
        "dw_w": rows(l1("dw_w").reshape(C, 9)),
        "w_om": rows(np.concatenate([l1("off_w"), l1("mask_w")], 1)),
        "b_om": at(np.concatenate([l1("off_b"), l1("mask_b")])),
        "l1_out_w": rows(l1("out_w")),
        "ones_mat": np.full((P, P), 1.0 / C, f32),
        "group_mat": group,
        "ident_mat": np.eye(P, dtype=f32),
        "keep_tab": keep,
        "bc_sel": bc_sel.reshape(PARTS * 2 * NS, -1),
        "point_sel": point_sel.reshape(PER_BLOCK * ROWD, -1),
        "grid_tab": grid,
    }


def kernel(**inputs):
    import concourse.bacc as _bacc
    from concourse.bass_utils import run_bass_kernel_spmd as _run

    nc = _bacc.Bacc("TRN2", target_bir_lowering=False, num_devices=1)
    arrays = laid_out(inputs)
    args = [nc.dram_tensor(f"in_{name}", a.shape, mybir.dt.from_np(a.dtype), kind="ExternalInput").ap() for name, a in arrays.items()]
    out = nc.dram_tensor("out_0_dram", (B, C, IMG, IMG), F32, kind="ExternalOutput").ap()
    build(nc, *args, out)
    r = _run(nc, [{f"in_{name}": a for name, a in arrays.items()}], core_ids=[0])
    return r.results[0]["out_0_dram"]
```

```python
import numpy as np
import concourse.bass as bass
from concourse import mybir
from contextlib import ExitStack

F32 = mybir.dt.float32
BF16 = mybir.dt.bfloat16
I32 = mybir.dt.int32
ALU = mybir.AluOpType
ACT = mybir.ActivationFunctionType
AX = mybir.AxisListType

B, C, HW = 4, 512, 4096
IMG = 64
P = 128
K = C // P
T = 512
NT = HW // T
SEQ = B * K
GN_EPS, LN_EPS = 1e-5, 1e-5
NORM_G, NORM_B, PROJ_B, DW_B, LN_G, LN_B, IN_B, OUT_B = range(8)


def over_slabs(ap):
    return ap.unsqueeze(1).broadcast_to([P, K, T])


class LayerNorm:

    def __init__(self, nc, name, sb, pb, sem, x, ones):
        self.nc, self.x, self.ones = nc, x, ones
        self.sq = sb(name + "_sq", [P, 2, K, T], F32)
        self.stat = pb(name + "_stat", [P, 2, T], F32)
        self.rstd = sb(name + "_rstd", [P, 2, T], F32)
        self.input_ready = sem(name + "_input_ready")
        self.mean_ready = sem(name + "_mean_ready")
        self.centred = sem(name + "_centred")
        self.squared = sem(name + "_squared")
        self.var_ready = sem(name + "_var_ready")
        self.std_ready = sem(name + "_std_ready")
        self.rstd_ready = sem(name + "_rstd_ready")
        self.scaled = sem(name + "_scaled")

    def pe_mean(self, pe, u, c):
        pe.wait_ge(self.input_ready, c + 1)
        for k in range(K):
            mm = self.nc.tensor.matmul(self.stat[:, u, :], self.ones[:, :], self.x[:, u, k, :], start=k == 0, stop=k == K - 1)
        mm.then_inc(self.mean_ready, 1)

    def dve_centre(self, dve, u, c):
        dve.wait_ge(self.mean_ready, c + 1)
        self.nc.vector.tensor_tensor(self.x[:, u], self.x[:, u], over_slabs(self.stat[:, u, :]), ALU.subtract).then_inc(self.centred, 1)

    def act_square(self, act, u, c):
        act.wait_ge(self.centred, c + 1)
        self.nc.scalar.activation(self.sq[:, u], self.x[:, u], ACT.Square).then_inc(self.squared, 1)

    def pe_var(self, pe, u, c):
        pe.wait_ge(self.squared, c + 1)
        for k in range(K):
            mm = self.nc.tensor.matmul(self.stat[:, u, :], self.ones[:, :], self.sq[:, u, k, :], start=k == 0, stop=k == K - 1)
        mm.then_inc(self.var_ready, 1)

    def act_std(self, act, u, c, eps):
        act.wait_ge(self.var_ready, c + 1)
        self.nc.scalar.activation(self.rstd[:, u, :], self.stat[:, u, :], ACT.Sqrt, bias=eps).then_inc(self.std_ready, 1)

    def dve_scale(self, dve, u, c):
        dve.wait_ge(self.std_ready, c + 1)
        self.nc.vector.reciprocal(self.rstd[:, u, :], self.rstd[:, u, :]).then_inc(self.rstd_ready, 1)
        dve.wait_ge(self.rstd_ready, c + 1)
        self.nc.vector.tensor_tensor(self.x[:, u], self.x[:, u], over_slabs(self.rstd[:, u, :]), ALU.mult).then_inc(self.scaled, 1)


def finish_group_norm(nc, sb, pb, sem, block, name, stats, group_avg, ready, eps_col):
    mv = sb(name + "_mv", [P, SEQ, 2], F32)
    mom = sb(name + "_mom", [P, 2, SEQ], F32)
    grp = sb(name + "_grp", [P, 2, SEQ], F32)
    aff = sb(name + "_aff", [P, 2, SEQ], F32)
    grp_ps = pb(name + "_grp_ps", [P, 2, SEQ], F32)
    step = sem(name + "_step")
    averaged = sem(name + "_averaged")
    rooted = sem(name + "_rooted")

    def dve_part(dve):
        n = [0]

        def link(ins):
            n[0] += 1
            ins.then_inc(step, 1)
            dve.wait_ge(step, n[0])

        if ready is not None:
            dve.wait_ge(*ready)
        for r in range(SEQ):
            nc.vector.bn_aggr(mv[:, r, :], stats[:, r, :, :].rearrange("p a b -> p (a b)")).then_inc(step, 1)
        n[0] = SEQ
        dve.wait_ge(step, SEQ)
        link(nc.vector.tensor_copy(mom[:, 0, :], mv[:, :, 0]))
        link(nc.vector.tensor_tensor(mom[:, 1, :], mv[:, :, 0], mv[:, :, 0], ALU.mult))
        link(nc.vector.tensor_tensor(mom[:, 1, :], mom[:, 1, :], mv[:, :, 1], ALU.add))
        done_mom = n[0]
        dve.wait_ge(averaged, 1)
        link(nc.vector.tensor_copy(grp[:, :, :], grp_ps[:, :, :]))
        link(nc.vector.tensor_tensor(aff[:, 0, :], grp[:, 0, :], grp[:, 0, :], ALU.mult))
        link(nc.vector.tensor_tensor(aff[:, 0, :], grp[:, 1, :], aff[:, 0, :], ALU.subtract))
        done_var = n[0]
        dve.wait_ge(rooted, 1)
        link(nc.vector.reciprocal(aff[:, 0, :], aff[:, 0, :]))
        link(nc.vector.tensor_tensor(aff[:, 1, :], grp[:, 0, :], aff[:, 0, :], ALU.mult))
        link(nc.vector.tensor_scalar(aff[:, 1, :], aff[:, 1, :], -1.0, None, ALU.mult))
        return done_mom, done_var

    dones = (SEQ + 3, SEQ + 6, SEQ + 9)

    def pe_part(pe):
        pe.wait_ge(step, dones[0])
        nc.tensor.matmul(grp_ps[:, :, :].rearrange("p a b -> p (a b)"), group_avg[:, :],
                         mom[:, :, :].rearrange("p a b -> p (a b)"), start=True, stop=True).then_inc(averaged, 1)

    def act_part(act):
        act.wait_ge(step, dones[1])
        nc.scalar.activation(aff[:, 0, :], aff[:, 0, :], ACT.Sqrt, bias=eps_col[:, 0:1]).then_inc(rooted, 1)

    return aff, dve_part, pe_part, act_part


def phase_input_norm(nc, sem, x, xn, halo, vectors, ones_mat, group_mat):
    halo_next = halo[:, 1:, :].rearrange("p (r t) c -> p r t c", t=NT)
    x_in = x.rearrange("b (k p) h w -> p (b k) (h w)", p=P)
    with ExitStack() as ctx:
        sb = lambda n, s, d: ctx.enter_context(nc.sbuf_tensor(n, s, d))
        pb = lambda n, s, d: ctx.enter_context(nc.psum_tensor(n, s, d))
        xs = sb("a_xs", [P, 2, HW], F32)
        stats = sb("a_stats", [P, SEQ, NT, 6], F32)
        ones = sb("a_ones", [P, P], F32)
        gavg = sb("a_gavg", [P, P], F32)
        gb = sb("a_gb", [P, 2, K], F32)
        aff_b = sb("a_aff_b", [P, 2, K], F32)
        eps = sb("a_eps", [P, 1], F32)
        xc = sb("a_xc", [P, 2, K, T], F32)
        xo = sb("a_xo", [P, 2, K, T], F32)
        zero = sb("a_zero", [P, SEQ, 3], F32)
        consts = sem("a_consts")
        eps_set = sem("a_eps_set")
        tile_loaded = [sem("a_tile_loaded0"), sem("a_tile_loaded1")]
        tile_free = sem("a_tile_free")
        chunk_loaded = [sem("a_chunk_loaded0"), sem("a_chunk_loaded1")]
        out_ready = sem("a_out_ready")
        out_stored = sem("a_out_stored")
        out_free = sem("a_out_free")
        affine_picked = sem("a_affine_picked")
        halo_stored = sem("a_halo_stored")
        ln = LayerNorm(nc, "a_ln", sb, pb, sem, xc, ones)
        block = ctx.enter_context(nc.Block())
        aff, gn_dve, gn_pe, gn_act = finish_group_norm(
            nc, sb, pb, sem, block, "a_gn", stats, gavg, (tile_free, 2 + SEQ), eps)
        gn_done = sem("a_gn_done")

        @block.sync
        def _(sp):
            sp.dma_start(ones[:, :], ones_mat).then_inc(consts, 16)
            sp.dma_start(gavg[:, :], group_mat).then_inc(consts, 16)
            sp.dma_start(gb[:, :, :], vectors[:, NORM_G:NORM_B + 1, :]).then_inc(consts, 16)
            sp.sem_inc(tile_free, 2)
            with sp.Fori(0, SEQ // 2) as q:
                for u in range(2):
                    sp.wait_ge(tile_free, 2 * q + u + 1)
                    sp.dma_start(xs[:, u, :], x_in[:, bass.ds(2 * q + u, 1), :].rearrange("p o t -> p (o t)")).then_inc(tile_loaded[u], 16)
            sp.sem_inc(out_ready, 2)
            with sp.Fori(0, B) as b:
                with sp.Fori(0, NT // 2) as t2:
                    for u in range(2):
                        sp.wait_ge(out_ready, b * NT + t2 * 2 + u + 1)
                        sp.dma_start(xc[:, u], x_in[:, bass.ds(b * K, K), bass.ds((t2 * 2 + u) * T, T)]).then_inc(chunk_loaded[u], 16)

        @block.gpsimd
        def _(pool):
            nc.gpsimd.memset(eps[:, :], GN_EPS).then_inc(eps_set, 1)
            nc.gpsimd.memset(zero[:, :, :], 0.0).then_inc(eps_set, 1)
            pool.sem_inc(out_free, 2)
            with pool.Fori(0, B) as b:
                with pool.Fori(0, NT // 2) as t2:
                    for u in range(2):
                        n = b * NT + t2 * 2 + u
                        pool.wait_ge(out_ready, n + 3)
                        pool.dma_start(xn[:, bass.ds(b * K, K), bass.ds((t2 * 2 + u) * T, T)], xo[:, u]).then_inc(out_stored, 16)
                        pool.dma_start(halo_next[:, bass.ds(b * K, K), bass.ds(t2 * 2 + u, 1), :].rearrange("p k o c -> p k (o c)"),
                                       xo[:, u, :, T - 3:T]).then_inc(out_stored, 16)
                        pool.wait_ge(out_stored, 32 * n + 32)
                        pool.sem_inc(out_free, 1)
            pool.wait_ge(eps_set, 2)
            pool.dma_start(halo[:, 0:SEQ * NT, :].rearrange("p (r t) c -> p r t c", t=NT)[:, :, 0, :], zero[:, :, :]).then_inc(halo_stored, 16)
            pool.wait_ge(halo_stored, 16)

        @block.vector
        def _(dve):
            with dve.Fori(0, SEQ // 2) as q:
                for u in range(2):
                    dve.wait_ge(tile_loaded[u], 16 * q + 16)
                    for t in range(NT):
                        bn = nc.vector.bn_stats(stats[:, bass.ds(2 * q + u, 1), t, :].rearrange("p o s -> p (o s)"), xs[:, u, t * T:(t + 1) * T])
                    bn.then_inc(tile_free, 1)
            gn_dve(dve)
            dve.sem_inc(gn_done, 1)
            with dve.Fori(0, B * NT // 2) as q:
                for u in range(2):
                    ln.dve_centre(dve, u, 2 * q + u)
                for u in range(2):
                    ln.dve_scale(dve, u, 2 * q + u)

        @block.tensor
        def _(pe):
            pe.wait_ge(consts, 48)
            gn_pe(pe)
            with pe.Fori(0, B * NT // 2) as q:
                for u in range(2):
                    ln.pe_mean(pe, u, 2 * q + u)
                for u in range(2):
                    ln.pe_var(pe, u, 2 * q + u)

        @block.scalar
        def _(act):
            act.wait_ge(eps_set, 2)
            gn_act(act)
            act.wait_ge(gn_done, 1)
            act.wait_ge(consts, 48)
            with act.Fori(0, B) as b:
                nc.scalar.activation(aff_b[:, :, :], aff[:, :, bass.ds(b * K, K)], ACT.Identity).then_inc(affine_picked, 1)
                act.wait_ge(affine_picked, b + 1)
                with act.Fori(0, NT // 2) as t2:
                    q = b * (NT // 2) + t2
                    for u in range(2):
                        act.wait_ge(chunk_loaded[u], 16 * q + 16)
                        for k in range(K):
                            gn = nc.scalar.activation(xc[:, u, k, :], xc[:, u, k, :], ACT.Identity,
                                                      scale=aff_b[:, 0, k:k + 1], bias=aff_b[:, 1, k:k + 1])
                        gn.then_inc(ln.input_ready, 1)
                    for u in range(2):
                        ln.act_square(act, u, 2 * q + u)
                    for u in range(2):
                        ln.act_std(act, u, 2 * q + u, eps[:, 0:1])
                    for u in range(2):
                        act.wait_ge(ln.scaled, 2 * q + u + 1)
                        act.wait_ge(out_free, 2 * q + u + 1)
                        for k in range(K):
                            o = nc.scalar.activation(xo[:, u, k, :], xc[:, u, k, :], ACT.Identity, scale=gb[:, 0, k:k + 1], bias=gb[:, 1, k:k + 1])
                        o.then_inc(out_ready, 1)


NS = 16
RANK = 8
TAPS = 4
E2 = 2
UNITS = SEQ * NT
J = NS * E2
NBUF = 8
BBUF = 4
S_PRE = (0, 0, 1, 1, 1, 1, 2, 2, 3, 3, 8, 8, 9, 9, 11, 12)
S_OUT = (7, 8)
S_ACT = (6, 11, 18, 18, 20, 21, 21, 22, 22)
S_POOL = (20, 24, 26, 30)
S_GATE = 4
S_DVE_OUT, S_DVE_DT = 10, 27
B_AHEAD = 6
B_COPY_AHEAD = 2


def at_steps(steps, what):
    return {s: [w for t, w in zip(steps, what) if t == s] for s in steps}


def wait(eng, sem, value):
    if not (isinstance(value, int) and value <= 0):
        eng.wait_ge(sem, value)


def phase_mamba(nc, sem, xn, halo, ym, w_in, w_conv, w_x, w_dtr, w_dt, w_out, a_log, mvec, keep_tab, sel_tab, ident_mat):
    with ExitStack() as ctx:
        sb = lambda n, s, d: ctx.enter_context(nc.sbuf_tensor(n, s, d))
        pb = lambda n, s, d: ctx.enter_context(nc.psum_tensor(n, s, d))
        win = sb("m_win", [P, 2 * E2 * P], F32)
        wcv = sb("m_wcv", [P, TAPS, E2 * P], F32)
        wx = sb("m_wx", [P, E2, 96], F32)
        wdtr = sb("m_wdtr", [P, E2, RANK], F32)
        wdt = sb("m_wdt", [RANK, E2 * P], F32)
        wout = sb("m_wout", [P, E2, P], F32)
        a = sb("m_a", [P, E2, NS], F32)
        mv = sb("m_mv", [P, 7], F32)
        keep = sb("m_keep", [P, UNITS], F32)
        sel = sb("m_sel", [96, 2 * NS, P], BF16)
        ident = sb("m_ident", [P, P], F32)
        x = sb("m_x", [P, 2, 3 + T], F32)
        xc = sb("m_xc", [P, 2, E2, T], F32)
        zs = sb("m_zs", [P, 2, E2, T], F32)
        dt = sb("m_dt", [P, 2, E2, T], F32)
        dtx = sb("m_dtx", [P, 2, E2, T], F32)
        bct = sb("m_bct", [96, 2, T], BF16)
        bcf = sb("m_bcf", [96, T], F32)
        bcr = sb("m_bcr", [64, T], F32)
        dtr = sb("m_dtr", [RANK, T], F32)
        v = sb("m_v", [P, E2, T], F32)
        ea = sb("m_ea", [P, E2, T], F32)
        eb = sb("m_eb", [P, E2, T], F32)
        ec = sb("m_ec", [P, E2, T], F32)
        h = sb("m_h", [P, J, T], F32)
        carry = sb("m_carry", [P, J], F32)
        da = sb("m_da", [P, NBUF, T], F32)
        dbx = sb("m_dbx", [P, NBUF, T], F32)
        hc = sb("m_hc", [P, NBUF, T], F32)
        b_all = sb("m_b_all", [P, BBUF, T], F32)
        yd = sb("m_yd", [P, E2, T], F32)
        yo = sb("m_yo", [P, T], F32)
        xo = sb("m_xo", [P, T], F32)
        y_ps = pb("m_y_ps", [P, E2, T], F32)
        b_ps = pb("m_b_ps", [P, 2, T], F32)
        c_ps = pb("m_c_ps", [P, 2, T], F32)
        pre = pb("m_pre", [P, 2, T], F32)

        consts = sem("m_consts")
        a_exped = sem("m_a_exped")
        a_ready = sem("m_a_ready")
        sel_ready = sem("m_sel_ready")
        carry_zeroed = sem("m_carry_zeroed")
        taps_folded = sem("m_taps_folded")
        x_loaded = [sem("m_x_loaded0"), sem("m_x_loaded1")]
        skip_loaded = sem("m_skip_loaded")
        pre_filled = sem("m_pre_filled")
        out_filled = sem("m_out_filled")
        pre_used = sem("m_pre_used")
        zs_ready = sem("m_zs_ready")
        act_chain = sem("m_act_chain")
        bc_rest = sem("m_bc_rest")
        bct_ready = sem("m_bct_ready")
        log_parts = sem("m_log_parts")
        softplus_tail = sem("m_softplus_tail")
        pool_chain = sem("m_pool_chain")
        dt_ready = sem("m_dt_ready")
        dtx_ready = sem("m_dtx_ready")
        carried = sem("m_carried")
        b_filled = sem("m_b_filled")
        c_filled = sem("m_c_filled")
        b_copied = sem("m_b_copied")
        decays = sem("m_decays")
        inputs = sem("m_inputs")
        scanned = sem("m_scanned")
        products = sem("m_products")
        summed = sem("m_summed")
        y_read = sem("m_y_read")
        yz_ready = sem("m_yz_ready")
        out_ready = sem("m_out_ready")
        out_stored = sem("m_out_stored")
        block = ctx.enter_context(nc.Block())

        def units(eng, run):
            run(0, 0, 0, False, True)
            with eng.Fori(0, UNITS // 2 - 1) as i:
                run(2 * i + 1, i, 1, True, True)
                run(2 * i + 2, i + 1, 0, True, True)
            run(UNITS - 1, UNITS // 2 - 1, 1, True, False)

        @block.sync
        def _(sp):
            sel_f = h[0:96, 0:8, :].rearrange("p a b -> p (a b)")
            for dst, src in ((win[:, :], w_in), (wcv[:, :, :].rearrange("p a b -> p (a b)"), w_conv.partition_broadcast(P)),
                             (wx[:, :, :], w_x), (wdtr[:, :, :], w_dtr), (wdt[:, :], w_dt), (wout[:, :, :], w_out), (a[:, :, :], a_log),
                             (mv[:, :], mvec), (keep[:, :], keep_tab), (sel_f, sel_tab), (ident[:, :], ident_mat)):
                sp.dma_start(dst, src).then_inc(consts, 16)

            def load(n, u):
                sp.dma_start(x[:, u, 3:3 + T], xn[:, bass.ds(n, 1), :].rearrange("p o t -> p (o t)")).then_inc(x_loaded[u], 16)
                sp.dma_start(x[:, u, 0:3], halo[:, bass.ds(n, 1), :].rearrange("p o t -> p (o t)")).then_inc(x_loaded[u], 16)

            def load_skip(n):
                sp.dma_start(xo[:, :], xn[:, bass.ds(n, 1), :].rearrange("p o t -> p (o t)")).then_inc(skip_loaded, 16)

            def run(n, u, has_prev, has_second):
                if has_second:
                    sp.wait_ge(pre_filled, 8 * n + 4)
                    load(n + 2, u)
                if has_prev:
                    load_skip(n - 1)
                    sp.wait_ge(out_ready, n)
                    sp.dma_start(ym[:, bass.ds(n - 1, 1), :].rearrange("p o t -> p (o t)"), yo[:, :]).then_inc(out_stored, 16)

            load(0, 0)
            load(1, 1)
            run(0, 0, False, True)
            with sp.Fori(0, UNITS // 2 - 2) as i:
                run(2 * i + 1, 1, True, True)
                run(2 * i + 2, 0, True, True)
            run(UNITS - 3, 1, True, True)
            run(UNITS - 2, 0, True, False)
            run(UNITS - 1, 1, True, False)
            load_skip(UNITS - 1)
            sp.wait_ge(out_ready, UNITS)
            sp.dma_start(ym[:, UNITS - 1, :], yo[:, :]).then_inc(out_stored, 16)
            sp.wait_ge(out_stored, 16 * UNITS)

        @block.tensor
        def _(pe):
            def product_term(out, terms, i, filled):
                mm = nc.tensor.matmul(out, terms[i][0], terms[i][1], start=i == 0, stop=i == len(terms) - 1)
                if i == len(terms) - 1:
                    mm.then_inc(filled, 1)

            def pre_step(g, i, n, m, u):
                if i == 0:
                    wait(pe, pre_used, 8 * n + PRE_AFTER[g])
                if (g, i) == (0, 0):
                    pe.wait_ge(x_loaded[u], 32 * m + 32)
                if (g, i) == (5, 0):
                    wait(pe, out_ready, n - 1)
                if g < 2:
                    product_term(pre[:, g, :], [(win[:, (g + 2) * P:(g + 3) * P], x[:, u, 3:3 + T])], i, pre_filled)
                elif g < 4:
                    product_term(pre[:, g - 2, :], [(wcv[:, tap, (g - 2) * P:(g - 1) * P], x[:, u, tap:tap + T]) for tap in range(TAPS)], i, pre_filled)
                elif g == 4:
                    product_term(pre[0:RANK, 1, :], [(wdtr[:, e, :], xc[:, u, e, :]) for e in range(E2)], i, pre_filled)
                elif g == 5:
                    product_term(pre[0:96, 0, :], [(wx[:, e, :], xc[:, u, e, :]) for e in range(E2)], i, pre_filled)
                else:
                    product_term(pre[:, 7 - g, :], [(wdt[:, (g - 6) * P:(g - 5) * P], dtr[:, :])], i, pre_filled)

            def out_step(n, i, pre_before):
                if i == 0:
                    pe.wait_ge(yz_ready, n + 1)
                    wait(pe, pre_used, pre_before)
                product_term(pre[:, 0, :], [(wout[:, e, :], yd[:, e, :]) for e in range(E2)], i, out_filled)

            def spread_b(n, u, s):
                if s == 0:
                    pe.wait_ge(bct_ready, n + 1)
                wait(pe, b_copied, NS * n + s - 1)
                nc.tensor.matmul(b_ps[:, s % 2, :], sel[:, s, :], bct[:, u, :], start=True, stop=True).then_inc(b_filled, 1)

            def spread_c(n, u, s):
                wait(pe, products, J * n + E2 * (s - 1))
                nc.tensor.matmul(c_ps[:, s % 2, :], sel[:, NS + s, :], bct[:, u, :], start=True, stop=True).then_inc(c_filled, 1)

            def run(n, m, u, has_prev, has_next):
                nm = m + u
                for s in range(NS):
                    if s + B_AHEAD < NS:
                        spread_b(n, u, s + B_AHEAD)
                    elif has_next:
                        spread_b(n + 1, 1 - u, s + B_AHEAD - NS)
                    if s + 1 < NS:
                        spread_c(n, u, s + 1)
                    elif has_next:
                        spread_c(n + 1, 1 - u, 0)
                    for e in range(E2):
                        j = E2 * s + e
                        pe.wait_ge(products, J * n + j + 1)
                        if j == 0:
                            wait(pe, y_read, n)
                        nc.tensor.matmul(y_ps[:, e, :], ident[:, :], hc[:, j % NBUF, :], start=s == 0, stop=s == NS - 1).then_inc(summed, 1)
                        if has_next:
                            for g, i in PRE_AT.get(j, ()):
                                pre_step(g, i, n + 1, nm, 1 - u)
                        if has_prev and j in S_OUT:
                            out_step(n - 1, S_OUT.index(j), 8 * n + (11 if has_next else 8))

            PRE_AT = at_steps(S_PRE, [(g, i) for g, terms in enumerate((1, 1, TAPS, TAPS, E2, E2, 1, 1)) for i in range(terms)])
            PRE_AFTER = (0, 0, 1, 2, 4, 4, 5, 6)
            pe.wait_ge(consts, 16 * 11)
            pe.wait_ge(sel_ready, 1)
            pe.wait_ge(taps_folded, TAPS)
            for j in sorted(PRE_AT):
                for g, i in PRE_AT[j]:
                    pre_step(g, i, 0, 0, 0)
            for s in range(B_AHEAD):
                spread_b(0, 0, s)
            spread_c(0, 0, 0)
            units(pe, run)
            for i in range(E2):
                out_step(UNITS - 1, i, 8 * UNITS)

        @block.scalar
        def _(act):
            act.wait_ge(consts, 16 * 11)
            nc.scalar.activation(a[:, :, :], a[:, :, :], ACT.Exp).then_inc(a_exped, 1)
            nc.scalar.activation(sel[:, :, :].rearrange("p a b -> p (a b)"), h[0:96, 0:8, :].rearrange("p a b -> p (a b)"), ACT.Copy).then_inc(sel_ready, 1)

            def gates(n, u):
                wait(act, yz_ready, n - 1)
                for g in range(2):
                    act.wait_ge(pre_filled, 8 * n + g + 1)
                    nc.scalar.activation(zs[:, u, g, :], pre[:, g, :], ACT.Copy).then_inc(pre_used, 1)

            def silus(n, u):
                wait(act, y_read, n - 1)
                for g in range(2):
                    act.wait_ge(pre_filled, 8 * n + g + 3)
                    nc.scalar.activation(xc[:, u, g, :], pre[:, g, :], ACT.Silu, bias=mv[:, g:g + 1]).then_inc(pre_used, 1)
                act.wait_ge(pre_used, 8 * n + 2)
                nc.scalar.activation(zs[:, u], zs[:, u], ACT.Silu).then_inc(zs_ready, 1)

            def copy_dtr(n, u):
                act.wait_ge(pre_filled, 8 * n + 5)
                nc.scalar.activation(dtr[:, :], pre[0:RANK, 1, :], ACT.Copy).then_inc(pre_used, 1)

            def copy_bc(n, u):
                act.wait_ge(pre_filled, 8 * n + 6)
                nc.scalar.activation(bcf[:, :], pre[0:96, 0, :], ACT.Copy).then_inc(pre_used, 1)
                act.wait_ge(pre_used, 8 * n + 6)
                wait(act, b_copied, NS * n - NS)
                wait(act, c_filled, NS * n - NS)
                nc.scalar.activation(bct[:, u, :], bcf[:, :], ACT.Copy).then_inc(act_chain, 1)

            def copy_dt(n, u):
                for e in range(E2):
                    act.wait_ge(pre_filled, 8 * n + 7 + e)
                    nc.scalar.activation(v[:, e, :], pre[:, 1 - e, :], ACT.Identity, bias=mv[:, 2 + e:3 + e]).then_inc(pre_used, 1)

            def mid_part(n, u):
                act.wait_ge(bc_rest, n + 1)
                nc.scalar.activation(bct[0:64, u, :], bcr[:, :], ACT.Copy).then_inc(act_chain, 1)

            def softplus_exp(n, u):
                act.wait_ge(pre_used, 8 * n + 8)
                nc.scalar.activation(ea[:, :, :], v[:, :, :], ACT.Abs).then_inc(act_chain, 1)
                act.wait_ge(act_chain, 6 * n + 3)
                nc.scalar.activation(ea[:, :, :], ea[:, :, :], ACT.Exp, scale=-1.0).then_inc(act_chain, 1)

            def softplus_log(n, u):
                act.wait_ge(act_chain, 6 * n + 4)
                nc.scalar.activation(eb[:, :, :], ea[:, :, :], ACT.Identity, bias=1.0).then_inc(act_chain, 1)
                act.wait_ge(act_chain, 6 * n + 5)
                nc.scalar.activation(ec[:, :, :], eb[:, :, :], ACT.Ln).then_inc(act_chain, 1)

            def softplus_low(n, u):
                nc.scalar.activation(eb[:, :, :], eb[:, :, :], ACT.Identity, bias=-1.0).then_inc(log_parts, 1)

            def copy_b(n, s):
                act.wait_ge(b_filled, NS * n + s + 1)
                wait(act, inputs, J * n + E2 * (s - BBUF + 1))
                nc.scalar.activation(b_all[:, s % BBUF, :], b_ps[:, s % 2, :], ACT.Copy).then_inc(b_copied, 1)

            def run(n, m, u, has_prev, has_next):
                act.wait_ge(dt_ready, n + 1)
                for s in range(NS):
                    if s + B_COPY_AHEAD < NS:
                        copy_b(n, s + B_COPY_AHEAD)
                    elif has_next:
                        copy_b(n + 1, s + B_COPY_AHEAD - NS)
                    for e in range(E2):
                        j = E2 * s + e
                        wait(act, scanned, J * n + j - NBUF + 1)
                        nc.scalar.activation(da[:, j % NBUF, :], dt[:, u, e, :], ACT.Exp, scale=a[:, e, s:s + 1]).then_inc(decays, 1)
                        if has_next:
                            for step in ACT_AT.get(j, ()):
                                step(n + 1, 1 - u)

            ACT_AT = at_steps(S_ACT, (gates, silus, copy_dtr, copy_bc, mid_part, copy_dt, softplus_exp, softplus_log, softplus_low))
            act.wait_ge(a_ready, 1)
            for j in sorted(ACT_AT):
                for step in ACT_AT[j]:
                    step(0, 0)
            for s in range(B_COPY_AHEAD):
                copy_b(0, s)
            units(act, run)

        @block.gpsimd
        def _(pool):
            def split_mid(n, u):
                pool.wait_ge(act_chain, 6 * n + 1)
                nc.gpsimd.tensor_tensor(bcr[:, :], bcf[0:64, :], bct[0:64, u, :], ALU.subtract).then_inc(bc_rest, 1)

            def split_low(n, u):
                pool.wait_ge(act_chain, 6 * n + 2)
                nc.gpsimd.tensor_tensor(bct[0:32, u, :], bcr[0:32, :], bct[0:32, u, :], ALU.subtract).then_inc(bct_ready, 1)

            def tail(n, u):
                pool.wait_ge(log_parts, n + 1)
                nc.gpsimd.tensor_tensor(ea[:, :, :], ea[:, :, :], eb[:, :, :], ALU.subtract).then_inc(pool_chain, 1)
                pool.wait_ge(pool_chain, n + 1)
                nc.gpsimd.tensor_tensor(ec[:, :, :], ec[:, :, :], ea[:, :, :], ALU.add).then_inc(softplus_tail, 1)

            def dt_times_x(n, u):
                pool.wait_ge(dt_ready, n + 1)
                nc.gpsimd.tensor_tensor(dtx[:, u], dt[:, u], xc[:, u], ALU.mult).then_inc(dtx_ready, 1)

            def gate(n, u):
                pool.wait_ge(y_read, n + 1)
                pool.wait_ge(zs_ready, n + 1)
                nc.gpsimd.tensor_tensor(yd[:, :, :], yd[:, :, :], zs[:, u], ALU.mult).then_inc(yz_ready, 1)

            def run(n, m, u, has_prev, has_next):
                for s in range(NS):
                    pool.wait_ge(b_copied, NS * n + s + 1)
                    for e in range(E2):
                        j = E2 * s + e
                        wait(pool, scanned, J * n + j - NBUF + 1)
                        if j == 0:
                            pool.wait_ge(dtx_ready, n + 1)
                        nc.gpsimd.tensor_tensor(dbx[:, j % NBUF, :], dtx[:, u, e, :], b_all[:, s % BBUF, :], ALU.mult).then_inc(inputs, 1)
                        if has_prev and j == S_GATE:
                            gate(n - 1, 1 - u)
                        if has_next:
                            for step in POOL_AT.get(j, ()):
                                step(n + 1, 1 - u)

            POOL_AT = at_steps(S_POOL, (split_mid, split_low, tail, dt_times_x))
            nc.gpsimd.memset(carry[:, :], 0.0).then_inc(carry_zeroed, 1)
            for j in sorted(POOL_AT):
                for step in POOL_AT[j]:
                    step(0, 0)
            units(pool, run)
            gate(UNITS - 1, 1)

        @block.vector
        def _(dve):
            dve.wait_ge(consts, 16 * 11)
            for tap in range(TAPS):
                nc.vector.tensor_tensor(wcv[:, tap, :], wcv[:, tap, :], win[:, 0:E2 * P], ALU.mult).then_inc(taps_folded, 1)
            dve.wait_ge(a_exped, 1)
            nc.vector.tensor_scalar(a[:, :, :], a[:, :, :], -1.0, None, ALU.mult).then_inc(a_ready, 1)
            dve.wait_ge(carry_zeroed, 1)

            def softplus_head(n, u):
                dve.wait_ge(softplus_tail, n + 1)
                nc.vector.scalar_tensor_tensor(dt[:, u].rearrange("p a b -> p (a b)"), v[:, :, :].rearrange("p a b -> p (a b)"), 0.0,
                                               ec[:, :, :].rearrange("p a b -> p (a b)"), ALU.max, ALU.add).then_inc(dt_ready, 1)

            def read_y(n, u):
                dve.wait_ge(summed, J * n + J)
                wait(dve, out_filled, n)
                for e in range(E2):
                    y = nc.vector.scalar_tensor_tensor(yd[:, e, :], xc[:, u, e, :], mv[:, 4 + e:5 + e], y_ps[:, e, :], ALU.mult, ALU.add)
                y.then_inc(y_read, 1)

            def output(n, u):
                dve.wait_ge(out_filled, n + 1)
                dve.wait_ge(skip_loaded, 16 * n + 16)
                wait(dve, out_stored, 16 * n)
                nc.vector.scalar_tensor_tensor(yo[:, :], xo[:, :], mv[:, 6:7], pre[:, 0, :], ALU.mult, ALU.add).then_inc(out_ready, 1)

            def product(n, j):
                s, e = divmod(j, E2)
                dve.wait_ge(scanned, J * n + j + 1)
                dve.wait_ge(c_filled, NS * n + s + 1)
                wait(dve, summed, J * n + j - NBUF + 1)
                nc.vector.tensor_tensor(hc[:, j % NBUF, :], h[:, j, :], c_ps[:, s % 2, :], ALU.mult).then_inc(products, 1)

            def run(n, m, u, has_prev, has_next):
                if has_prev:
                    dve.wait_ge(scanned, J * n)
                    nc.vector.tensor_tensor(carry[:, :], h[:, :, T - 1], keep[:, bass.ds(n, 1)].broadcast_to([P, J]), ALU.mult).then_inc(carried, 1)
                    dve.wait_ge(carried, n)
                for j in range(J):
                    dve.wait_ge(decays, J * n + j + 1)
                    dve.wait_ge(inputs, J * n + j + 1)
                    nc.vector.tensor_tensor_scan(h[:, j, :], da[:, j % NBUF, :], dbx[:, j % NBUF, :], carry[:, j:j + 1],
                                                 ALU.mult, ALU.add).then_inc(scanned, 1)
                    if j:
                        product(n, j - 1)
                    if has_prev:
                        if j == 1:
                            read_y(n - 1, 1 - u)
                        elif j == S_DVE_OUT:
                            output(n - 1, 1 - u)
                    if has_next and j == S_DVE_DT:
                        softplus_head(n + 1, 1 - u)
                product(n, J - 1)

            softplus_head(0, 0)
            units(dve, run)
            read_y(UNITS - 1, 1)
            output(UNITS - 1, 1)


def phase_project(nc, sem, ym, x, x2, stats_out, vectors, w_proj, ones_mat):
    x_in = x.rearrange("b (k p) h w -> p (b k) (h w)", p=P)
    y_in = ym.rearrange("p (r t) c -> p r (t c)", t=NT)
    with ExitStack() as ctx:
        sb = lambda n, s, d: ctx.enter_context(nc.sbuf_tensor(n, s, d))
        pb = lambda n, s, d: ctx.enter_context(nc.psum_tensor(n, s, d))
        ones = sb("p_ones", [P, P], F32)
        vec = sb("p_vec", [P, 3, K], F32)
        w = sb("p_w", [P, K, C], F32)
        eps = sb("p_eps", [P, 1], F32)
        y = sb("p_y", [P, 2, K, T], F32)
        yn = sb("p_yn", [P, 2, K, T], F32)
        res = sb("p_res", [P, 2, K, T], F32)
        stats = sb("p_stats", [P, SEQ, NT, 6], F32)
        out_ps = pb("p_out_ps", [P, 4, T], F32)
        consts = sem("p_consts")
        eps_set = sem("p_eps_set")
        y_loaded = [sem("p_y_loaded0"), sem("p_y_loaded1")]
        x_loaded = [sem("p_x_loaded0"), sem("p_x_loaded1")]
        res_free = sem("p_res_free")
        yn_ready = sem("p_yn_ready")
        bank_filled = sem("p_bank_filled")
        bank_read = sem("p_bank_read")
        stats_done = sem("p_stats_done")
        stored = sem("p_stored")
        ln = LayerNorm(nc, "p_ln", sb, pb, sem, y, ones)
        block = ctx.enter_context(nc.Block())
        CHUNKS = B * NT

        @block.sync
        def _(sp):
            sp.dma_start(ones[:, :], ones_mat).then_inc(consts, 16)
            sp.dma_start(vec[:, :, :], vectors[:, NORM_G:PROJ_B + 1, :]).then_inc(consts, 16)
            sp.dma_start(w[:, :, :], w_proj).then_inc(consts, 16)
            sp.sem_inc(yn_ready, 2)
            with sp.Fori(0, B) as b:
                with sp.Fori(0, NT // 2) as t2:
                    q = b * (NT // 2) + t2
                    for u in range(2):
                        sp.wait_ge(yn_ready, 2 * q + u + 1)
                        sp.dma_start(y[:, u], y_in[:, bass.ds(b * K, K), bass.ds((t2 * 2 + u) * T, T)]).then_inc(y_loaded[u], 16)
                        sp.wait_ge(res_free, 2 * q + u + 1)
                        sp.dma_start(res[:, u], x_in[:, bass.ds(b * K, K), bass.ds((t2 * 2 + u) * T, T)]).then_inc(x_loaded[u], 16)

        @block.gpsimd
        def _(pool):
            nc.gpsimd.memset(eps[:, :], LN_EPS).then_inc(eps_set, 1)
            pool.sem_inc(res_free, 2)
            with pool.Fori(0, B) as b:
                with pool.Fori(0, NT // 2) as t2:
                    for u in range(2):
                        n = b * NT + t2 * 2 + u
                        pool.wait_ge(stats_done, n + 1)
                        pool.dma_start(x2[:, bass.ds(b * K, K), bass.ds((t2 * 2 + u) * T, T)], res[:, u]).then_inc(stored, 16)
                        pool.wait_ge(stored, 16 * n + 16)
                        pool.sem_inc(res_free, 1)
            pool.dma_start(stats_out, stats[:, :, :, :]).then_inc(stored, 16)
            pool.wait_ge(stored, 16 * CHUNKS + 16)

        @block.tensor
        def _(pe):
            pe.wait_ge(consts, 48)
            with pe.Fori(0, CHUNKS // 2) as q:
                for u in range(2):
                    ln.pe_mean(pe, u, 2 * q + u)
                for u in range(2):
                    ln.pe_var(pe, u, 2 * q + u)
                for u in range(2):
                    c = 2 * q + u
                    pe.wait_ge(yn_ready, c + 3)
                    for o in range(K):
                        pe.wait_ge(bank_read, 4 * c + o + 1)
                        for k in range(K):
                            mm = nc.tensor.matmul(out_ps[:, o, :], w[:, k, o * P:(o + 1) * P], yn[:, u, k, :], start=k == 0, stop=k == K - 1)
                        mm.then_inc(bank_filled, 1)

        @block.scalar
        def _(act):
            act.sem_inc(bank_read, 4)
            act.wait_ge(eps_set, 1)
            act.wait_ge(consts, 48)
            with act.Fori(0, CHUNKS // 2) as q:
                for u in range(2):
                    act.wait_ge(y_loaded[u], 16 * q + 16)
                    act.sem_inc(ln.input_ready, 1)
                for u in range(2):
                    ln.act_square(act, u, 2 * q + u)
                for u in range(2):
                    ln.act_std(act, u, 2 * q + u, eps[:, 0:1])
                for u in range(2):
                    c = 2 * q + u
                    act.wait_ge(ln.scaled, c + 1)
                    for k in range(K):
                        o = nc.scalar.activation(yn[:, u, k, :], y[:, u, k, :], ACT.Identity, scale=vec[:, 0, k:k + 1], bias=vec[:, 1, k:k + 1])
                    o.then_inc(yn_ready, 1)

        @block.vector
        def _(dve):
            with dve.Fori(0, B) as b:
                with dve.Fori(0, NT // 2) as t2:
                    q = b * (NT // 2) + t2
                    for u in range(2):
                        ln.dve_centre(dve, u, 2 * q + u)
                    for u in range(2):
                        ln.dve_scale(dve, u, 2 * q + u)
                    for u in range(2):
                        c = 2 * q + u
                        dve.wait_ge(x_loaded[u], 16 * q + 16)
                        for k in range(K):
                            dve.wait_ge(bank_filled, 4 * c + k + 1)
                            nc.vector.scalar_tensor_tensor(res[:, u, k, :], out_ps[:, k, :], vec[:, 2, k:k + 1], res[:, u, k, :],
                                                           ALU.add, ALU.add).then_inc(bank_read, 1)
                        dve.wait_ge(bank_read, 4 * c + 8)
                        for k in range(K):
                            bn = nc.vector.bn_stats(stats[:, bass.ds(b * K + k, 1), bass.ds(t2 * 2 + u, 1), :].rearrange("p o n s -> p (o n s)"),
                                                    res[:, u, k, :])
                        bn.then_inc(stats_done, 1)


G = 16
PTS = 9
NOFF = G * PTS * 2
NMASK = G * PTS
ROWS = T // IMG
TT = T // P
PADI = IMG + 2
NCOL = NOFF + NMASK
REACH = 3
PADW = IMG + 2 * REACH


def phase_offsets(nc, sem, x2, stats_in, xproj, offsets, masks, peak, vectors, w_in, dw_w, w_om, b_om, ones_mat, group_mat):
    with ExitStack() as ctx:
        sb = lambda n, s, d: ctx.enter_context(nc.sbuf_tensor(n, s, d))
        pb = lambda n, s, d: ctx.enter_context(nc.psum_tensor(n, s, d))
        ones = sb("o_ones", [P, P], F32)
        gavg = sb("o_gavg", [P, P], F32)
        vec = sb("o_vec", [P, 4, K], F32)
        w = sb("o_w", [P, K, C], F32)
        wom = sb("o_wom", [P, K, NCOL], F32)
        bom = sb("o_bom", [P, NCOL], F32)
        dw = sb("o_dw", [P, K, 9], F32)
        eps = sb("o_eps", [P, 1], F32)
        stats = sb("o_stats", [P, SEQ, NT, 6], F32)
        aff_b = sb("o_aff_b", [P, 2, K], F32)
        raw = sb("o_raw", [P, 2, K, T], F32)
        g = sb("o_g", [P, K, PADI, PADI], F32)
        d = sb("o_d", [P, 2, K, T], F32)
        xp = sb("o_xp", [P, K, ROWS, PADW], F32)
        zero = sb("o_zero", [P, K, REACH * PADW], F32)
        om = sb("o_om", [P, TT, NCOL], F32)
        small = sb("o_small", [P, 2, TT, G], F32)
        peaks = sb("o_peaks", [P, B * NT], F32)
        out_ps = pb("o_out_ps", [P, 4, T], F32)
        consts = sem("o_consts")
        eps_set = sem("o_eps_set")
        border_set = sem("o_border_set")
        xp_border_set = sem("o_xp_border_set")
        zeros_set = sem("o_zeros_set")
        rows_stored = sem("o_rows_stored")
        affine_picked = sem("o_affine_picked")
        raw_loaded = [sem("o_raw_loaded0"), sem("o_raw_loaded1")]
        normed = sem("o_normed")
        convolved = sem("o_convolved")
        geluded = sem("o_geluded")
        bank_filled = sem("o_bank_filled")
        bank_read_act = sem("o_bank_read_act")
        bank_read_dve = sem("o_bank_read_dve")
        xp_ready = sem("o_xp_ready")
        xp_stored = sem("o_xp_stored")
        om_step = sem("o_om_step")
        exp_done = sem("o_exp_done")
        om_ready = sem("o_om_ready")
        om_stored = sem("o_om_stored")
        chunk_done = sem("o_chunk_done")
        ln = LayerNorm(nc, "o_ln", sb, pb, sem, d, ones)
        block = ctx.enter_context(nc.Block())
        aff, gn_dve, gn_pe, gn_act = finish_group_norm(
            nc, sb, pb, sem, block, "o_gn", stats, gavg, (consts, 16 * 8), eps)
        CH = B * NT
        OM = 7

        @block.sync
        def _(sp):
            for dst, src in ((ones[:, :], ones_mat), (gavg[:, :], group_mat), (vec[:, :, :], vectors[:, DW_B:IN_B + 1, :]),
                             (w[:, :, :], w_in), (wom[:, :, :], w_om), (bom[:, :], b_om.partition_broadcast(P)),
                             (dw[:, :, :], dw_w), (stats[:, :, :, :], stats_in)):
                sp.dma_start(dst, src).then_inc(consts, 16)
            sp.sem_inc(normed, 2)
            with sp.Fori(0, B) as b:
                with sp.Fori(0, NT // 2) as t2:
                    for u in range(2):
                        sp.wait_ge(normed, b * NT + t2 * 2 + u + 1)
                        sp.dma_start(raw[:, u], x2[:, bass.ds(b * K, K), bass.ds((t2 * 2 + u) * T, T)]).then_inc(raw_loaded[u], 16)

        @block.gpsimd
        def _(pool):
            nc.gpsimd.memset(eps[:, :], LN_EPS).then_inc(eps_set, 1)
            nc.gpsimd.memset(g[:, :, :, :].rearrange("p k a b -> p (k a b)"), 0.0).then_inc(border_set, 1)
            nc.gpsimd.memset(xp[:, :, :, :].rearrange("p k a b -> p (k a b)"), 0.0).then_inc(xp_border_set, 1)
            nc.gpsimd.memset(zero[:, :, :].rearrange("p k a -> p (k a)"), 0.0).then_inc(zeros_set, 1)
            pool.wait_ge(zeros_set, 1)
            for b in range(B):
                for r in (0, PADW - REACH):
                    pool.dma_start(xproj[:, b * K:(b + 1) * K, r * PADW:(r + REACH) * PADW], zero[:, :, :]).then_inc(rows_stored, 16)
            with pool.Fori(0, B) as b:
                with pool.Fori(0, NT) as t:
                    n = b * NT + t
                    pool.wait_ge(xp_ready, n + 1)
                    pool.dma_start(xproj[:, bass.ds(b * K, K), bass.ds((t * ROWS + REACH) * PADW, ROWS * PADW)],
                                   xp[:, :, :, :].rearrange("p k a b -> p k (a b)")).then_inc(xp_stored, 16)
                    pool.wait_ge(om_ready, n + 1)
                    pool.dma_start(offsets[:, bass.ds(n * TT, TT), :], om[:, :, 0:NOFF]).then_inc(om_stored, 16)
                    pool.dma_start(masks[:, bass.ds(n * TT, TT), :], om[:, :, NOFF:NCOL]).then_inc(om_stored, 16)
                    pool.wait_ge(xp_stored, 16 * n + 16)
                    pool.wait_ge(om_stored, 32 * n + 32)
                    pool.sem_inc(chunk_done, 1)
            pool.dma_start(peak, peaks[:, :]).then_inc(om_stored, 16)
            pool.wait_ge(om_stored, 32 * CH + 16)
            pool.wait_ge(rows_stored, 16 * 2 * B)

        @block.tensor
        def _(pe):
            pe.wait_ge(consts, 16 * 8)
            gn_pe(pe)
            with pe.Fori(0, B) as b:
                with pe.Fori(0, NT // 2) as t2:
                    for u in range(2):
                        c = b * NT + t2 * 2 + u
                        pe.wait_ge(normed, (b + 1) * NT + 2)
                        for o in range(K):
                            wait(pe, bank_read_act, 4 * c + o + 1)
                            if o == 0:
                                wait(pe, bank_read_dve, c + 1)
                            for k in range(K):
                                mm = nc.tensor.matmul(out_ps[:, o, :], w[:, k, o * P:(o + 1) * P],
                                                      g[:, k, bass.ds((t2 * 2 + u) * ROWS + 1, ROWS), 1:1 + IMG], start=k == 0, stop=k == K - 1)
                            mm.then_inc(bank_filled, 1)
                        if u == 0:
                            for v in range(2):
                                ln.pe_mean(pe, v, b * NT + t2 * 2 + v)
                            for v in range(2):
                                ln.pe_var(pe, v, b * NT + t2 * 2 + v)
                        pe.wait_ge(geluded, c + 1)
                        pe.wait_ge(bank_read_act, 4 * c + 8)
                        for t in range(TT):
                            for k in range(K):
                                mm = nc.tensor.matmul(out_ps[:, t, 0:NCOL], d[:, u, k, t * P:(t + 1) * P], wom[:, k, :], start=k == 0, stop=k == K - 1)
                        mm.then_inc(bank_filled, 1)

        @block.scalar
        def _(act):
            act.sem_inc(bank_read_act, 4)
            act.wait_ge(eps_set, 1)
            gn_act(act)
            act.wait_ge(xp_border_set, 1)
            act.wait_ge(consts, 16 * 8)
            with act.Fori(0, B) as b:
                with act.Fori(0, NT // 2) as t2:
                    for u in range(2):
                        c = b * NT + t2 * 2 + u
                        act.wait_ge(chunk_done, c + 1)
                        for k in range(K):
                            act.wait_ge(bank_filled, 5 * c + k + 1)
                            nc.scalar.activation(xp[:, k, :, REACH:REACH + IMG], out_ps[:, k, :].rearrange("p (r c) -> p r c", c=IMG), ACT.Identity, bias=vec[:, 3, k:k + 1]).then_inc(bank_read_act, 1)
                        act.wait_ge(bank_read_act, 4 * c + 8)
                        act.sem_inc(xp_ready, 1)
                        if u == 0:
                            for v in range(2):
                                ln.act_square(act, v, b * NT + t2 * 2 + v)
                            for v in range(2):
                                ln.act_std(act, v, b * NT + t2 * 2 + v, eps[:, 0:1])
                        act.wait_ge(ln.scaled, c + 1)
                        for k in range(K):
                            a = nc.scalar.activation(d[:, u, k, :], d[:, u, k, :], ACT.Gelu, scale=vec[:, 1, k:k + 1], bias=vec[:, 2, k:k + 1])
                        a.then_inc(geluded, 1)
                        act.wait_ge(om_step, OM * c + 3)
                        nc.scalar.activation(om[:, :, NOFF:NCOL], om[:, :, NOFF:NCOL], ACT.Exp).then_inc(exp_done, 1)

        @block.vector
        def _(dve):
            dve.sem_inc(bank_read_dve, 1)
            dve.sem_inc(chunk_done, 1)
            gn_dve(dve)
            dve.wait_ge(border_set, 1)
            lg = om[:, :, NOFF:NCOL].rearrange("p t (g q) -> p t g q", q=PTS)
            per_point = lambda s: s.unsqueeze(3).broadcast_to([P, TT, G, PTS])
            with dve.Fori(0, B) as b:
                dve.wait_ge(bank_filled, 5 * NT * b)
                nc.vector.tensor_scalar(aff_b[:, :, :], aff[:, :, bass.ds(b * K, K)], 1.0, None, ALU.mult).then_inc(affine_picked, 1)
                with dve.Fori(0, NT // 2) as t2:
                    for u in range(2):
                        dve.wait_ge(affine_picked, b + 1)
                        dve.wait_ge(raw_loaded[u], 16 * (b * (NT // 2) + t2) + 16)
                        for k in range(K):
                            a = nc.vector.tensor_scalar(g[:, k, bass.ds((t2 * 2 + u) * ROWS + 1, ROWS), 1:1 + IMG],
                                                        raw[:, u, k, :].rearrange("p (r c) -> p r c", c=IMG),
                                                        aff_b[:, 0, k:k + 1], aff_b[:, 1, k:k + 1], ALU.mult, ALU.add)
                        a.then_inc(normed, 1)
                with dve.Fori(0, NT // 2) as t2:
                    for u in range(2):
                        c = b * NT + t2 * 2 + u
                        dve.wait_ge(normed, (b + 1) * NT + 2)
                        dve.wait_ge(bank_read_dve, c)
                        for k in range(K):
                            for tap in range(9):
                                r, s = divmod(tap, 3)
                                src = g[:, k, bass.ds((t2 * 2 + u) * ROWS + r, ROWS), s:s + IMG]
                                dst = d[:, u, k, :].rearrange("p (r c) -> p r c", c=IMG)
                                if tap == 0:
                                    i = nc.vector.tensor_scalar(dst, src, dw[:, k, 0:1], vec[:, 0, k:k + 1], ALU.mult, ALU.add)
                                else:
                                    i = nc.vector.scalar_tensor_tensor(dst, src, dw[:, k, tap:tap + 1], dst, ALU.mult, ALU.add)
                                i.then_inc(convolved, 1)
                                dve.wait_ge(convolved, 36 * c + 9 * k + tap + 1)
                        dve.sem_inc(ln.input_ready, 1)
                    for u in range(2):
                        ln.dve_centre(dve, u, b * NT + t2 * 2 + u)
                    for u in range(2):
                        ln.dve_scale(dve, u, b * NT + t2 * 2 + u)
                    for u in range(2):
                        c = b * NT + t2 * 2 + u
                        dve.wait_ge(bank_filled, 5 * c + 5)
                        dve.wait_ge(chunk_done, c + 1)
                        nc.vector.tensor_tensor(om[:, :, :], out_ps[:, :, 0:NCOL], bom[:, :].unsqueeze(1).broadcast_to([P, TT, NCOL]),
                                                ALU.add).then_inc(om_step, 1)
                        dve.wait_ge(om_step, OM * c + 1)
                        dve.sem_inc(bank_read_dve, 1)
                        nc.vector.tensor_reduce(small[:, 0], lg, AX.X, ALU.max).then_inc(om_step, 1)
                        dve.wait_ge(om_step, OM * c + 2)
                        nc.vector.tensor_tensor(lg, lg, per_point(small[:, 0]), ALU.subtract).then_inc(om_step, 1)
                        nc.vector.tensor_reduce(peaks[:, bass.ds(c, 1)], om[:, :, 0:NOFF], AX.XY, ALU.max, apply_absolute_value=True).then_inc(om_step, 1)
                        dve.wait_ge(exp_done, c + 1)
                        nc.vector.tensor_reduce(small[:, 1], lg, AX.X, ALU.add).then_inc(om_step, 1)
                        dve.wait_ge(om_step, OM * c + 5)
                        nc.vector.reciprocal(small[:, 1], small[:, 1]).then_inc(om_step, 1)
                        dve.wait_ge(om_step, OM * c + 6)
                        nc.vector.tensor_tensor(lg, lg, per_point(small[:, 1]), ALU.mult).then_inc(om_step, 1)
                        dve.wait_ge(om_step, OM * c + 7)
                        dve.sem_inc(om_ready, 1)


WIN = 2 * REACH + 1
D = WIN * WIN
HATS = 5
PARTS = 3
GK = G // K
ROWD = PARTS * GK
PER_BLOCK = 10
BLOCKS = -(-D // PER_BLOCK)
PROD_BUF = 2
POOL_BUF = 4
PAIRS = (D + 1) // 2


def phase_sample(nc, sem, x2, xproj, offsets, masks, out, vectors, w_out, sel_tab, ident_mat):
    with ExitStack() as ctx:
        sb = lambda n, s, d: ctx.enter_context(nc.sbuf_tensor(n, s, d))
        pb = lambda n, s, d: ctx.enter_context(nc.psum_tensor(n, s, d))
        vec = sb("s_vec", [P, 1, K], F32)
        w = sb("s_w", [P, K, C], F32)
        sel = sb("s_sel", [PER_BLOCK * ROWD, PER_BLOCK, P], BF16)
        ident = sb("s_ident", [P, P], F32)
        identb = sb("s_identb", [P, P], BF16)
        img = sb("s_img", [P, 2, K, (ROWS + 2 * REACH) * PADW], F32)
        off = sb("s_off", [P, TT, NOFF], F32)
        msk = sb("s_msk", [P, TT, NMASK], F32)
        hx = sb("s_hx", [P, TT * G, PTS, HATS], F32)
        hy = sb("s_hy", [P, TT * G, PTS, HATS], F32)
        outer = sb("s_outer", [P, 2, TT * G, HATS, HATS], F32)
        wts = sb("s_wts", [P, TT * G, WIN, WIN], F32)
        wtp = sb("s_wtp", [P, TT, K, D * ROWD], BF16)
        wtt = sb("s_wtt", [PER_BLOCK * ROWD, K, BLOCKS, T], BF16)
        dist = sb("s_dist", [P, HATS], F32)
        prod = sb("s_prod", [P, PROD_BUF, 2, T], F32)
        prod_pool = sb("s_prod_pool", [P, POOL_BUF, 2, T], F32)
        sums_pool = sb("s_sums_pool", [P, 2, 2, T], F32)
        dcn = sb("s_dcn", [P, K, T], F32)
        res = sb("s_res", [P, K, T], F32)
        spread = pb("s_spread", [P, 2, 2, T], F32)
        acc = pb("s_acc", [P, 2, T], F32)
        tps = pb("s_tps", [P, 2 * T], BF16)
        out_ps = pb("s_out_ps", [P, T], F32)
        consts = sem("s_consts")
        sel_ready = sem("s_sel_ready")
        img_loaded = [sem("s_img_loaded0"), sem("s_img_loaded1")]
        off_loaded = sem("s_off_loaded")
        res_loaded = sem("s_res_loaded")
        stored = sem("s_stored")
        dist_ready = sem("s_dist_ready")
        hat_step = sem("s_hat_step")
        masked = sem("s_masked")
        outer_ready = sem("s_outer_ready")
        added = sem("s_added")
        part_cast = sem("s_part_cast")
        part_left = sem("s_part_left")
        transposed = sem("s_transposed")
        wtt_ready = sem("s_wtt_ready")
        spread_ready = sem("s_spread_ready")
        multiplied = sem("s_multiplied")
        pe_summed = sem("s_pe_summed")
        last_summed = sem("s_last_summed")
        pool_summed = sem("s_pool_summed")
        acc_read = sem("s_acc_read")
        out_filled = sem("s_out_filled")
        out_ready = sem("s_out_ready")
        block = ctx.enter_context(nc.Block())
        CH = B * NT
        NB = K * BLOCKS
        NP = K * PAIRS
        POOL_PAIRS = [p for p in range(PAIRS - 1) if p % 2 == 1]
        PE_PAIRS = [p for p in range(PAIRS) if p not in POOL_PAIRS]
        ADDS = len(POOL_PAIRS) - 1
        LAST_SUM_AT = 3
        OUT_AT = [5 + 3 * t // 2 for t in range(K * K)]
        OUT_DONE_AT = [OUT_AT[K * o + K - 1] + 1 for o in range(K)]
        LEAVE_AT = [2 * q for q in range(2 * K)]
        MASKED_AT = 12
        OUTER_AT = [18 + 6 * q for q in range(PTS)]
        CLEAR_AT = 20
        ADD_AT = [26 + 6 * q for q in range(PTS)]

        def pool_number(n, c):
            return K * ADDS * n + c + 1

        def units(eng, run):
            run(0, 0, False, True, True)
            run(1, 1, True, True, True)
            with eng.Fori(1, CH // 2 - 1) as i:
                run(2 * i, 0, True, True, True)
                run(2 * i + 1, 1, True, True, True)
            run(CH - 2, 0, True, True, False)
            run(CH - 1, 1, True, False, False)

        def block_rows(blk):
            return min(PER_BLOCK, D - blk * PER_BLOCK) * ROWD

        def part_view(i, k):
            return wtp[:, :, k, :].rearrange("p t (d q g) -> p t d q g", q=PARTS, g=GK)[:, :, :, i, :]

        def weight_view(k):
            return wts[:, :, :, :].rearrange("p (t k g) y x -> p k t (y x) g", k=K, g=GK)[:, k]

        @block.sync
        def _(sp):
            sel_f = wts[0:PER_BLOCK * ROWD, 0:27, :, :].rearrange("p a b c -> p (a b c)")[:, 0:PER_BLOCK * P]
            for dst, src in ((vec[:, :, :], vectors[:, OUT_B:OUT_B + 1, :]), (w[:, :, :], w_out), (sel_f, sel_tab), (ident[:, :], ident_mat)):
                sp.dma_start(dst, src).then_inc(consts, 16)

            def load_image(n, u):
                sp.dma_start(img[:, u], xproj[:, bass.ds((n // NT) * K, K), bass.ds((n % NT) * (ROWS * PADW), (ROWS + 2 * REACH) * PADW)]).then_inc(img_loaded[u], 16)

            def load_offsets(n):
                sp.dma_start(off[:, :, :], offsets[:, bass.ds(n * TT, TT), :]).then_inc(off_loaded, 16)
                sp.dma_start(msk[:, :, :], masks[:, bass.ds(n * TT, TT), :]).then_inc(off_loaded, 16)

            def run(n, u, has_prev, has_1, has_2):
                if has_1:
                    wait(sp, multiplied, NP * n)
                    load_image(n + 1, 1 - u)
                if has_2:
                    sp.wait_ge(masked, n + 2)
                    load_offsets(n + 2)
                if has_prev:
                    sp.wait_ge(out_ready, K * n)
                    sp.dma_start(outv[:, bass.ds(((n - 1) // NT) * K, K), bass.ds(((n - 1) % NT) * T, T)], res[:, :, :]).then_inc(stored, 16)
                    sp.wait_ge(stored, 16 * n)
                sp.dma_start(res[:, :, :], x2[:, bass.ds((n // NT) * K, K), bass.ds((n % NT) * T, T)]).then_inc(res_loaded, 16)

            outv = out.rearrange("b (k p) h w -> p (b k) (h w)", p=P)
            load_image(0, 0)
            load_offsets(0)
            sp.wait_ge(masked, 1)
            load_offsets(1)
            units(sp, run)
            sp.wait_ge(out_ready, K * CH)
            sp.dma_start(outv[:, SEQ - K:SEQ, HW - T:HW], res[:, :, :]).then_inc(stored, 16)
            sp.wait_ge(stored, 16 * CH)

        @block.scalar
        def _(act):
            act.wait_ge(consts, 64)
            sel_f = wts[0:PER_BLOCK * ROWD, 0:27, :, :].rearrange("p a b c -> p (a b c)")[:, 0:PER_BLOCK * P]
            nc.scalar.activation(sel[:, :, :].rearrange("p a b -> p (a b)"), sel_f, ACT.Copy).then_inc(sel_ready, 1)
            nc.scalar.activation(identb[:, :], ident[:, :], ACT.Copy).then_inc(sel_ready, 1)

            def hats(n):
                act.wait_ge(off_loaded, 32 * n + 32)
                wait(act, outer_ready, PTS * n)
                o = off[:, :, :].rearrange("p t (q c) -> p (t q) c", c=2)
                for c, dst in ((0, hx), (1, hy)):
                    for r in range(HATS):
                        a = nc.scalar.activation(dst[:, :, :, r].rearrange("p a b -> p (a b)"), o[:, :, c], ACT.Abs, bias=dist[:, r:r + 1])
                a.then_inc(hat_step, 1)
                act.wait_ge(hat_step, 2 * n + 1)
                for dst in (hx, hy):
                    d = dst[:, :, :, :].rearrange("p a b c -> p (a b c)")
                    a = nc.scalar.activation(d, d, ACT.Relu, scale=-1.0, bias=1.0)
                a.then_inc(hat_step, 1)

            def cast_part(n, i, k):
                if i > 0:
                    act.wait_ge(part_left, 2 * K * n + 2 * k + 1)
                elif k == 0:
                    act.wait_ge(added, 10 * n + 10)
                    wait(act, transposed, NB * n)
                nc.scalar.activation(part_view(i, k), weight_view(k), ACT.Copy).then_inc(part_cast, 1)

            def copy_block(n, i):
                k, blk = divmod(i, BLOCKS)
                rows = block_rows(blk)
                act.wait_ge(transposed, NB * n + i + 1)
                nc.scalar.activation(wtt[0:rows, k, blk, :], tps[0:rows, 0:T], ACT.Copy).then_inc(wtt_ready, 1)

            def copy_sum(n, k):
                act.wait_ge(last_summed, K * n + k + 1)
                wait(act, out_filled, K * n)
                nc.scalar.activation(dcn[:, k, :], acc[:, k % 2, :], ACT.Copy).then_inc(acc_read, 1)

            def run(n, u, has_prev, has_1, has_2):
                if has_1:
                    for k in range(K):
                        cast_part(n + 1, 0, k)
                    cast_part(n + 1, 1, 0)
                    cast_part(n + 1, 1, 1)
                for k in range(K):
                    for blk in range(BLOCKS):
                        if has_1:
                            copy_block(n + 1, k * BLOCKS + blk)
                        if blk == 0:
                            if k > 0:
                                copy_sum(n, k - 1)
                            elif has_prev:
                                copy_sum(n - 1, K - 1)
                        if has_1 and k == 0 and blk < K - 2:
                            cast_part(n + 1, 1, blk + 2)
                        if has_2 and (k, blk) == (0, 0):
                            hats(n + 2)

            act.wait_ge(dist_ready, HATS)
            hats(0)
            for i in range(2):
                for k in range(K):
                    cast_part(0, i, k)
            for i in range(NB):
                copy_block(0, i)
            hats(1)
            units(act, run)
            copy_sum(CH - 1, K - 1)

        @block.gpsimd
        def _(pool):
            for r in range(HATS):
                nc.gpsimd.memset(dist[:, r:r + 1], float(HATS // 2 - r)).then_inc(dist_ready, 1)

            def masked_hats(n):
                pool.wait_ge(hat_step, 2 * n + 2)
                nc.gpsimd.tensor_tensor(hy[:, :, :, :].rearrange("p a b c -> p (a b) c"), hy[:, :, :, :].rearrange("p a b c -> p (a b) c"),
                                        msk[:, :, :].rearrange("p a b -> p (a b)").unsqueeze(2).broadcast_to([P, TT * G * PTS, HATS]),
                                        ALU.mult).then_inc(masked, 1)
                pool.wait_ge(masked, n + 1)

            def outer_product(n, q):
                wait(pool, added, 10 * n + q)
                nc.gpsimd.tensor_tensor(outer[:, q % 2], hy[:, :, q, :].unsqueeze(3).broadcast_to([P, TT * G, HATS, HATS]),
                                        hx[:, :, q, :].unsqueeze(2).broadcast_to([P, TT * G, HATS, HATS]), ALU.mult).then_inc(outer_ready, 1)

            def weights(n):
                masked_hats(n)
                for q in range(PTS):
                    outer_product(n, q)

            def add_pair(n, k, c):
                pool.wait_ge(multiplied, NP * n + PAIRS * k + POOL_PAIRS[c + 1] + 1)
                wait(pool, pool_summed, pool_number(n, ADDS * k + c - 1))
                s = sums_pool[:, k % 2]
                nc.gpsimd.tensor_tensor(s, s, prod_pool[:, (ADDS * k + c) % POOL_BUF], ALU.add).then_inc(pool_summed, 1)

            def run(n, u, has_prev, has_1, has_2):
                for i in range(NP):
                    k, pair = divmod(i, PAIRS)
                    if pair in POOL_PAIRS[1:]:
                        add_pair(n, k, POOL_PAIRS.index(pair) - 1)
                    if has_2 and i == MASKED_AT:
                        masked_hats(n + 2)
                    if has_2 and i in OUTER_AT:
                        outer_product(n + 2, OUTER_AT.index(i))

            weights(0)
            weights(1)
            units(pool, run)

        @block.vector
        def _(dve):
            def clear_window(n):
                wait(dve, part_left, 2 * K * n)
                nc.vector.memset(wts[:, :, :, :].rearrange("p a b c -> p (a b c)"), 0.0).then_inc(added, 1)

            def add_point(n, q):
                ix, iy = divmod(q, 3)
                dve.wait_ge(outer_ready, PTS * n + q + 1)
                dve.wait_ge(added, 10 * n + q + 1)
                v = wts[:, :, iy:iy + HATS, ix:ix + HATS]
                nc.vector.tensor_tensor(v, v, outer[:, q % 2], ALU.add).then_inc(added, 1)

            def leave_part(n, k, i):
                dve.wait_ge(part_cast, 2 * K * n + K * i + k + 1)
                nc.vector.tensor_tensor(weight_view(k) if i == 0 else part_view(2, k), weight_view(k), part_view(i, k), ALU.subtract).then_inc(part_left, 1)

            def finish_output(n, o):
                dve.wait_ge(out_filled, K * n + o + 1)
                dve.wait_ge(res_loaded, 16 * n + 16)
                nc.vector.scalar_tensor_tensor(res[:, o, :], out_ps[:, :], vec[:, 0, o:o + 1], res[:, o, :], ALU.add, ALU.add).then_inc(out_ready, 1)

            def run(n, u, has_prev, has_1, has_2):
                dve.wait_ge(img_loaded[u], 16 * ((n + 2) // 2) if isinstance(n, int) else 8 * (n - u) + 16)
                for i in range(NP):
                    k, pair = divmod(i, PAIRS)
                    d0 = 2 * pair
                    ds = [d for d in (d0, d0 + 1) if d < D]
                    at = [(d // WIN) * PADW + d % WIN for d in ds]
                    dve.wait_ge(spread_ready, NP * n + i + 1)
                    if pair in PE_PAIRS:
                        c = len(PE_PAIRS) * k + PE_PAIRS.index(pair)
                        wait(dve, pe_summed, K * len(PE_PAIRS) * n + c - PROD_BUF + 1)
                        dst = prod[:, c % PROD_BUF, 0:len(ds), :]
                    elif pair == POOL_PAIRS[0]:
                        wait(dve, last_summed, K * n + k - 1)
                        dst = sums_pool[:, k % 2]
                    else:
                        c = ADDS * k + POOL_PAIRS.index(pair) - 1
                        wait(dve, pool_summed, pool_number(n, c - POOL_BUF))
                        dst = prod_pool[:, c % POOL_BUF]
                    nc.vector.tensor_tensor(
                        dst.rearrange("p a (r c) -> p a r c", c=IMG),
                        spread[:, i % 2, 0:len(ds), :].rearrange("p a (r c) -> p a r c", c=IMG),
                        window(u, k, at), ALU.mult).then_inc(multiplied, 1)
                    if has_1 and i in LEAVE_AT:
                        leave_part(n + 1, *divmod(LEAVE_AT.index(i), 2))
                    if has_prev and i in OUT_DONE_AT:
                        finish_output(n - 1, OUT_DONE_AT.index(i))
                    if has_2 and i == CLEAR_AT:
                        clear_window(n + 2)
                    if has_2 and i in ADD_AT:
                        add_point(n + 2, ADD_AT.index(i))

            def window(u, k, at):
                base = img[:, u, k, at[0]:at[0] + 1]
                steps = [[at[1] - at[0], 2]] if len(at) == 2 else [[1, 1]]
                return bass.AP(tensor=base.tensor, offset=base.offset, ap=[list(base.ap[0])] + steps + [[PADW, ROWS], [1, IMG]])

            def weights(n):
                clear_window(n)
                for q in range(PTS):
                    add_point(n, q)

            dve.wait_ge(sel_ready, 2)
            weights(0)
            for k in range(K):
                for i in range(2):
                    leave_part(0, k, i)
            weights(1)
            units(dve, run)
            for o in range(K):
                finish_output(CH - 1, o)

        @block.tensor
        def _(pe):
            def transpose_block(n, i):
                k, blk = divmod(i, BLOCKS)
                rows = block_rows(blk)
                if blk == 0:
                    pe.wait_ge(part_left, 2 * K * n + 2 * k + 2)
                wait(pe, wtt_ready, NB * n + i)
                for t in range(TT):
                    mm = nc.tensor.transpose(tps[0:rows, t * P:(t + 1) * P], wtp[:, t, k, blk * PER_BLOCK * ROWD:blk * PER_BLOCK * ROWD + rows], identb[:, :])
                mm.then_inc(transposed, 1)

            def spread_pair(n, i):
                k, pair = divmod(i, PAIRS)
                blk = 2 * pair // PER_BLOCK
                rows = block_rows(blk)
                pe.wait_ge(wtt_ready, NB * n + k * BLOCKS + blk + 1)
                wait(pe, multiplied, NP * n + i - 1)
                for a, d in enumerate(d for d in (2 * pair, 2 * pair + 1) if d < D):
                    mm = nc.tensor.matmul(spread[:, i % 2, a, :], sel[0:rows, d % PER_BLOCK, :], wtt[0:rows, k, blk, :], start=True, stop=True)
                mm.then_inc(spread_ready, 1)

            def sum_pair(n, i):
                k, pair = divmod(i, PAIRS)
                c = len(PE_PAIRS) * k + PE_PAIRS.index(pair)
                pe.wait_ge(multiplied, NP * n + i + 1)
                if pair == 0:
                    wait(pe, acc_read, K * n + k - 1)
                for a, d in enumerate(d for d in (2 * pair, 2 * pair + 1) if d < D):
                    mm = nc.tensor.matmul(acc[:, k % 2, :], ident[:, :], prod[:, c % PROD_BUF, a, :], start=d == 0, stop=False)
                mm.then_inc(pe_summed, 1)

            def last_sum(n, k):
                pe.wait_ge(pool_summed, pool_number(n, ADDS * (k + 1) - 1))
                for a in range(2):
                    mm = nc.tensor.matmul(acc[:, k % 2, :], ident[:, :], sums_pool[:, k % 2, a, :], start=False, stop=a == 1)
                mm.then_inc(last_summed, 1)

            def project_out(n, o, k):
                if k == 0:
                    pe.wait_ge(acc_read, K * n + K)
                    wait(pe, out_ready, K * n + o)
                mm = nc.tensor.matmul(out_ps[:, :], w[:, k, o * P:(o + 1) * P], dcn[:, k, :], start=k == 0, stop=k == K - 1)
                if k == K - 1:
                    mm.then_inc(out_filled, 1)

            def run(n, u, has_prev, has_1, has_2):
                for i in range(NP):
                    k, pair = divmod(i, PAIRS)
                    if i + 2 < NP:
                        spread_pair(n, i + 2)
                    elif has_1:
                        spread_pair(n + 1, i + 2 - NP)
                    if pair in PE_PAIRS:
                        sum_pair(n, i)
                    if pair == LAST_SUM_AT:
                        if k > 0:
                            last_sum(n, k - 1)
                        elif has_prev:
                            last_sum(n - 1, K - 1)
                    if has_prev and i in OUT_AT:
                        project_out(n - 1, *divmod(OUT_AT.index(i), K))
                    if has_1 and (pair % (PER_BLOCK // 2) == PER_BLOCK // 2 - 1 or pair == PAIRS - 1):
                        transpose_block(n + 1, k * BLOCKS + pair // (PER_BLOCK // 2))

            pe.wait_ge(consts, 64)
            pe.wait_ge(sel_ready, 2)
            for i in range(NB):
                transpose_block(0, i)
            spread_pair(0, 0)
            spread_pair(0, 1)
            units(pe, run)
            last_sum(CH - 1, K - 1)
            for o in range(K):
                for k in range(K):
                    project_out(CH - 1, o, k)


CORNERS = 4
CG = C // G
PIX = PADW * PADW


def phase_sample_any(nc, sem, x2, xproj, offsets, masks, peak, table, out, vectors, w_out, ident_mat, grid_tab):
    with ExitStack() as ctx:
        sb = lambda n, s, d: ctx.enter_context(nc.sbuf_tensor(n, s, d))
        pb = lambda n, s, d: ctx.enter_context(nc.psum_tensor(n, s, d))
        TILES = B * HW // P
        PX = 100
        GRID = 2 * PTS + G + 2 * TILES
        peaks = sb("g_peaks", [P, B * NT], F32)
        top = sb("g_top", [P, 2], F32)
        flag = sb("g_flag", [P, 1], I32)
        consts = sem("g_consts")
        peak_step = sem("g_peak_step")

        with nc.Block() as block:
            @block.sync
            def _(sp):
                sp.dma_start(peaks[:, :], peak).then_inc(consts, 16)

            @block.vector
            def _(dve):
                dve.wait_ge(consts, 16)
                nc.vector.tensor_reduce(top[:, 0:1], peaks[:, :], AX.X, ALU.max).then_inc(peak_step, 1)
                dve.wait_ge(peak_step, 2)
                nc.vector.tensor_scalar(flag[:, :], top[:, 1:2], 2.0, None, ALU.is_gt).then_inc(peak_step, 1)

            @block.gpsimd
            def _(pool):
                pool.wait_ge(peak_step, 1)
                nc.gpsimd.partition_all_reduce(top[:, 1:2], top[:, 0:1], P, bass.bass_isa.ReduceOp.max).then_inc(peak_step, 1)

        vec = sb("g_vec", [P, 1, K], F32)
        w = sb("g_w", [P, K, C], F32)
        ident = sb("g_ident", [P, P], F32)
        grid = sb("g_grid", [P, GRID], F32)
        img = sb("g_img", [P, PIX], F32)
        tr = sb("g_tr", [PX, P], F32)
        off = sb("g_off", [P, NOFF], F32)
        msk = sb("g_msk", [P, NMASK], F32)
        pos = sb("g_pos", [P, 2, NMASK], F32)
        low = sb("g_low", [P, 2, NMASK], F32)
        lowi = sb("g_lowi", [P, 2, NMASK], I32)
        over = sb("g_over", [P, 2, NMASK], F32)
        cw = sb("g_cw", [P, CORNERS, NMASK], F32)
        row = sb("g_row", [P, NMASK], F32)
        cwg = sb("g_cwg", [P, CORNERS, PTS], F32)
        rowg = sb("g_rowg", [P, CORNERS, PTS], I32)
        got = sb("g_got", [P, CORNERS * PTS, CG], F32)
        sampled = sb("g_sampled", [P, C], F32)
        dcn = sb("g_dcn", [P, K, P], F32)
        res = sb("g_res", [P, K, P], F32)
        ps = pb("g_ps", [P, T], F32)
        img_loaded = sem("g_img_loaded")
        tr_ready = sem("g_tr_ready")
        tr_copied = sem("g_tr_copied")
        table_stored = sem("g_table_stored")
        table_done = sem("g_table_done")
        tile_loaded = sem("g_tile_loaded")
        step = sem("g_step")
        rows_ready = sem("g_rows_ready")
        gathered = sem("g_gathered")
        turns = sem("g_turns")
        group_gathered = sem("g_group_gathered")
        cwg_ready = sem("g_cwg_ready")
        products = sem("g_products")
        group_done = sem("g_group_done")
        flipped = sem("g_flipped")
        flip_copied = sem("g_flip_copied")
        out_filled = sem("g_out_filled")
        out_ready = sem("g_out_ready")
        stored = sem("g_stored")
        block = ctx.enter_context(nc.Block())
        STEPS = 16
        outv = out.rearrange("b (k p) h w -> p (b k) (h w)", p=P)

        table_v = table.rearrange("(g q) c -> q g c", q=PIX)

        @block.sync
        def _(sp):
            with sp.If(sp.value_load(flag[0:1, 0:1], min_val=0, max_val=1) > 0):
                sp.sem_inc(table_done, 1)
                for dst, src in ((vec[:, :, :], vectors[:, OUT_B:OUT_B + 1, :]), (w[:, :, :], w_out), (ident[:, :], ident_mat), (grid[:, :], grid_tab)):
                    sp.dma_start(dst, src).then_inc(consts, 16)
                with sp.Fori(0, SEQ) as r:
                    sp.wait_ge(tr_ready, (PIX // PX) * r + 1)
                    sp.dma_start(img[:, :], xproj[:, bass.ds(r, 1), :].rearrange("p o t -> p (o t)")).then_inc(img_loaded, 16)
                    with sp.Fori(0, PIX // PX) as i:
                        sp.wait_ge(tr_copied, r * (PIX // PX) + i + 2)
                        sp.dma_start(table_v[bass.ds(i * PX, PX), bass.ds(r * GK, GK), :], tr[:, :].rearrange("q (g c) -> q g c", c=CG)).then_inc(table_stored, 16)
                        sp.wait_ge(table_stored, (r * (PIX // PX) + i) * 16 + 16)
                        sp.sem_inc(table_done, 1)
                with sp.Fori(0, TILES) as n:
                    slabs = sp.snap((n // (HW // P)) * K)
                    pixels = sp.snap((n % (HW // P)) * P)
                    sp.wait_ge(out_ready, K * n + 1)
                    sp.dma_start(off[:, :], offsets[:, bass.ds(n, 1), :].rearrange("p o q -> p (o q)")).then_inc(tile_loaded, 16)
                    sp.dma_start(msk[:, :], masks[:, bass.ds(n, 1), :].rearrange("p o q -> p (o q)")).then_inc(tile_loaded, 16)
                    sp.dma_start(res[:, :, :], x2[:, bass.ds(slabs, K), bass.ds(pixels, P)]).then_inc(tile_loaded, 16)
                    sp.wait_ge(out_ready, K * n + K + 1)
                    sp.dma_start(outv[:, bass.ds(slabs, K), bass.ds(pixels, P)], res[:, :, :]).then_inc(stored, 16)
                    sp.wait_ge(stored, 16 * n + 16)
                    sp.sem_inc(turns, 1)

        @block.tensor
        def _(pe):
            with pe.If(pe.value_load(flag[0:1, 0:1], min_val=0, max_val=1) > 0):
                pe.sem_inc(tr_ready, 1)
                pe.wait_ge(consts, 80)
                with pe.Fori(0, SEQ) as r:
                    pe.wait_ge(img_loaded, 16 * r + 16)
                    for i in range(PIX // PX):
                        pe.wait_ge(tr_copied, r * (PIX // PX) + i + 1)
                        nc.tensor.transpose(ps[0:PX, 0:P], img[:, i * PX:(i + 1) * PX], ident[:, :]).then_inc(tr_ready, 1)
                with pe.Fori(0, TILES) as n:
                    pe.wait_ge(group_done, G * n + G)
                    for k in range(K):
                        pe.wait_ge(flip_copied, K * n + k + 1)
                        if k == 0:
                            pe.wait_ge(out_ready, K * n + 1)
                        nc.tensor.transpose(ps[:, 0:P], sampled[:, k * P:(k + 1) * P], ident[:, :]).then_inc(flipped, 1)
                    pe.wait_ge(flip_copied, K * n + K + 1)
                    for o in range(K):
                        pe.wait_ge(out_ready, K * n + o + 1)
                        for k in range(K):
                            mm = nc.tensor.matmul(ps[:, 0:P], w[:, k, o * P:(o + 1) * P], dcn[:, k, :], start=k == 0, stop=k == K - 1)
                        mm.then_inc(out_filled, 1)

        @block.scalar
        def _(act):
            with act.If(act.value_load(flag[0:1, 0:1], min_val=0, max_val=1) > 0):
                act.sem_inc(tr_copied, 1)
                act.sem_inc(flip_copied, 1)
                with act.Fori(0, SEQ * PIX // PX) as i:
                    act.wait_ge(tr_ready, i + 2)
                    act.wait_ge(table_done, i + 1)
                    nc.scalar.activation(tr[:, :], ps[0:PX, 0:P], ACT.Copy).then_inc(tr_copied, 1)
                with act.Fori(0, TILES) as n:
                    for k in range(K):
                        act.wait_ge(flipped, K * n + k + 1)
                        nc.scalar.activation(dcn[:, k, :], ps[:, 0:P], ACT.Copy).then_inc(flip_copied, 1)

        @block.gpsimd
        def _(pool):
            with pool.If(pool.value_load(flag[0:1, 0:1], min_val=0, max_val=1) > 0):
                pool.sem_inc(group_gathered, 1)
                pool.wait_ge(table_done, SEQ * PIX // PX + 1)
                with pool.Fori(0, TILES) as n:
                    with pool.Fori(0, G) as g:
                        pool.wait_ge(rows_ready, n * G + g + 1)
                        pool.sem_inc(turns, 1)
                        for q in range(CORNERS * PTS):
                            nc.gpsimd.indirect_dma_start(
                                out=got[:, q, :], out_offset=None, in_=table,
                                in_offset=bass.IndirectOffsetOnAxis(ap=rowg[:, q // PTS, q % PTS:q % PTS + 1], axis=0),
                            ).then_inc(gathered, 16)
                        pool.wait_ge(gathered, 16 * CORNERS * PTS)
                        pool.dma_reset(range(gathered.num, gathered.num + 1))
                        pool.sem_clear(gathered)
                        pool.sem_inc(group_gathered, 1)

        @block.vector
        def _(dve):
            with dve.If(dve.value_load(flag[0:1, 0:1], min_val=0, max_val=1) > 0):
                v = nc.vector
                dve.sem_inc(out_ready, 1)
                dve.wait_ge(consts, 80)
                with dve.Fori(0, TILES) as n:
                    done = [0]

                    def link(ins):
                        done[0] += 1
                        ins.then_inc(step, 1)
                        dve.wait_ge(step, STEPS * n + done[0])

                    dve.wait_ge(tile_loaded, 48 * n + 48)
                    for c in range(2):
                        o = off[:, :].rearrange("p (g q c) -> p g q c", q=PTS, c=2)[:, :, :, c]
                        at = grid[:, c * PTS:(c + 1) * PTS].unsqueeze(1).broadcast_to([P, G, PTS])
                        link(v.tensor_tensor(pos[:, c, :].rearrange("p (g q) -> p g q", q=PTS), o, at, ALU.add))
                    tile_y = grid[:, bass.ds(2 * PTS + G + n, 1)].broadcast_to([P, NMASK])
                    link(v.tensor_tensor(pos[:, 1, :], pos[:, 1, :], tile_y, ALU.add))
                    link(v.tensor_scalar(pos[:, :, :], pos[:, :, :], float(REACH - 1), float(REACH + IMG), ALU.max, ALU.min))
                    link(v.tensor_copy(lowi[:, :, :], pos[:, :, :]))
                    link(v.tensor_copy(low[:, :, :], lowi[:, :, :]))
                    link(v.tensor_tensor(over[:, :, :], low[:, :, :], pos[:, :, :], ALU.is_gt))
                    link(v.tensor_tensor(low[:, :, :], low[:, :, :], over[:, :, :], ALU.subtract))
                    link(v.tensor_tensor(pos[:, :, :], pos[:, :, :], low[:, :, :], ALU.subtract))
                    link(v.tensor_tensor(over[:, 1, :], msk[:, :], pos[:, 1, :], ALU.mult))
                    link(v.tensor_tensor(over[:, 0, :], msk[:, :], over[:, 1, :], ALU.subtract))
                    fx = pos[:, 0, :].unsqueeze(1).broadcast_to([P, 2, NMASK])
                    link(v.tensor_tensor(cw[:, 1:4:2, :], over[:, :, :], fx, ALU.mult))
                    link(v.tensor_tensor(cw[:, 0:4:2, :], over[:, :, :], cw[:, 1:4:2, :], ALU.subtract))
                    link(v.scalar_tensor_tensor(row[:, :], low[:, 1, :], float(PADW), low[:, 0, :], ALU.mult, ALU.add))
                    link(v.tensor_tensor(row[:, :].rearrange("p (g q) -> p g q", q=PTS), row[:, :].rearrange("p (g q) -> p g q", q=PTS),
                                         grid[:, 2 * PTS:2 * PTS + G].unsqueeze(2).broadcast_to([P, G, PTS]), ALU.add))
                    tile_row = grid[:, bass.ds(2 * PTS + G + TILES + n, 1)].broadcast_to([P, NMASK])
                    v.tensor_tensor(row[:, :], row[:, :], tile_row, ALU.add).then_inc(step, 1)
                    assert done[0] + 1 == STEPS
                    with dve.Fori(0, G) as g:
                        dve.wait_ge(step, STEPS * n + STEPS)
                        dve.wait_ge(group_gathered, n * G + g + 1)
                        for c, move in enumerate((0, 1, PADW, PADW + 1)):
                            i = v.tensor_scalar(rowg[:, c, :], row[:, bass.ds(g * PTS, PTS)], float(move), None, ALU.add)
                        i.then_inc(rows_ready, 1)
                        i = v.tensor_scalar(cwg[:, :, :], cw[:, :, bass.ds(g * PTS, PTS)], 1.0, None, ALU.mult).then_inc(cwg_ready, 1)
                        dve.wait_ge(cwg_ready, n * G + g + 1)
                        dve.wait_ge(group_gathered, n * G + g + 2)
                        v.tensor_tensor(got[:, :, :], got[:, :, :], cwg[:, :, :].rearrange("p a b -> p (a b)").unsqueeze(2).broadcast_to([P, CORNERS * PTS, CG]),
                                        ALU.mult).then_inc(products, 1)
                        dve.wait_ge(products, n * G + g + 1)
                        v.tensor_reduce(sampled[:, bass.ds(g * CG, CG)], got[:, :, :].rearrange("p a b -> p b a"), AX.X, ALU.add).then_inc(group_done, 1)
                    for o in range(K):
                        dve.wait_ge(out_filled, K * n + o + 1)
                        v.scalar_tensor_tensor(res[:, o, :], ps[:, 0:P], vec[:, 0, o:o + 1], res[:, o, :], ALU.add, ALU.add).then_inc(out_ready, 1)


def build(nc, x, vectors, mvec, w_in, w_conv, w_x, w_dtr, w_dt, w_out, a_log, w_proj, l1_in_w, dw_w, w_om, b_om, l1_out_w,
          ones_mat, group_mat, ident_mat, keep_tab, bc_sel, point_sel, grid_tab, out):
    dram = lambda name, shape: nc.dram_tensor(name, shape, F32, kind="Internal").ap()
    xn = dram("xn_scratch", (P, UNITS, T))
    halo = dram("halo_scratch", (P, UNITS + 1, 3))
    ym = dram("ym_scratch", (P, UNITS, T))
    x2 = dram("x2_scratch", (P, SEQ, HW))
    stats = dram("stats_scratch", (P, SEQ, NT, 6))
    xproj = dram("xproj_scratch", (P, SEQ, PADW * PADW))
    offsets = dram("offsets_scratch", (P, B * HW // P, NOFF))
    masks = dram("masks_scratch", (P, B * HW // P, NMASK))
    peak = dram("peak_scratch", (P, B * NT))
    table = dram("table_scratch", (B * G * PADW * PADW, CG))
    with ExitStack() as ctx:
        sem = lambda name: ctx.enter_context(nc.semaphore(name))
        phase_input_norm(nc, sem, x, xn.rearrange("p (r t) c -> p r (t c)", t=NT), halo, vectors, ones_mat, group_mat)
        phase_mamba(nc, sem, xn, halo, ym, w_in, w_conv, w_x, w_dtr, w_dt, w_out, a_log, mvec, keep_tab, bc_sel, ident_mat)
        phase_project(nc, sem, ym, x, x2, stats, vectors, w_proj, ones_mat)
        phase_offsets(nc, sem, x2, stats, xproj, offsets, masks, peak, vectors, l1_in_w, dw_w, w_om, b_om, ones_mat, group_mat)
        phase_sample(nc, sem, x2, xproj, offsets, masks, out, vectors, l1_out_w, point_sel, ident_mat)
        phase_sample_any(nc, sem, x2, xproj, offsets, masks, peak, table, out, vectors, l1_out_w, ident_mat, grid_tab)


def laid_out(inputs):
    at = np.ascontiguousarray
    l0 = lambda name: np.asarray(inputs["L0_conv_" + name])
    l1 = lambda name: np.asarray(inputs["L1_conv_" + name])
    columns = lambda v: v.reshape(-1, P).T
    rows = lambda m: at(m.reshape(-1, P, m.shape[1]).transpose(1, 0, 2))
    f32 = np.float32
    x_proj = l0("x_proj_w")
    bc_sel = np.zeros((PARTS * 2 * NS, 2 * NS, P), f32)
    for r in range(2 * NS):
        for part in range(PARTS):
            bc_sel[part * 2 * NS + r, r] = 1
    point_sel = np.zeros((PER_BLOCK * ROWD, PER_BLOCK, P), f32)
    for d in range(PER_BLOCK):
        for part in range(PARTS):
            for g in range(GK):
                point_sel[d * ROWD + part * GK + g, d, g * CG:(g + 1) * CG] = 1
    keep = np.ones((P, UNITS), f32)
    keep[:, ::NT] = 0
    group = np.zeros((P, P), f32)
    per = C // 32
    for g in range(P // per):
        group[g * per:(g + 1) * per, g * per:(g + 1) * per] = 1.0 / per
    pixel, point, tile = np.arange(P), np.arange(PTS), np.arange(B * HW // P)
    per_image = HW // P
    grid = np.concatenate([
        (pixel % IMG)[:, None] + (point // 3 - 1)[None] + REACH,
        (pixel // IMG)[:, None] + (point % 3 - 1)[None] + REACH,
        np.broadcast_to(np.arange(G) * PADW * PADW, (P, G)),
        np.broadcast_to((P // IMG) * (tile % per_image), (P, tile.size)),
        np.broadcast_to((tile // per_image) * G * PADW * PADW, (P, tile.size)),
    ], 1).astype(f32)
    return {
        "x": at(np.asarray(inputs["x"])),
        "vectors": at(np.stack([columns(v) for v in (l0("norm_g"), l0("norm_b"), l0("proj_b"), l1("dw_b"), l1("ln_g"), l1("ln_b"), l1("in_b"), l1("out_b"))], 1)),
        "mvec": at(np.concatenate([columns(l0("conv_b")), columns(l0("dt_proj_b")), columns(l0("D_param")), np.broadcast_to(l0("skip_scale")[None], (P, 1))], 1)),
        "w_in": at(l0("in_proj_w").T),
        "w_conv": at(l0("conv_w").T).reshape(-1),
        "w_x": at(np.tile(rows(x_proj[RANK:].T), (1, 1, PARTS))),
        "w_dtr": rows(x_proj[:RANK].T),
        "w_dt": at(l0("dt_proj_w").T),
        "w_out": rows(l0("out_proj_w").T),
        "a_log": rows(l0("A_log")),
        "w_proj": rows(l0("proj_w").T),
        "l1_in_w": rows(l1("in_w")),
        "dw_w": rows(l1("dw_w").reshape(C, 9)),
        "w_om": rows(np.concatenate([l1("off_w"), l1("mask_w")], 1)),
        "b_om": at(np.concatenate([l1("off_b"), l1("mask_b")])),
        "l1_out_w": rows(l1("out_w")),
        "ones_mat": np.full((P, P), 1.0 / C, f32),
        "group_mat": group,
        "ident_mat": np.eye(P, dtype=f32),
        "keep_tab": keep,
        "bc_sel": bc_sel.reshape(PARTS * 2 * NS, -1),
        "point_sel": point_sel.reshape(PER_BLOCK * ROWD, -1),
        "grid_tab": grid,
    }


def kernel(**inputs):
    import concourse.bacc as _bacc
    from concourse.bass_utils import run_bass_kernel_spmd as _run

    nc = _bacc.Bacc("TRN2", target_bir_lowering=False, num_devices=1)
    arrays = laid_out(inputs)
    args = [nc.dram_tensor(f"in_{name}", a.shape, mybir.dt.from_np(a.dtype), kind="ExternalInput").ap() for name, a in arrays.items()]
    out = nc.dram_tensor("out_0_dram", (B, C, IMG, IMG), F32, kind="ExternalOutput").ap()
    build(nc, *args, out)
    r = _run(nc, [{f"in_{name}": a for name, a in arrays.items()}], core_ids=[0])
    return r.results[0]["out_0_dram"]
```

```python
import numpy as np
import concourse.bass as bass
from concourse import mybir
from contextlib import ExitStack

F32 = mybir.dt.float32
BF16 = mybir.dt.bfloat16
I32 = mybir.dt.int32
ALU = mybir.AluOpType
ACT = mybir.ActivationFunctionType
AX = mybir.AxisListType

B, C, HW = 4, 512, 4096
IMG = 64
P = 128
K = C // P
T = 512
NT = HW // T
SEQ = B * K
GN_EPS, LN_EPS = 1e-5, 1e-5
NORM_G, NORM_B, PROJ_B, DW_B, LN_G, LN_B, IN_B, OUT_B = range(8)


def over_slabs(ap):
    return ap.unsqueeze(1).broadcast_to([P, K, T])


class LayerNorm:

    def __init__(self, nc, name, sb, pb, sem, x, ones):
        self.nc, self.x, self.ones = nc, x, ones
        self.sq = sb(name + "_sq", [P, 2, K, T], F32)
        self.stat = pb(name + "_stat", [P, 2, T], F32)
        self.rstd = sb(name + "_rstd", [P, 2, T], F32)
        self.input_ready = sem(name + "_input_ready")
        self.mean_ready = sem(name + "_mean_ready")
        self.centred = sem(name + "_centred")
        self.squared = sem(name + "_squared")
        self.var_ready = sem(name + "_var_ready")
        self.std_ready = sem(name + "_std_ready")
        self.rstd_ready = sem(name + "_rstd_ready")
        self.scaled = sem(name + "_scaled")

    def pe_mean(self, pe, u, c, x=None):
        x = u if x is None else x
        pe.wait_ge(self.input_ready, c + 1)
        for k in range(K):
            mm = self.nc.tensor.matmul(self.stat[:, u, :], self.ones[:, :], self.x[:, x, k, :], start=k == 0, stop=k == K - 1)
        mm.then_inc(self.mean_ready, 1)

    def dve_centre(self, dve, u, c, x=None):
        x = u if x is None else x
        dve.wait_ge(self.mean_ready, c + 1)
        self.nc.vector.tensor_tensor(self.x[:, x], self.x[:, x], over_slabs(self.stat[:, u, :]), ALU.subtract).then_inc(self.centred, 1)

    def act_square(self, act, u, c, x=None):
        x = u if x is None else x
        act.wait_ge(self.centred, c + 1)
        self.nc.scalar.activation(self.sq[:, u], self.x[:, x], ACT.Square).then_inc(self.squared, 1)

    def pe_var(self, pe, u, c):
        pe.wait_ge(self.squared, c + 1)
        for k in range(K):
            mm = self.nc.tensor.matmul(self.stat[:, u, :], self.ones[:, :], self.sq[:, u, k, :], start=k == 0, stop=k == K - 1)
        mm.then_inc(self.var_ready, 1)

    def act_std(self, act, u, c, eps):
        act.wait_ge(self.var_ready, c + 1)
        self.nc.scalar.activation(self.rstd[:, u, :], self.stat[:, u, :], ACT.Sqrt, bias=eps).then_inc(self.std_ready, 1)

    def dve_scale(self, dve, u, c, x=None):
        x = u if x is None else x
        dve.wait_ge(self.std_ready, c + 1)
        self.nc.vector.reciprocal(self.rstd[:, u, :], self.rstd[:, u, :]).then_inc(self.rstd_ready, 1)
        dve.wait_ge(self.rstd_ready, c + 1)
        self.nc.vector.tensor_tensor(self.x[:, x], self.x[:, x], over_slabs(self.rstd[:, u, :]), ALU.mult).then_inc(self.scaled, 1)


def finish_group_norm(nc, sb, pb, sem, block, name, stats, group_avg, ready, eps_col):
    mv = sb(name + "_mv", [P, SEQ, 2], F32)
    mom = sb(name + "_mom", [P, 2, SEQ], F32)
    grp = sb(name + "_grp", [P, 2, SEQ], F32)
    aff = sb(name + "_aff", [P, 2, SEQ], F32)
    grp_ps = pb(name + "_grp_ps", [P, 2, SEQ], F32)
    step = sem(name + "_step")
    averaged = sem(name + "_averaged")
    rooted = sem(name + "_rooted")

    def dve_part(dve):
        n = [0]

        def link(ins):
            n[0] += 1
            ins.then_inc(step, 1)
            dve.wait_ge(step, n[0])

        if ready is not None:
            dve.wait_ge(*ready)
        for r in range(SEQ):
            nc.vector.bn_aggr(mv[:, r, :], stats[:, r, :, :].rearrange("p a b -> p (a b)")).then_inc(step, 1)
        n[0] = SEQ
        dve.wait_ge(step, SEQ)
        link(nc.vector.tensor_copy(mom[:, 0, :], mv[:, :, 0]))
        link(nc.vector.tensor_tensor(mom[:, 1, :], mv[:, :, 0], mv[:, :, 0], ALU.mult))
        link(nc.vector.tensor_tensor(mom[:, 1, :], mom[:, 1, :], mv[:, :, 1], ALU.add))
        done_mom = n[0]
        dve.wait_ge(averaged, 1)
        link(nc.vector.tensor_copy(grp[:, :, :], grp_ps[:, :, :]))
        link(nc.vector.tensor_tensor(aff[:, 0, :], grp[:, 0, :], grp[:, 0, :], ALU.mult))
        link(nc.vector.tensor_tensor(aff[:, 0, :], grp[:, 1, :], aff[:, 0, :], ALU.subtract))
        done_var = n[0]
        dve.wait_ge(rooted, 1)
        link(nc.vector.reciprocal(aff[:, 0, :], aff[:, 0, :]))
        link(nc.vector.tensor_tensor(aff[:, 1, :], grp[:, 0, :], aff[:, 0, :], ALU.mult))
        link(nc.vector.tensor_scalar(aff[:, 1, :], aff[:, 1, :], -1.0, None, ALU.mult))
        return done_mom, done_var

    dones = (SEQ + 3, SEQ + 6, SEQ + 9)

    def pe_part(pe):
        pe.wait_ge(step, dones[0])
        nc.tensor.matmul(grp_ps[:, :, :].rearrange("p a b -> p (a b)"), group_avg[:, :],
                         mom[:, :, :].rearrange("p a b -> p (a b)"), start=True, stop=True).then_inc(averaged, 1)

    def act_part(act):
        act.wait_ge(step, dones[1])
        nc.scalar.activation(aff[:, 0, :], aff[:, 0, :], ACT.Sqrt, bias=eps_col[:, 0:1]).then_inc(rooted, 1)

    return aff, dve_part, pe_part, act_part


def phase_input_norm(nc, sem, x, xn, halo, vectors, ones_mat, group_mat):
    halo_next = halo[:, 1:, :].rearrange("p (r t) c -> p r t c", t=NT)
    x_in = x.rearrange("b (k p) h w -> p (b k) (h w)", p=P)
    with ExitStack() as ctx:
        sb = lambda n, s, d: ctx.enter_context(nc.sbuf_tensor(n, s, d))
        pb = lambda n, s, d: ctx.enter_context(nc.psum_tensor(n, s, d))
        xs = sb("a_xs", [P, 2, HW], F32)
        stats = sb("a_stats", [P, SEQ, NT, 6], F32)
        ones = sb("a_ones", [P, P], F32)
        gavg = sb("a_gavg", [P, P], F32)
        gb = sb("a_gb", [P, 2, K], F32)
        aff_b = sb("a_aff_b", [P, 2, K], F32)
        eps = sb("a_eps", [P, 1], F32)
        xc = sb("a_xc", [P, 4, K, T], F32)
        xo = sb("a_xo", [P, 2, K, T], F32)
        zero = sb("a_zero", [P, SEQ, 3], F32)
        consts = sem("a_consts")
        eps_set = sem("a_eps_set")
        tile_loaded = [sem("a_tile_loaded0"), sem("a_tile_loaded1")]
        tile_free = sem("a_tile_free")
        chunk_loaded = [sem(f"a_chunk_loaded{i}") for i in range(4)]
        out_ready = sem("a_out_ready")
        out_stored = sem("a_out_stored")
        out_free = sem("a_out_free")
        affine_picked = sem("a_affine_picked")
        halo_stored = sem("a_halo_stored")
        ln = LayerNorm(nc, "a_ln", sb, pb, sem, xc, ones)
        block = ctx.enter_context(nc.Block())
        aff, gn_dve, gn_pe, gn_act = finish_group_norm(
            nc, sb, pb, sem, block, "a_gn", stats, gavg, (tile_free, 2 + SEQ), eps)
        gn_done = sem("a_gn_done")
        PAIRS = B * NT // 2

        @block.sync
        def _(sp):
            sp.dma_start(ones[:, :], ones_mat).then_inc(consts, 16)
            sp.dma_start(gavg[:, :], group_mat).then_inc(consts, 16)
            sp.dma_start(gb[:, :, :], vectors[:, NORM_G:NORM_B + 1, :]).then_inc(consts, 16)
            sp.sem_inc(tile_free, 2)
            with sp.Fori(0, SEQ // 2) as q:
                for u in range(2):
                    sp.wait_ge(tile_free, 2 * q + u + 1)
                    sp.dma_start(xs[:, u, :], x_in[:, bass.ds(2 * q + u, 1), :].rearrange("p o t -> p (o t)")).then_inc(tile_loaded[u], 16)
            sp.sem_inc(out_ready, 4)
            with sp.Fori(0, B) as b:
                with sp.Fori(0, NT // 4) as t4:
                    for i in range(4):
                        sp.wait_ge(out_ready, b * NT + t4 * 4 + i + 1)
                        sp.dma_start(xc[:, i], x_in[:, bass.ds(b * K, K), bass.ds((t4 * 4 + i) * T, T)]).then_inc(chunk_loaded[i], 16)

        @block.gpsimd
        def _(pool):
            nc.gpsimd.memset(eps[:, :], GN_EPS).then_inc(eps_set, 1)
            nc.gpsimd.memset(zero[:, :, :], 0.0).then_inc(eps_set, 1)
            pool.sem_inc(out_free, 2)
            with pool.Fori(0, B) as b:
                with pool.Fori(0, NT // 2) as t2:
                    for u in range(2):
                        n = b * NT + t2 * 2 + u
                        pool.wait_ge(out_ready, n + 5)
                        pool.dma_start(xn[:, bass.ds(b * K, K), bass.ds((t2 * 2 + u) * T, T)], xo[:, u]).then_inc(out_stored, 16)
                        pool.dma_start(halo_next[:, bass.ds(b * K, K), bass.ds(t2 * 2 + u, 1), :].rearrange("p k o c -> p k (o c)"),
                                       xo[:, u, :, T - 3:T]).then_inc(out_stored, 16)
                        pool.wait_ge(out_stored, 32 * n + 32)
                        pool.sem_inc(out_free, 1)
            pool.wait_ge(eps_set, 2)
            pool.dma_start(halo[:, 0:SEQ * NT, :].rearrange("p (r t) c -> p r t c", t=NT)[:, :, 0, :], zero[:, :, :]).then_inc(halo_stored, 16)
            pool.wait_ge(halo_stored, 16)

        @block.vector
        def _(dve):
            with dve.Fori(0, SEQ // 2) as q:
                for u in range(2):
                    dve.wait_ge(tile_loaded[u], 16 * q + 16)
                    for t in range(NT):
                        bn = nc.vector.bn_stats(stats[:, bass.ds(2 * q + u, 1), t, :].rearrange("p o s -> p (o s)"), xs[:, u, t * T:(t + 1) * T])
                    bn.then_inc(tile_free, 1)
            gn_dve(dve)
            dve.sem_inc(gn_done, 1)

            def centre(p, q):
                for u in range(2):
                    ln.dve_centre(dve, u, 2 * p + u, 2 * q + u)

            def scale(p, q):
                for u in range(2):
                    ln.dve_scale(dve, u, 2 * p + u, 2 * q + u)

            centre(0, 0)
            with dve.Fori(0, PAIRS // 2 - 1) as i:
                for q in range(2):
                    scale(2 * i + q, q)
                    centre(2 * i + q + 1, 1 - q)
            scale(PAIRS - 2, 0)
            centre(PAIRS - 1, 1)
            scale(PAIRS - 1, 1)

        @block.tensor
        def _(pe):
            pe.wait_ge(consts, 48)
            gn_pe(pe)

            def mean(p, q):
                for u in range(2):
                    wait(pe, ln.std_ready, 2 * p + u - 1)
                    ln.pe_mean(pe, u, 2 * p + u, 2 * q + u)

            def variance(p):
                for u in range(2):
                    ln.pe_var(pe, u, 2 * p + u)

            mean(0, 0)
            variance(0)
            with pe.Fori(0, PAIRS // 2 - 1) as i:
                for q in range(2):
                    mean(2 * i + q + 1, 1 - q)
                    variance(2 * i + q + 1)
            mean(PAIRS - 1, 1)
            variance(PAIRS - 1)

        @block.scalar
        def _(act):
            act.wait_ge(eps_set, 2)
            gn_act(act)
            act.wait_ge(gn_done, 1)
            act.wait_ge(consts, 48)
            def pick_affine(b):
                wait(act, ln.input_ready, b * NT)
                nc.scalar.activation(aff_b[:, :, :], aff[:, :, bass.ds(b * K, K)], ACT.Identity).then_inc(affine_picked, 1)
                act.wait_ge(affine_picked, b + 1)

            def group_normed(m, q):
                for u in range(2):
                    act.wait_ge(chunk_loaded[2 * q + u], 16 * m + 16)
                    for k in range(K):
                        gn = nc.scalar.activation(xc[:, 2 * q + u, k, :], xc[:, 2 * q + u, k, :], ACT.Identity,
                                                  scale=aff_b[:, 0, k:k + 1], bias=aff_b[:, 1, k:k + 1])
                    gn.then_inc(ln.input_ready, 1)

            def square(p, q):
                for u in range(2):
                    ln.act_square(act, u, 2 * p + u, 2 * q + u)

            def root(p):
                for u in range(2):
                    ln.act_std(act, u, 2 * p + u, eps[:, 0:1])

            def output(p, q):
                for u in range(2):
                    act.wait_ge(ln.scaled, 2 * p + u + 1)
                    act.wait_ge(out_free, 2 * p + u + 1)
                    for k in range(K):
                        o = nc.scalar.activation(xo[:, u, k, :], xc[:, 2 * q + u, k, :], ACT.Identity, scale=gb[:, 0, k:k + 1], bias=gb[:, 1, k:k + 1])
                    o.then_inc(out_ready, 1)

            def run(p, q, m):
                root(p)
                group_normed(m, 1 - q)
                output(p, q)
                square(p + 1, 1 - q)

            pick_affine(0)
            group_normed(0, 0)
            square(0, 0)
            per_image = NT // 2
            for i in range(per_image - 1):
                run(i, i % 2, (i + 1) // 2)
            with act.Fori(1, B) as b:
                pick_affine(b)
                for i in range(-1, per_image - 1):
                    run(b * per_image + i, i % 2, b * (per_image // 2) + (i + 1) // 2)
            root(PAIRS - 1)
            output(PAIRS - 1, 1)


NS = 16
RANK = 8
TAPS = 4
E2 = 2
UNITS = SEQ * NT
J = NS * E2
NBUF = 8
BBUF = 4
S_PRE = (0, 0, 1, 1, 1, 2, 2, 3, 3, 3, 8, 9, 9, 10, 12, 13)
S_OUT = (3, 5)
S_ACT = (6, 10, 18, 19, 20, 21, 22, 23, 23)
S_POOL = (27, 29)
S_DVE = (14, 18, 25)
S_GATE_AFTER = 1
S_DVE_OUT = 11
B_AHEAD = 6
B_COPY_AHEAD = 2


def at_steps(steps, what):
    return {s: [w for t, w in zip(steps, what) if t == s] for s in steps}


def wait(eng, sem, value):
    if not (isinstance(value, int) and value <= 0):
        eng.wait_ge(sem, value)


def phase_mamba(nc, sem, xn, halo, ym, w_in, w_conv, w_x, w_dtr, w_dt, w_out, a_log, mvec, keep_tab, sel_tab, ident_mat):
    with ExitStack() as ctx:
        sb = lambda n, s, d: ctx.enter_context(nc.sbuf_tensor(n, s, d))
        pb = lambda n, s, d: ctx.enter_context(nc.psum_tensor(n, s, d))
        win = sb("m_win", [P, 2 * E2 * P], F32)
        wcv = sb("m_wcv", [P, TAPS, E2 * P], F32)
        wx = sb("m_wx", [P, E2, 96], F32)
        wdtr = sb("m_wdtr", [P, E2, RANK], F32)
        wdt = sb("m_wdt", [RANK, E2 * P], F32)
        wout = sb("m_wout", [P, E2, P], F32)
        a = sb("m_a", [P, E2, NS], F32)
        mv = sb("m_mv", [P, 7], F32)
        keep = sb("m_keep", [P, UNITS], F32)
        sel = sb("m_sel", [96, 2 * NS, P], BF16)
        ident = sb("m_ident", [P, P], F32)
        x = sb("m_x", [P, 2, 3 + T], F32)
        xc = sb("m_xc", [P, 2, E2, T], F32)
        zs = sb("m_zs", [P, 2, E2, T], F32)
        dt = sb("m_dt", [P, 2, E2, T], F32)
        dtx = sb("m_dtx", [P, 2, E2, T], F32)
        bct = sb("m_bct", [96, 2, T], BF16)
        bcf = sb("m_bcf", [96, T], F32)
        bcr = sb("m_bcr", [64, T], F32)
        dtr = sb("m_dtr", [RANK, T], F32)
        v = sb("m_v", [P, E2, T], F32)
        ea = sb("m_ea", [P, E2, T], F32)
        eb = sb("m_eb", [P, E2, T], F32)
        ec = sb("m_ec", [P, E2, T], F32)
        h = sb("m_h", [P, J, T], F32)
        carry = sb("m_carry", [P, J], F32)
        da = sb("m_da", [P, NBUF, T], F32)
        dbx = sb("m_dbx", [P, NBUF, T], F32)
        hc = sb("m_hc", [P, NBUF, T], F32)
        b_all = sb("m_b_all", [P, BBUF, T], F32)
        yd = sb("m_yd", [P, E2, T], F32)
        yo = sb("m_yo", [P, T], F32)
        xo = sb("m_xo", [P, T], F32)
        y_ps = pb("m_y_ps", [P, E2, T], F32)
        b_ps = pb("m_b_ps", [P, 2, T], F32)
        c_ps = pb("m_c_ps", [P, 2, T], F32)
        pre = pb("m_pre", [P, 2, T], F32)

        consts = sem("m_consts")
        act_set_up = sem("m_act_set_up")
        dve_set_up = sem("m_dve_set_up")
        x_loaded = [sem("m_x_loaded0"), sem("m_x_loaded1")]
        skip_loaded = sem("m_skip_loaded")
        pre_filled = sem("m_pre_filled")
        out_filled = sem("m_out_filled")
        pre_used = sem("m_pre_used")
        zs_ready = sem("m_zs_ready")
        act_chain = sem("m_act_chain")
        bc_rest = sem("m_bc_rest")
        bct_ready = sem("m_bct_ready")
        log_parts = sem("m_log_parts")
        softplus_tail = sem("m_softplus_tail")
        pool_chain = sem("m_pool_chain")
        dt_ready = sem("m_dt_ready")
        dtx_ready = sem("m_dtx_ready")
        carried = sem("m_carried")
        b_filled = sem("m_b_filled")
        c_filled = sem("m_c_filled")
        b_copied = sem("m_b_copied")
        decays = sem("m_decays")
        inputs = sem("m_inputs")
        scanned = sem("m_scanned")
        products = sem("m_products")
        summed = sem("m_summed")
        y_read = sem("m_y_read")
        yz_ready = sem("m_yz_ready")
        out_ready = sem("m_out_ready")
        out_stored = sem("m_out_stored")
        block = ctx.enter_context(nc.Block())

        def units(eng, run):
            run(0, 0, 0, False, True)
            with eng.Fori(0, UNITS // 2 - 1) as i:
                run(2 * i + 1, i, 1, True, True)
                run(2 * i + 2, i + 1, 0, True, True)
            run(UNITS - 1, UNITS // 2 - 1, 1, True, False)

        @block.sync
        def _(sp):
            sel_f = h[0:96, 0:8, :].rearrange("p a b -> p (a b)")
            for dst, src in ((win[:, :], w_in), (wcv[:, :, :].rearrange("p a b -> p (a b)"), w_conv.partition_broadcast(P)),
                             (wx[:, :, :], w_x), (wdtr[:, :, :], w_dtr), (wdt[:, :], w_dt), (wout[:, :, :], w_out), (a[:, :, :], a_log),
                             (mv[:, :], mvec), (keep[:, :], keep_tab), (sel_f, sel_tab), (ident[:, :], ident_mat)):
                sp.dma_start(dst, src).then_inc(consts, 16)

            def load(n, u):
                sp.dma_start(x[:, u, 3:3 + T], xn[:, bass.ds(n, 1), :].rearrange("p o t -> p (o t)")).then_inc(x_loaded[u], 16)
                sp.dma_start(x[:, u, 0:3], halo[:, bass.ds(n, 1), :].rearrange("p o t -> p (o t)")).then_inc(x_loaded[u], 16)

            def load_skip(n):
                sp.dma_start(xo[:, :], xn[:, bass.ds(n, 1), :].rearrange("p o t -> p (o t)")).then_inc(skip_loaded, 16)

            def run(n, u, has_prev, has_second):
                if has_second:
                    sp.wait_ge(pre_filled, 8 * n + 4)
                    load(n + 2, u)
                if has_prev:
                    load_skip(n - 1)
                    sp.wait_ge(out_ready, n)
                    sp.dma_start(ym[:, bass.ds(n - 1, 1), :].rearrange("p o t -> p (o t)"), yo[:, :]).then_inc(out_stored, 16)

            load(0, 0)
            load(1, 1)
            run(0, 0, False, True)
            with sp.Fori(0, UNITS // 2 - 2) as i:
                run(2 * i + 1, 1, True, True)
                run(2 * i + 2, 0, True, True)
            run(UNITS - 3, 1, True, True)
            run(UNITS - 2, 0, True, False)
            run(UNITS - 1, 1, True, False)
            load_skip(UNITS - 1)
            sp.wait_ge(out_ready, UNITS)
            sp.dma_start(ym[:, UNITS - 1, :], yo[:, :]).then_inc(out_stored, 16)
            sp.wait_ge(out_stored, 16 * UNITS)

        @block.tensor
        def _(pe):
            def product_term(out, terms, i, filled):
                mm = nc.tensor.matmul(out, terms[i][0], terms[i][1], start=i == 0, stop=i == len(terms) - 1)
                if i == len(terms) - 1:
                    mm.then_inc(filled, 1)

            def pre_step(g, i, n, m, u):
                if i == 0:
                    wait(pe, pre_used, 8 * n + PRE_AFTER[g])
                if (g, i) == (0, 0):
                    pe.wait_ge(x_loaded[u], 32 * m + 32)
                if (g, i) == (5, 0):
                    wait(pe, out_ready, n - 1)
                if g < 2:
                    product_term(pre[:, g, :], [(win[:, (g + 2) * P:(g + 3) * P], x[:, u, 3:3 + T])], i, pre_filled)
                elif g < 4:
                    product_term(pre[:, g - 2, :], [(wcv[:, tap, (g - 2) * P:(g - 1) * P], x[:, u, tap:tap + T]) for tap in range(TAPS)], i, pre_filled)
                elif g == 4:
                    product_term(pre[0:RANK, 1, :], [(wdtr[:, e, :], xc[:, u, e, :]) for e in range(E2)], i, pre_filled)
                elif g == 5:
                    product_term(pre[0:96, 0, :], [(wx[:, e, :], xc[:, u, e, :]) for e in range(E2)], i, pre_filled)
                else:
                    product_term(pre[:, 7 - g, :], [(wdt[:, (g - 6) * P:(g - 5) * P], dtr[:, :])], i, pre_filled)

            def out_step(n, i, pre_before):
                if i == 0:
                    pe.wait_ge(yz_ready, n + 1)
                    wait(pe, pre_used, pre_before)
                product_term(pre[:, 0, :], [(wout[:, e, :], yd[:, e, :]) for e in range(E2)], i, out_filled)

            def spread_b(n, u, s):
                if s == 0:
                    pe.wait_ge(bct_ready, n + 1)
                wait(pe, b_copied, NS * n + s - 1)
                nc.tensor.matmul(b_ps[:, s % 2, :], sel[:, s, :], bct[:, u, :], start=True, stop=True).then_inc(b_filled, 1)

            def spread_c(n, u, s):
                wait(pe, products, J * n + E2 * (s - 1))
                nc.tensor.matmul(c_ps[:, s % 2, :], sel[:, NS + s, :], bct[:, u, :], start=True, stop=True).then_inc(c_filled, 1)

            def run(n, m, u, has_prev, has_next):
                nm = m + u
                for s in range(NS):
                    if s + B_AHEAD < NS:
                        spread_b(n, u, s + B_AHEAD)
                    elif has_next:
                        spread_b(n + 1, 1 - u, s + B_AHEAD - NS)
                    if s + 1 < NS:
                        spread_c(n, u, s + 1)
                    elif has_next:
                        spread_c(n + 1, 1 - u, 0)
                    for e in range(E2):
                        j = E2 * s + e
                        pe.wait_ge(products, J * n + j + 1)
                        if j == 0:
                            wait(pe, y_read, n)
                        nc.tensor.matmul(y_ps[:, e, :], ident[:, :], hc[:, j % NBUF, :], start=s == 0, stop=s == NS - 1).then_inc(summed, 1)
                        if has_next:
                            for g, i in PRE_AT.get(j, ()):
                                pre_step(g, i, n + 1, nm, 1 - u)
                        if has_prev and j in S_OUT:
                            out_step(n - 1, S_OUT.index(j), 8 * n + (11 if has_next else 8))

            PRE_AT = at_steps(S_PRE, [(g, i) for g, terms in enumerate((1, 1, TAPS, TAPS, E2, E2, 1, 1)) for i in range(terms)])
            PRE_AFTER = (0, 0, 1, 2, 4, 4, 5, 6)
            pe.wait_ge(consts, 16 * 11)
            pe.wait_ge(act_set_up, 2)
            pe.wait_ge(dve_set_up, TAPS)
            for j in sorted(PRE_AT):
                for g, i in PRE_AT[j]:
                    pre_step(g, i, 0, 0, 0)
            for s in range(B_AHEAD):
                spread_b(0, 0, s)
            spread_c(0, 0, 0)
            units(pe, run)
            for i in range(E2):
                out_step(UNITS - 1, i, 8 * UNITS)

        @block.scalar
        def _(act):
            act.wait_ge(consts, 16 * 11)
            nc.scalar.activation(a[:, :, :], a[:, :, :], ACT.Exp).then_inc(act_set_up, 1)
            nc.scalar.activation(sel[:, :, :].rearrange("p a b -> p (a b)"), h[0:96, 0:8, :].rearrange("p a b -> p (a b)"), ACT.Copy).then_inc(act_set_up, 1)

            def gates(n, u):
                wait(act, yz_ready, n - 1)
                for g in range(2):
                    act.wait_ge(pre_filled, 8 * n + g + 1)
                    nc.scalar.activation(zs[:, u, g, :], pre[:, g, :], ACT.Copy).then_inc(pre_used, 1)

            def silus(n, u):
                wait(act, y_read, n - 1)
                for g in range(2):
                    act.wait_ge(pre_filled, 8 * n + g + 3)
                    nc.scalar.activation(xc[:, u, g, :], pre[:, g, :], ACT.Silu, bias=mv[:, g:g + 1]).then_inc(pre_used, 1)
                act.wait_ge(pre_used, 8 * n + 2)
                nc.scalar.activation(zs[:, u], zs[:, u], ACT.Silu).then_inc(zs_ready, 1)

            def copy_dtr(n, u):
                act.wait_ge(pre_filled, 8 * n + 5)
                nc.scalar.activation(dtr[:, :], pre[0:RANK, 1, :], ACT.Copy).then_inc(pre_used, 1)

            def copy_bc(n, u):
                act.wait_ge(pre_filled, 8 * n + 6)
                nc.scalar.activation(bcf[:, :], pre[0:96, 0, :], ACT.Copy).then_inc(pre_used, 1)
                act.wait_ge(pre_used, 8 * n + 6)
                wait(act, b_copied, NS * n - NS)
                wait(act, c_filled, NS * n - NS)
                nc.scalar.activation(bct[:, u, :], bcf[:, :], ACT.Copy).then_inc(act_chain, 1)

            def copy_dt(n, u):
                for e in range(E2):
                    act.wait_ge(pre_filled, 8 * n + 7 + e)
                    nc.scalar.activation(v[:, e, :], pre[:, 1 - e, :], ACT.Identity, bias=mv[:, 2 + e:3 + e]).then_inc(pre_used, 1)

            def mid_part(n, u):
                act.wait_ge(bc_rest, n + 1)
                nc.scalar.activation(bct[0:64, u, :], bcr[:, :], ACT.Copy).then_inc(act_chain, 1)

            def softplus_exp(n, u):
                act.wait_ge(pre_used, 8 * n + 8)
                nc.scalar.activation(ea[:, :, :], v[:, :, :], ACT.Abs).then_inc(act_chain, 1)
                act.wait_ge(act_chain, 6 * n + 3)
                nc.scalar.activation(ea[:, :, :], ea[:, :, :], ACT.Exp, scale=-1.0).then_inc(act_chain, 1)

            def softplus_log(n, u):
                act.wait_ge(act_chain, 6 * n + 4)
                nc.scalar.activation(eb[:, :, :], ea[:, :, :], ACT.Identity, bias=1.0).then_inc(act_chain, 1)
                act.wait_ge(act_chain, 6 * n + 5)
                nc.scalar.activation(ec[:, :, :], eb[:, :, :], ACT.Ln).then_inc(act_chain, 1)

            def softplus_low(n, u):
                nc.scalar.activation(eb[:, :, :], eb[:, :, :], ACT.Identity, bias=-1.0).then_inc(log_parts, 1)

            def copy_b(n, s):
                act.wait_ge(b_filled, NS * n + s + 1)
                wait(act, inputs, J * n + E2 * (s - BBUF + 1))
                nc.scalar.activation(b_all[:, s % BBUF, :], b_ps[:, s % 2, :], ACT.Copy).then_inc(b_copied, 1)

            def run(n, m, u, has_prev, has_next):
                act.wait_ge(dt_ready, n + 1)
                for s in range(NS):
                    if s + B_COPY_AHEAD < NS:
                        copy_b(n, s + B_COPY_AHEAD)
                    elif has_next:
                        copy_b(n + 1, s + B_COPY_AHEAD - NS)
                    for e in range(E2):
                        j = E2 * s + e
                        wait(act, scanned, J * n + j - NBUF + 1)
                        nc.scalar.activation(da[:, j % NBUF, :], dt[:, u, e, :], ACT.Exp, scale=a[:, e, s:s + 1]).then_inc(decays, 1)
                        if has_next:
                            for step in ACT_AT.get(j, ()):
                                step(n + 1, 1 - u)

            ACT_AT = at_steps(S_ACT, (gates, silus, copy_dtr, copy_bc, mid_part, copy_dt, softplus_exp, softplus_log, softplus_low))
            act.wait_ge(dve_set_up, TAPS + 1)
            for j in sorted(ACT_AT):
                for step in ACT_AT[j]:
                    step(0, 0)
            for s in range(B_COPY_AHEAD):
                copy_b(0, s)
            units(act, run)

        @block.gpsimd
        def _(pool):
            def tail(n, u):
                pool.wait_ge(log_parts, n + 1)
                nc.gpsimd.tensor_tensor(ea[:, :, :], ea[:, :, :], eb[:, :, :], ALU.subtract).then_inc(pool_chain, 1)
                pool.wait_ge(pool_chain, n + 1)
                nc.gpsimd.tensor_tensor(ec[:, :, :], ec[:, :, :], ea[:, :, :], ALU.add).then_inc(softplus_tail, 1)

            def dt_times_x(n, u):
                pool.wait_ge(dt_ready, n + 1)
                nc.gpsimd.tensor_tensor(dtx[:, u], dt[:, u], xc[:, u], ALU.mult).then_inc(dtx_ready, 1)

            def run(n, m, u, has_prev, has_next):
                for s in range(NS):
                    pool.wait_ge(b_copied, NS * n + s + 1)
                    for e in range(E2):
                        j = E2 * s + e
                        wait(pool, scanned, J * n + j - NBUF + 1)
                        if j == 0:
                            pool.wait_ge(dtx_ready, n + 1)
                        nc.gpsimd.tensor_tensor(dbx[:, j % NBUF, :], dtx[:, u, e, :], b_all[:, s % BBUF, :], ALU.mult).then_inc(inputs, 1)
                        if has_next:
                            for step in POOL_AT.get(j, ()):
                                step(n + 1, 1 - u)

            POOL_AT = at_steps(S_POOL, (tail, dt_times_x))
            for j in sorted(POOL_AT):
                for step in POOL_AT[j]:
                    step(0, 0)
            units(pool, run)

        @block.vector
        def _(dve):
            dve.wait_ge(consts, 16 * 11)
            for tap in range(TAPS):
                nc.vector.tensor_tensor(wcv[:, tap, :], wcv[:, tap, :], win[:, 0:E2 * P], ALU.mult).then_inc(dve_set_up, 1)
            dve.wait_ge(act_set_up, 1)
            nc.vector.tensor_scalar(a[:, :, :], a[:, :, :], -1.0, None, ALU.mult).then_inc(dve_set_up, 1)
            nc.vector.memset(carry[:, :], 0.0).then_inc(dve_set_up, 1)
            dve.wait_ge(dve_set_up, TAPS + 2)

            def split_mid(n, u):
                dve.wait_ge(act_chain, 6 * n + 1)
                nc.vector.tensor_tensor(bcr[:, :], bcf[0:64, :], bct[0:64, u, :], ALU.subtract).then_inc(bc_rest, 1)

            def split_low(n, u):
                dve.wait_ge(act_chain, 6 * n + 2)
                nc.vector.tensor_tensor(bct[0:32, u, :], bcr[0:32, :], bct[0:32, u, :], ALU.subtract).then_inc(bct_ready, 1)

            def gate(n, u):
                dve.wait_ge(y_read, n + 1)
                dve.wait_ge(zs_ready, n + 1)
                nc.vector.tensor_tensor(yd[:, :, :], yd[:, :, :], zs[:, u], ALU.mult).then_inc(yz_ready, 1)

            def softplus_head(n, u):
                dve.wait_ge(softplus_tail, n + 1)
                nc.vector.scalar_tensor_tensor(dt[:, u].rearrange("p a b -> p (a b)"), v[:, :, :].rearrange("p a b -> p (a b)"), 0.0,
                                               ec[:, :, :].rearrange("p a b -> p (a b)"), ALU.max, ALU.add).then_inc(dt_ready, 1)

            def read_y(n, u):
                dve.wait_ge(summed, J * n + J)
                wait(dve, out_filled, n)
                for e in range(E2):
                    y = nc.vector.scalar_tensor_tensor(yd[:, e, :], xc[:, u, e, :], mv[:, 4 + e:5 + e], y_ps[:, e, :], ALU.mult, ALU.add)
                y.then_inc(y_read, 1)

            def output(n, u):
                dve.wait_ge(out_filled, n + 1)
                dve.wait_ge(skip_loaded, 16 * n + 16)
                wait(dve, out_stored, 16 * n)
                nc.vector.scalar_tensor_tensor(yo[:, :], xo[:, :], mv[:, 6:7], pre[:, 0, :], ALU.mult, ALU.add).then_inc(out_ready, 1)

            def product(n, j):
                s, e = divmod(j, E2)
                dve.wait_ge(scanned, J * n + j + 1)
                dve.wait_ge(c_filled, NS * n + s + 1)
                wait(dve, summed, J * n + j - NBUF + 1)
                nc.vector.tensor_tensor(hc[:, j % NBUF, :], h[:, j, :], c_ps[:, s % 2, :], ALU.mult).then_inc(products, 1)

            def run(n, m, u, has_prev, has_next):
                if has_prev:
                    dve.wait_ge(scanned, J * n)
                    nc.vector.tensor_tensor(carry[:, :], h[:, :, T - 1], keep[:, bass.ds(n, 1)].broadcast_to([P, J]), ALU.mult).then_inc(carried, 1)
                    dve.wait_ge(carried, n)
                for j in range(J):
                    dve.wait_ge(decays, J * n + j + 1)
                    dve.wait_ge(inputs, J * n + j + 1)
                    nc.vector.tensor_tensor_scan(h[:, j, :], da[:, j % NBUF, :], dbx[:, j % NBUF, :], carry[:, j:j + 1],
                                                 ALU.mult, ALU.add).then_inc(scanned, 1)
                    if j:
                        product(n, j - 1)
                    if has_prev:
                        if j == 1:
                            read_y(n - 1, 1 - u)
                        elif j == S_DVE_OUT:
                            output(n - 1, 1 - u)
                        elif j == 1 + S_GATE_AFTER:
                            gate(n - 1, 1 - u)
                    if has_next:
                        for step in DVE_AT.get(j, ()):
                            step(n + 1, 1 - u)
                product(n, J - 1)

            DVE_AT = at_steps(S_DVE, (split_mid, split_low, softplus_head))
            for j in sorted(DVE_AT):
                for step in DVE_AT[j]:
                    step(0, 0)
            units(dve, run)
            read_y(UNITS - 1, 1)
            gate(UNITS - 1, 1)
            output(UNITS - 1, 1)


def phase_project(nc, sem, ym, x, x2, stats_out, vectors, w_proj, ones_mat):
    x_in = x.rearrange("b (k p) h w -> p (b k) (h w)", p=P)
    y_in = ym.rearrange("p (r t) c -> p r (t c)", t=NT)
    with ExitStack() as ctx:
        sb = lambda n, s, d: ctx.enter_context(nc.sbuf_tensor(n, s, d))
        pb = lambda n, s, d: ctx.enter_context(nc.psum_tensor(n, s, d))
        ones = sb("p_ones", [P, P], F32)
        vec = sb("p_vec", [P, 3, K], F32)
        w = sb("p_w", [P, K, C], F32)
        eps = sb("p_eps", [P, 1], F32)
        y = sb("p_y", [P, 4, K, T], F32)
        yn = sb("p_yn", [P, 2, K, T], F32)
        res = sb("p_res", [P, 2, K, T], F32)
        stats = sb("p_stats", [P, SEQ, NT, 6], F32)
        out_ps = pb("p_out_ps", [P, 4, T], F32)
        consts = sem("p_consts")
        eps_set = sem("p_eps_set")
        y_loaded = [sem(f"p_y_loaded{i}") for i in range(4)]
        x_loaded = [sem("p_x_loaded0"), sem("p_x_loaded1")]
        res_free = sem("p_res_free")
        yn_ready = sem("p_yn_ready")
        bank_filled = sem("p_bank_filled")
        bank_read = sem("p_bank_read")
        stats_done = sem("p_stats_done")
        stored = sem("p_stored")
        ln = LayerNorm(nc, "p_ln", sb, pb, sem, y, ones)
        block = ctx.enter_context(nc.Block())
        CHUNKS = B * NT
        PAIRS_B = NT // 2

        def pairs(eng, run):
            with eng.Fori(0, B - 1) as b:
                for i in range(PAIRS_B):
                    run(b * PAIRS_B + i, b, 2 * i, i % 2, True, True)
            for i in range(PAIRS_B):
                run((B - 1) * PAIRS_B + i, B - 1, 2 * i, i % 2, i + 1 < PAIRS_B, i + 2 < PAIRS_B)

        @block.sync
        def _(sp):
            sp.dma_start(ones[:, :], ones_mat).then_inc(consts, 16)
            sp.dma_start(vec[:, :, :], vectors[:, NORM_G:PROJ_B + 1, :]).then_inc(consts, 16)
            sp.dma_start(w[:, :, :], w_proj).then_inc(consts, 16)
            sp.sem_inc(yn_ready, 4)

            def load_y(p, b, t, q):
                for u in range(2):
                    sp.wait_ge(yn_ready, 2 * p + u + 1)
                    sp.dma_start(y[:, 2 * q + u], y_in[:, bass.ds(b * K, K), bass.ds((t + u) * T, T)]).then_inc(y_loaded[2 * q + u], 16)

            def run(p, b, t, q, has_1, has_2):
                if has_2:
                    wraps = t + 4 >= NT
                    load_y(p + 2, b + 1 if wraps else b, (t + 4) % NT, q)
                for u in range(2):
                    sp.wait_ge(res_free, 2 * p + u + 1)
                    sp.dma_start(res[:, u], x_in[:, bass.ds(b * K, K), bass.ds((t + u) * T, T)]).then_inc(x_loaded[u], 16)

            load_y(0, 0, 0, 0)
            load_y(1, 0, 2, 1)
            pairs(sp, run)

        @block.gpsimd
        def _(pool):
            nc.gpsimd.memset(eps[:, :], LN_EPS).then_inc(eps_set, 1)
            pool.sem_inc(res_free, 2)
            with pool.Fori(0, B) as b:
                with pool.Fori(0, NT // 2) as t2:
                    for u in range(2):
                        n = b * NT + t2 * 2 + u
                        pool.wait_ge(stats_done, n + 1)
                        pool.dma_start(x2[:, bass.ds(b * K, K), bass.ds((t2 * 2 + u) * T, T)], res[:, u]).then_inc(stored, 16)
                        pool.wait_ge(stored, 16 * n + 16)
                        pool.sem_inc(res_free, 1)
            pool.dma_start(stats_out, stats[:, :, :, :]).then_inc(stored, 16)
            pool.wait_ge(stored, 16 * CHUNKS + 16)

        @block.tensor
        def _(pe):
            def mean(p, q):
                for u in range(2):
                    wait(pe, ln.std_ready, 2 * p + u - 1)
                    ln.pe_mean(pe, u, 2 * p + u, 2 * q + u)

            def variance(p):
                for u in range(2):
                    ln.pe_var(pe, u, 2 * p + u)

            def project(c, u):
                pe.wait_ge(yn_ready, c + 5)
                for o in range(K):
                    pe.wait_ge(bank_read, 4 * c + o + 1)
                    for k in range(K):
                        mm = nc.tensor.matmul(out_ps[:, o, :], w[:, k, o * P:(o + 1) * P], yn[:, u, k, :], start=k == 0, stop=k == K - 1)
                    mm.then_inc(bank_filled, 1)

            def run(p, b, t, q, has_1, has_2):
                project(2 * p, 0)
                if has_1:
                    variance(p + 1)
                project(2 * p + 1, 1)
                if has_2:
                    mean(p + 2, q)

            pe.wait_ge(consts, 48)
            mean(0, 0)
            variance(0)
            mean(1, 1)
            pairs(pe, run)

        @block.scalar
        def _(act):
            def pass_input(m, q):
                for u in range(2):
                    act.wait_ge(y_loaded[2 * q + u], 16 * m + 16)
                    act.sem_inc(ln.input_ready, 1)

            def square(p, q):
                for u in range(2):
                    ln.act_square(act, u, 2 * p + u, 2 * q + u)

            def normed(p, q):
                for u in range(2):
                    ln.act_std(act, u, 2 * p + u, eps[:, 0:1])
                for u in range(2):
                    c = 2 * p + u
                    act.wait_ge(ln.scaled, c + 1)
                    wait(act, bank_filled, 4 * c - 4)
                    for k in range(K):
                        o = nc.scalar.activation(yn[:, u, k, :], y[:, 2 * q + u, k, :], ACT.Identity, scale=vec[:, 0, k:k + 1], bias=vec[:, 1, k:k + 1])
                    o.then_inc(yn_ready, 1)

            def run(p, b, t, q, has_1, has_2):
                if has_2:
                    pass_input(b * (PAIRS_B // 2) + t // 4 + 1, q)
                if has_1:
                    normed(p + 1, 1 - q)
                if has_2:
                    square(p + 2, q)

            act.sem_inc(bank_read, 4)
            act.wait_ge(eps_set, 1)
            act.wait_ge(consts, 48)
            pass_input(0, 0)
            pass_input(0, 1)
            square(0, 0)
            normed(0, 0)
            square(1, 1)
            pairs(act, run)

        @block.vector
        def _(dve):
            def centre(p, q):
                for u in range(2):
                    ln.dve_centre(dve, u, 2 * p + u, 2 * q + u)

            def scale(p, q):
                for u in range(2):
                    ln.dve_scale(dve, u, 2 * p + u, 2 * q + u)

            def add_residual(p, b, t, u):
                c = 2 * p + u
                dve.wait_ge(x_loaded[u], 16 * p + 16)
                for k in range(K):
                    dve.wait_ge(bank_filled, 4 * c + k + 1)
                    nc.vector.scalar_tensor_tensor(res[:, u, k, :], out_ps[:, k, :], vec[:, 2, k:k + 1], res[:, u, k, :],
                                                   ALU.add, ALU.add).then_inc(bank_read, 1)
                dve.wait_ge(bank_read, 4 * c + 8)
                for k in range(K):
                    bn = nc.vector.bn_stats(stats[:, bass.ds(b * K + k, 1), t + u:t + u + 1, :].rearrange("p o n s -> p (o n s)"), res[:, u, k, :])
                bn.then_inc(stats_done, 1)

            def run(p, b, t, q, has_1, has_2):
                add_residual(p, b, t, 0)
                if has_1:
                    scale(p + 1, 1 - q)
                add_residual(p, b, t, 1)
                if has_2:
                    centre(p + 2, q)

            centre(0, 0)
            scale(0, 0)
            centre(1, 1)
            pairs(dve, run)


G = 16
PTS = 9
NOFF = G * PTS * 2
NMASK = G * PTS
ROWS = T // IMG
TT = T // P
PADI = IMG + 2
NCOL = NOFF + NMASK
REACH = 3
PADW = IMG + 2 * REACH


def phase_offsets(nc, sem, x2, stats_in, xproj, offsets, masks, peak, vectors, w_in, dw_w, w_om, b_om, ones_mat, group_mat):
    with ExitStack() as ctx:
        sb = lambda n, s, d: ctx.enter_context(nc.sbuf_tensor(n, s, d))
        pb = lambda n, s, d: ctx.enter_context(nc.psum_tensor(n, s, d))
        ones = sb("o_ones", [P, P], F32)
        gavg = sb("o_gavg", [P, P], F32)
        vec = sb("o_vec", [P, 4, K], F32)
        w = sb("o_w", [P, K, C], F32)
        wom = sb("o_wom", [P, K, NCOL], F32)
        bom = sb("o_bom", [1, NCOL], F32)
        row = sb("o_row", [1, P], F32)
        dw = sb("o_dw", [P, K, 9], F32)
        eps = sb("o_eps", [P, 1], F32)
        stats = sb("o_stats", [P, SEQ, NT, 6], F32)
        aff_b = sb("o_aff_b", [P, 2, K], F32)
        raw = sb("o_raw", [P, 2, K, T], F32)
        g = sb("o_g", [P, K, PADI, PADI], F32)
        d = sb("o_d", [P, 4, K, T], F32)
        xp = sb("o_xp", [P, K, ROWS, PADW], F32)
        zero = sb("o_zero", [P, K, REACH * PADW], F32)
        om = sb("o_om", [P, 2, TT, NCOL], F32)
        small = sb("o_small", [P, 2, TT, G], F32)
        peaks = sb("o_peaks", [P, B * NT], F32)
        proj_ps = pb("o_proj_ps", [P, 2, T], F32)
        om_ps = pb("o_om_ps", [P, 2, T], F32)
        consts = sem("o_consts")
        filled = sem("o_filled")
        rows_stored = sem("o_rows_stored")
        affine_picked = sem("o_affine_picked")
        raw_loaded = [sem("o_raw_loaded0"), sem("o_raw_loaded1")]
        normed = sem("o_normed")
        convolved = sem("o_convolved")
        geluded = sem("o_geluded")
        proj_filled = sem("o_proj_filled")
        proj_read = sem("o_proj_read")
        xp_stored = sem("o_xp_stored")
        om_filled = sem("o_om_filled")
        om_copied = sem("o_om_copied")
        less_max = sem("o_less_max")
        exp_done = sem("o_exp_done")
        om_ready = sem("o_om_ready")
        om_stored = [sem("o_om_stored0"), sem("o_om_stored1")]
        peak_stored = sem("o_peak_stored")
        ln = LayerNorm(nc, "o_ln", sb, pb, sem, d, ones)
        block = ctx.enter_context(nc.Block())
        aff, gn_dve, gn_pe, gn_act = finish_group_norm(
            nc, sb, pb, sem, block, "o_gn", stats, gavg, (consts, 16 * 8), eps)
        CH = B * NT

        def pairs(eng, run, image=None):
            half = NT // 2
            if image:
                image(0)
            for i in range(half):
                run(i, 0, 2 * i, i % 2, i >= 1, i >= 2)
            with eng.Fori(1, B) as b:
                if image:
                    image(b)
                with eng.Fori(0, half // 2) as i:
                    for q in range(2):
                        run(b * half + 2 * i + q, b, 4 * i + 2 * q, q, True, True)

        @block.sync
        def _(sp):
            for dst, src in ((ones[:, :], ones_mat), (gavg[:, :], group_mat), (vec[:, :, :], vectors[:, DW_B:IN_B + 1, :]),
                             (w[:, :, :], w_in), (wom[:, :, :], w_om), (bom[:, :], b_om.rearrange("(o n) -> o n", o=1)),
                             (dw[:, :, :], dw_w), (stats[:, :, :, :], stats_in)):
                sp.dma_start(dst, src).then_inc(consts, 16)
            sp.sem_inc(normed, 2)
            with sp.Fori(0, B) as b:
                with sp.Fori(0, NT // 2) as t2:
                    for u in range(2):
                        sp.wait_ge(normed, b * NT + t2 * 2 + u + 1)
                        sp.dma_start(raw[:, u], x2[:, bass.ds(b * K, K), bass.ds((t2 * 2 + u) * T, T)]).then_inc(raw_loaded[u], 16)

        @block.gpsimd
        def _(pool):
            nc.gpsimd.memset(eps[:, :], LN_EPS).then_inc(filled, 1)
            nc.gpsimd.memset(row[:, :], 1.0).then_inc(filled, 1)
            nc.gpsimd.memset(g[:, :, :, :].rearrange("p k a b -> p (k a b)"), 0.0).then_inc(filled, 1)
            nc.gpsimd.memset(xp[:, :, :, :].rearrange("p k a b -> p (k a b)"), 0.0).then_inc(filled, 1)
            nc.gpsimd.memset(zero[:, :, :].rearrange("p k a -> p (k a)"), 0.0).then_inc(filled, 1)
            pool.wait_ge(filled, 5)
            for b in range(B):
                for r in (0, PADW - REACH):
                    pool.dma_start(xproj[:, b * K:(b + 1) * K, r * PADW:(r + REACH) * PADW], zero[:, :, :]).then_inc(rows_stored, 16)
            with pool.Fori(0, CH // 2) as i:
                for u in range(2):
                    n = 2 * i + u
                    pool.wait_ge(om_ready, 3 * n + 3)
                    pool.dma_start(offsets[:, bass.ds(n * TT, TT), :], om[:, u, :, 0:NOFF]).then_inc(om_stored[u], 16)
                    pool.dma_start(masks[:, bass.ds(n * TT, TT), :], om[:, u, :, NOFF:NCOL]).then_inc(om_stored[u], 16)
            pool.dma_start(peak, peaks[:, :]).then_inc(peak_stored, 16)
            for u in range(2):
                pool.wait_ge(om_stored[u], 16 * CH)
            pool.wait_ge(peak_stored, 16)
            pool.wait_ge(rows_stored, 16 * 2 * B)

        @block.tensor
        def _(pe):
            def project_in(c, o, b, t, u):
                if o == 0:
                    pe.wait_ge(normed, c + 3)
                wait(pe, proj_read, 4 * c + o - 1)
                for k in range(K):
                    mm = nc.tensor.matmul(proj_ps[:, o % 2, :], w[:, k, o * P:(o + 1) * P],
                                          g[:, k, bass.ds(t * ROWS + 1, ROWS), 1:1 + IMG], start=k == 0, stop=k == K - 1)
                mm.then_inc(proj_filled, 1)

            def project_offsets(c, x):
                pe.wait_ge(geluded, c + 1)
                for t in range(TT):
                    wait(pe, om_copied, 4 * c + t - 1)
                    nc.tensor.matmul(om_ps[:, t % 2, 0:NCOL], row[:, :], bom[:, :], start=True, stop=False)
                    for k in range(K):
                        mm = nc.tensor.matmul(om_ps[:, t % 2, 0:NCOL], d[:, x, k, t * P:(t + 1) * P], wom[:, k, :], start=False, stop=k == K - 1)
                    mm.then_inc(om_filled, 1)

            def run(p, b, t, q, lag_1, lag_2):
                if lag_1:
                    for u in range(2):
                        ln.pe_mean(pe, u, 2 * p - 2 + u, 2 * (1 - q) + u)
                for u in range(2):
                    if t is not None:
                        for o in range(K):
                            project_in(2 * p + u, o, b, t + u, u)
                    if lag_1 and u == 0:
                        for v in range(2):
                            ln.pe_var(pe, v, 2 * p - 2 + v)
                if lag_1:
                    for u in range(2):
                        project_offsets(2 * p - 2 + u, 2 * (1 - q) + u)

            pe.wait_ge(consts, 16 * 8)
            pe.wait_ge(filled, 2)
            gn_pe(pe)
            pairs(pe, run)
            run(CH // 2, None, None, 0, True, True)

        @block.scalar
        def _(act):
            def copy_projection(c, o, t):
                act.wait_ge(proj_filled, 4 * c + o + 1)
                if o == 0:
                    wait(act, xp_stored, 16 * c)
                nc.scalar.activation(xp[:, o, :, REACH:REACH + IMG], proj_ps[:, o % 2, :].rearrange("p (r c) -> p r c", c=IMG), ACT.Identity,
                                     bias=vec[:, 3, o:o + 1]).then_inc(proj_read, 1)

            def store_projection(c, b, t):
                act.wait_ge(proj_read, 4 * c + 4)
                act.dma_start(xproj[:, bass.ds(b * K, K), bass.ds((t * ROWS + REACH) * PADW, ROWS * PADW)],
                              xp[:, :, :, :].rearrange("p k a b -> p k (a b)")).then_inc(xp_stored, 16)

            def gelu(c, x):
                act.wait_ge(ln.scaled, c + 1)
                for k in range(K):
                    a = nc.scalar.activation(d[:, x, k, :], d[:, x, k, :], ACT.Gelu, scale=vec[:, 1, k:k + 1], bias=vec[:, 2, k:k + 1])
                a.then_inc(geluded, 1)

            def copy_offsets(c, m, u):
                wait(act, om_stored[u], 32 * m)
                for t in range(TT):
                    act.wait_ge(om_filled, 4 * c + t + 1)
                    nc.scalar.activation(om[:, u, t, :], om_ps[:, t % 2, 0:NCOL], ACT.Copy).then_inc(om_copied, 1)

            def exponent(c, u):
                act.wait_ge(less_max, 3 * c + 2)
                nc.scalar.activation(om[:, u, :, NOFF:NCOL], om[:, u, :, NOFF:NCOL], ACT.Exp).then_inc(exp_done, 1)

            def run(p, b, t, q, lag_1, lag_2):
                for u in range(2):
                    for o in range(K):
                        if t is not None:
                            copy_projection(2 * p + u, o, t + u)
                        if lag_1 and (u, o) == (0, 1):
                            for v in range(2):
                                ln.act_square(act, v, 2 * p - 2 + v, 2 * (1 - q) + v)
                    if t is not None:
                        store_projection(2 * p + u, b, t + u)
                    if lag_1 and u == 0:
                        for v in range(2):
                            ln.act_std(act, v, 2 * p - 2 + v, eps[:, 0:1])
                if lag_1:
                    for u in range(2):
                        gelu(2 * p - 2 + u, 2 * (1 - q) + u)
                    for u in range(2):
                        copy_offsets(2 * p - 2 + u, p - 1, u)
                    for u in range(2):
                        exponent(2 * p - 2 + u, u)

            act.wait_ge(filled, 2)
            gn_act(act)
            act.wait_ge(filled, 4)
            act.wait_ge(consts, 16 * 8)
            pairs(act, run)
            run(CH // 2, None, None, 0, True, True)
            act.wait_ge(xp_stored, 16 * CH)

        @block.vector
        def _(dve):
            per_point = lambda s: s.unsqueeze(3).broadcast_to([P, TT, G, PTS])

            def logits(u):
                return om[:, u, :, NOFF:NCOL].rearrange("p t (g q) -> p t g q", q=PTS)

            def norm_image(b):
                wait(dve, proj_filled, 4 * NT * b)
                nc.vector.tensor_scalar(aff_b[:, :, :], aff[:, :, bass.ds(b * K, K)], 1.0, None, ALU.mult).then_inc(affine_picked, 1)
                with dve.Fori(0, NT // 2) as t2:
                    for u in range(2):
                        dve.wait_ge(affine_picked, b + 1)
                        dve.wait_ge(raw_loaded[u], 16 * (b * (NT // 2) + t2) + 16)
                        for k in range(K):
                            a = nc.vector.tensor_scalar(g[:, k, bass.ds((t2 * 2 + u) * ROWS + 1, ROWS), 1:1 + IMG],
                                                        raw[:, u, k, :].rearrange("p (r c) -> p r c", c=IMG),
                                                        aff_b[:, 0, k:k + 1], aff_b[:, 1, k:k + 1], ALU.mult, ALU.add)
                        a.then_inc(normed, 1)

            def convolve(c, k, b, t, x, reused):
                if k == 0:
                    dve.wait_ge(normed, (b + 1) * NT + 2)
                    if reused:
                        dve.wait_ge(om_filled, 4 * c - 12)
                for tap in range(9):
                    r, s = divmod(tap, 3)
                    src = g[:, k, bass.ds(t * ROWS + r, ROWS), s:s + IMG]
                    dst = d[:, x, k, :].rearrange("p (r c) -> p r c", c=IMG)
                    if tap == 0:
                        i = nc.vector.tensor_scalar(dst, src, dw[:, k, 0:1], vec[:, 0, k:k + 1], ALU.mult, ALU.add)
                    else:
                        i = nc.vector.scalar_tensor_tensor(dst, src, dw[:, k, tap:tap + 1], dst, ALU.mult, ALU.add)
                    i.then_inc(convolved, 1)
                    dve.wait_ge(convolved, 36 * c + 9 * k + tap + 1)
                if k == K - 1:
                    dve.sem_inc(ln.input_ready, 1)

            def take_maximum(c, u):
                dve.wait_ge(om_copied, 4 * c + 4)
                wait(dve, less_max, 3 * c)
                nc.vector.tensor_reduce(small[:, 0], logits(u), AX.X, ALU.max).then_inc(less_max, 1)
                dve.wait_ge(less_max, 3 * c + 1)
                nc.vector.tensor_tensor(logits(u), logits(u), per_point(small[:, 0]), ALU.subtract).then_inc(less_max, 1)
                nc.vector.tensor_reduce(peaks[:, bass.ds(c, 1)], om[:, u, :, 0:NOFF], AX.XY, ALU.max, apply_absolute_value=True).then_inc(less_max, 1)

            def divide(c, u):
                dve.wait_ge(exp_done, c + 1)
                wait(dve, om_ready, 3 * c)
                nc.vector.tensor_reduce(small[:, 1], logits(u), AX.X, ALU.add).then_inc(om_ready, 1)
                dve.wait_ge(om_ready, 3 * c + 1)
                nc.vector.reciprocal(small[:, 1], small[:, 1]).then_inc(om_ready, 1)
                dve.wait_ge(om_ready, 3 * c + 2)
                nc.vector.tensor_tensor(logits(u), logits(u), per_point(small[:, 1]), ALU.mult).then_inc(om_ready, 1)

            def run(p, b, t, q, lag_1, lag_2):
                for u in range(2):
                    for k in range(K):
                        if t is not None:
                            convolve(2 * p + u, k, b, t + u, 2 * q + u, lag_2)
                        if lag_2 and (u, k) == (0, 0):
                            take_maximum(2 * p - 3, 1)
                        if lag_1 and (u, k) == (0, 1):
                            for v in range(2):
                                ln.dve_centre(dve, v, 2 * p - 2 + v, 2 * (1 - q) + v)
                        if lag_2 and (u, k) == (0, 2):
                            for v in range(2):
                                divide(2 * p - 4 + v, v)
                        if lag_1 and (u, k) == (1, 1):
                            for v in range(2):
                                ln.dve_scale(dve, v, 2 * p - 2 + v, 2 * (1 - q) + v)
                if lag_1:
                    take_maximum(2 * p - 2, 0)

            gn_dve(dve)
            dve.wait_ge(filled, 3)
            pairs(dve, run, norm_image)
            run(CH // 2, None, None, 0, True, True)
            take_maximum(CH - 1, 1)
            for v in range(2):
                divide(CH - 2 + v, v)


WIN = 2 * REACH + 1
D = WIN * WIN
HATS = 5
PARTS = 3
GK = G // K
ROWD = PARTS * GK
PER_BLOCK = 10
BLOCKS = -(-D // PER_BLOCK)
PROD_BUF = 2
POOL_BUF = 4
PAIRS = (D + 1) // 2


def phase_sample(nc, sem, x2, xproj, offsets, masks, out, vectors, w_out, sel_tab, ident_mat):
    with ExitStack() as ctx:
        sb = lambda n, s, d: ctx.enter_context(nc.sbuf_tensor(n, s, d))
        pb = lambda n, s, d: ctx.enter_context(nc.psum_tensor(n, s, d))
        vec = sb("s_vec", [P, 1, K], F32)
        w = sb("s_w", [P, K, C], F32)
        sel = sb("s_sel", [PER_BLOCK * ROWD, PER_BLOCK, P], BF16)
        ident = sb("s_ident", [P, P], F32)
        identb = sb("s_identb", [P, P], BF16)
        img = sb("s_img", [P, 2, K, (ROWS + 2 * REACH) * PADW], F32)
        off = sb("s_off", [P, TT, NOFF], F32)
        msk = sb("s_msk", [P, TT, NMASK], F32)
        hx = sb("s_hx", [P, TT * G, PTS, HATS], F32)
        hy = sb("s_hy", [P, TT * G, PTS, HATS], F32)
        outer = sb("s_outer", [P, 2, TT * G, HATS, HATS], F32)
        wts = sb("s_wts", [P, TT * G, WIN, WIN], F32)
        wtp = sb("s_wtp", [P, TT, K, D * ROWD], BF16)
        wtt = sb("s_wtt", [PER_BLOCK * ROWD, K, BLOCKS, T], BF16)
        dist = sb("s_dist", [P, HATS], F32)
        prod = sb("s_prod", [P, PROD_BUF, 2, T], F32)
        prod_pool = sb("s_prod_pool", [P, POOL_BUF, 2, T], F32)
        sums_pool = sb("s_sums_pool", [P, 2, 2, T], F32)
        dcn = sb("s_dcn", [P, K, T], F32)
        res = sb("s_res", [P, K, T], F32)
        spread = pb("s_spread", [P, 2, 2, T], F32)
        acc = pb("s_acc", [P, 2, T], F32)
        tps = pb("s_tps", [P, 2 * T], BF16)
        out_ps = pb("s_out_ps", [P, T], F32)
        consts = sem("s_consts")
        sel_ready = sem("s_sel_ready")
        img_loaded = [sem("s_img_loaded0"), sem("s_img_loaded1")]
        off_loaded = sem("s_off_loaded")
        res_loaded = sem("s_res_loaded")
        stored = sem("s_stored")
        dist_ready = sem("s_dist_ready")
        hat_step = sem("s_hat_step")
        masked = sem("s_masked")
        outer_ready = sem("s_outer_ready")
        added = sem("s_added")
        part_cast = sem("s_part_cast")
        part_left = sem("s_part_left")
        transposed = sem("s_transposed")
        wtt_ready = sem("s_wtt_ready")
        spread_ready = sem("s_spread_ready")
        multiplied = sem("s_multiplied")
        pe_summed = sem("s_pe_summed")
        last_summed = sem("s_last_summed")
        pool_summed = sem("s_pool_summed")
        acc_read = sem("s_acc_read")
        out_filled = sem("s_out_filled")
        out_ready = sem("s_out_ready")
        block = ctx.enter_context(nc.Block())
        CH = B * NT
        NB = K * BLOCKS
        NP = K * PAIRS
        POOL_PAIRS = [p for p in range(PAIRS - 1) if p % 2 == 1]
        PE_PAIRS = [p for p in range(PAIRS) if p not in POOL_PAIRS]
        ADDS = len(POOL_PAIRS) - 1
        LAST_SUM_AT = 3
        OUT_AT = [5 + 3 * t // 2 for t in range(K * K)]
        OUT_DONE_AT = [OUT_AT[K * o + K - 1] + 1 for o in range(K)]
        LEAVE_AT = [2 * q for q in range(2 * K)]
        MASKED_AT = 12
        OUTER_AT = [18 + 5 * q for q in range(PTS)]
        CLEAR_AT = 20
        ADD_AT = [26 + 5 * q for q in range(PTS)]

        def pool_number(n, c):
            return K * ADDS * n + c + 1

        def units(eng, run):
            run(0, 0, False, True, True)
            run(1, 1, True, True, True)
            with eng.Fori(1, CH // 2 - 1) as i:
                run(2 * i, 0, True, True, True)
                run(2 * i + 1, 1, True, True, True)
            run(CH - 2, 0, True, True, False)
            run(CH - 1, 1, True, False, False)

        def block_rows(blk):
            return min(PER_BLOCK, D - blk * PER_BLOCK) * ROWD

        def part_view(i, k):
            return wtp[:, :, k, :].rearrange("p t (d q g) -> p t d q g", q=PARTS, g=GK)[:, :, :, i, :]

        def weight_view(k):
            return wts[:, :, :, :].rearrange("p (t k g) y x -> p k t (y x) g", k=K, g=GK)[:, k]

        @block.sync
        def _(sp):
            sel_f = wts[0:PER_BLOCK * ROWD, 0:27, :, :].rearrange("p a b c -> p (a b c)")[:, 0:PER_BLOCK * P]
            for dst, src in ((vec[:, :, :], vectors[:, OUT_B:OUT_B + 1, :]), (w[:, :, :], w_out), (sel_f, sel_tab), (ident[:, :], ident_mat)):
                sp.dma_start(dst, src).then_inc(consts, 16)

            def load_image(n, u):
                sp.dma_start(img[:, u], xproj[:, bass.ds((n // NT) * K, K), bass.ds((n % NT) * (ROWS * PADW), (ROWS + 2 * REACH) * PADW)]).then_inc(img_loaded[u], 16)

            def load_offsets(n):
                sp.dma_start(off[:, :, :], offsets[:, bass.ds(n * TT, TT), :]).then_inc(off_loaded, 16)
                sp.dma_start(msk[:, :, :], masks[:, bass.ds(n * TT, TT), :]).then_inc(off_loaded, 16)

            def run(n, u, has_prev, has_1, has_2):
                if has_1:
                    wait(sp, multiplied, NP * n)
                    load_image(n + 1, 1 - u)
                if has_2:
                    sp.wait_ge(masked, n + 2)
                    load_offsets(n + 2)
                if has_prev:
                    sp.wait_ge(out_ready, K * n)
                    sp.dma_start(outv[:, bass.ds(((n - 1) // NT) * K, K), bass.ds(((n - 1) % NT) * T, T)], res[:, :, :]).then_inc(stored, 16)
                    sp.wait_ge(stored, 16 * n)
                sp.dma_start(res[:, :, :], x2[:, bass.ds((n // NT) * K, K), bass.ds((n % NT) * T, T)]).then_inc(res_loaded, 16)

            outv = out.rearrange("b (k p) h w -> p (b k) (h w)", p=P)
            load_image(0, 0)
            load_offsets(0)
            sp.wait_ge(masked, 1)
            load_offsets(1)
            units(sp, run)
            sp.wait_ge(out_ready, K * CH)
            sp.dma_start(outv[:, SEQ - K:SEQ, HW - T:HW], res[:, :, :]).then_inc(stored, 16)
            sp.wait_ge(stored, 16 * CH)

        @block.scalar
        def _(act):
            act.wait_ge(consts, 64)
            sel_f = wts[0:PER_BLOCK * ROWD, 0:27, :, :].rearrange("p a b c -> p (a b c)")[:, 0:PER_BLOCK * P]
            nc.scalar.activation(sel[:, :, :].rearrange("p a b -> p (a b)"), sel_f, ACT.Copy).then_inc(sel_ready, 1)
            nc.scalar.activation(identb[:, :], ident[:, :], ACT.Copy).then_inc(sel_ready, 1)

            def hats(n):
                act.wait_ge(off_loaded, 32 * n + 32)
                wait(act, outer_ready, PTS * n)
                o = off[:, :, :].rearrange("p t (q c) -> p (t q) c", c=2)
                for c, dst in ((0, hx), (1, hy)):
                    for r in range(HATS):
                        a = nc.scalar.activation(dst[:, :, :, r].rearrange("p a b -> p (a b)"), o[:, :, c], ACT.Abs, bias=dist[:, r:r + 1])
                a.then_inc(hat_step, 1)
                act.wait_ge(hat_step, 2 * n + 1)
                for dst in (hx, hy):
                    d = dst[:, :, :, :].rearrange("p a b c -> p (a b c)")
                    a = nc.scalar.activation(d, d, ACT.Relu, scale=-1.0, bias=1.0)
                a.then_inc(hat_step, 1)

            def cast_part(n, i, k):
                if i > 0:
                    act.wait_ge(part_left, 2 * K * n + 2 * k + 1)
                elif k == 0:
                    act.wait_ge(added, 10 * n + 10)
                    wait(act, transposed, NB * n)
                nc.scalar.activation(part_view(i, k), weight_view(k), ACT.Copy).then_inc(part_cast, 1)

            def copy_block(n, i):
                k, blk = divmod(i, BLOCKS)
                rows = block_rows(blk)
                act.wait_ge(transposed, NB * n + i + 1)
                nc.scalar.activation(wtt[0:rows, k, blk, :], tps[0:rows, 0:T], ACT.Copy).then_inc(wtt_ready, 1)

            def copy_sum(n, k):
                act.wait_ge(last_summed, K * n + k + 1)
                wait(act, out_filled, K * n)
                nc.scalar.activation(dcn[:, k, :], acc[:, k % 2, :], ACT.Copy).then_inc(acc_read, 1)

            def run(n, u, has_prev, has_1, has_2):
                if has_1:
                    for k in range(K):
                        cast_part(n + 1, 0, k)
                    cast_part(n + 1, 1, 0)
                    cast_part(n + 1, 1, 1)
                for k in range(K):
                    for blk in range(BLOCKS):
                        if has_1:
                            copy_block(n + 1, k * BLOCKS + blk)
                        if blk == 0:
                            if k > 0:
                                copy_sum(n, k - 1)
                            elif has_prev:
                                copy_sum(n - 1, K - 1)
                        if has_1 and k == 0 and blk < K - 2:
                            cast_part(n + 1, 1, blk + 2)
                        if has_2 and (k, blk) == (0, 0):
                            hats(n + 2)

            act.wait_ge(dist_ready, HATS)
            hats(0)
            for i in range(2):
                for k in range(K):
                    cast_part(0, i, k)
            for i in range(NB):
                copy_block(0, i)
            hats(1)
            units(act, run)
            copy_sum(CH - 1, K - 1)

        @block.gpsimd
        def _(pool):
            for r in range(HATS):
                nc.gpsimd.memset(dist[:, r:r + 1], float(HATS // 2 - r)).then_inc(dist_ready, 1)

            def masked_hats(n):
                pool.wait_ge(hat_step, 2 * n + 2)
                nc.gpsimd.tensor_tensor(hy[:, :, :, :].rearrange("p a b c -> p (a b) c"), hy[:, :, :, :].rearrange("p a b c -> p (a b) c"),
                                        msk[:, :, :].rearrange("p a b -> p (a b)").unsqueeze(2).broadcast_to([P, TT * G * PTS, HATS]),
                                        ALU.mult).then_inc(masked, 1)
                pool.wait_ge(masked, n + 1)

            def outer_product(n, q):
                wait(pool, added, 10 * n + q)
                nc.gpsimd.tensor_tensor(outer[:, q % 2], hy[:, :, q, :].unsqueeze(3).broadcast_to([P, TT * G, HATS, HATS]),
                                        hx[:, :, q, :].unsqueeze(2).broadcast_to([P, TT * G, HATS, HATS]), ALU.mult).then_inc(outer_ready, 1)

            def weights(n):
                masked_hats(n)
                for q in range(PTS):
                    outer_product(n, q)

            def add_pair(n, k, c):
                pool.wait_ge(multiplied, NP * n + PAIRS * k + POOL_PAIRS[c + 1] + 1)
                wait(pool, pool_summed, pool_number(n, ADDS * k + c - 1))
                s = sums_pool[:, k % 2]
                nc.gpsimd.tensor_tensor(s, s, prod_pool[:, (ADDS * k + c) % POOL_BUF], ALU.add).then_inc(pool_summed, 1)

            def run(n, u, has_prev, has_1, has_2):
                for i in range(NP):
                    k, pair = divmod(i, PAIRS)
                    if pair in POOL_PAIRS[1:]:
                        add_pair(n, k, POOL_PAIRS.index(pair) - 1)
                    if has_2 and i == MASKED_AT:
                        masked_hats(n + 2)
                    if has_2 and i in OUTER_AT:
                        outer_product(n + 2, OUTER_AT.index(i))

            weights(0)
            weights(1)
            units(pool, run)

        @block.vector
        def _(dve):
            def clear_window(n):
                wait(dve, part_left, 2 * K * n)
                nc.vector.memset(wts[:, :, :, :].rearrange("p a b c -> p (a b c)"), 0.0).then_inc(added, 1)

            def add_point(n, q):
                ix, iy = divmod(q, 3)
                dve.wait_ge(outer_ready, PTS * n + q + 1)
                dve.wait_ge(added, 10 * n + q + 1)
                v = wts[:, :, iy:iy + HATS, ix:ix + HATS]
                nc.vector.tensor_tensor(v, v, outer[:, q % 2], ALU.add).then_inc(added, 1)

            def leave_part(n, k, i):
                dve.wait_ge(part_cast, 2 * K * n + K * i + k + 1)
                nc.vector.tensor_tensor(weight_view(k) if i == 0 else part_view(2, k), weight_view(k), part_view(i, k), ALU.subtract).then_inc(part_left, 1)

            def finish_output(n, o):
                dve.wait_ge(out_filled, K * n + o + 1)
                dve.wait_ge(res_loaded, 16 * n + 16)
                nc.vector.scalar_tensor_tensor(res[:, o, :], out_ps[:, :], vec[:, 0, o:o + 1], res[:, o, :], ALU.add, ALU.add).then_inc(out_ready, 1)

            def run(n, u, has_prev, has_1, has_2):
                dve.wait_ge(img_loaded[u], 16 * ((n + 2) // 2) if isinstance(n, int) else 8 * (n - u) + 16)
                for i in range(NP):
                    k, pair = divmod(i, PAIRS)
                    d0 = 2 * pair
                    ds = [d for d in (d0, d0 + 1) if d < D]
                    at = [(d // WIN) * PADW + d % WIN for d in ds]
                    dve.wait_ge(spread_ready, NP * n + i + 1)
                    if pair in PE_PAIRS:
                        c = len(PE_PAIRS) * k + PE_PAIRS.index(pair)
                        wait(dve, pe_summed, K * len(PE_PAIRS) * n + c - PROD_BUF + 1)
                        dst = prod[:, c % PROD_BUF, 0:len(ds), :]
                    elif pair == POOL_PAIRS[0]:
                        wait(dve, last_summed, K * n + k - 1)
                        dst = sums_pool[:, k % 2]
                    else:
                        c = ADDS * k + POOL_PAIRS.index(pair) - 1
                        wait(dve, pool_summed, pool_number(n, c - POOL_BUF))
                        dst = prod_pool[:, c % POOL_BUF]
                    nc.vector.tensor_tensor(
                        dst.rearrange("p a (r c) -> p a r c", c=IMG),
                        spread[:, i % 2, 0:len(ds), :].rearrange("p a (r c) -> p a r c", c=IMG),
                        window(u, k, at), ALU.mult).then_inc(multiplied, 1)
                    if has_1 and i in LEAVE_AT:
                        leave_part(n + 1, *divmod(LEAVE_AT.index(i), 2))
                    if has_prev and i in OUT_DONE_AT:
                        finish_output(n - 1, OUT_DONE_AT.index(i))
                    if has_2 and i == CLEAR_AT:
                        clear_window(n + 2)
                    if has_2 and i in ADD_AT:
                        add_point(n + 2, ADD_AT.index(i))

            def window(u, k, at):
                base = img[:, u, k, at[0]:at[0] + 1]
                steps = [[at[1] - at[0], 2]] if len(at) == 2 else [[1, 1]]
                return bass.AP(tensor=base.tensor, offset=base.offset, ap=[list(base.ap[0])] + steps + [[PADW, ROWS], [1, IMG]])

            def weights(n):
                clear_window(n)
                for q in range(PTS):
                    add_point(n, q)

            dve.wait_ge(sel_ready, 2)
            weights(0)
            for k in range(K):
                for i in range(2):
                    leave_part(0, k, i)
            weights(1)
            units(dve, run)
            for o in range(K):
                finish_output(CH - 1, o)

        @block.tensor
        def _(pe):
            def transpose_block(n, i):
                k, blk = divmod(i, BLOCKS)
                rows = block_rows(blk)
                if blk == 0:
                    pe.wait_ge(part_left, 2 * K * n + 2 * k + 2)
                wait(pe, wtt_ready, NB * n + i)
                for t in range(TT):
                    mm = nc.tensor.transpose(tps[0:rows, t * P:(t + 1) * P], wtp[:, t, k, blk * PER_BLOCK * ROWD:blk * PER_BLOCK * ROWD + rows], identb[:, :])
                mm.then_inc(transposed, 1)

            def spread_pair(n, i):
                k, pair = divmod(i, PAIRS)
                blk = 2 * pair // PER_BLOCK
                rows = block_rows(blk)
                pe.wait_ge(wtt_ready, NB * n + k * BLOCKS + blk + 1)
                wait(pe, multiplied, NP * n + i - 1)
                for a, d in enumerate(d for d in (2 * pair, 2 * pair + 1) if d < D):
                    mm = nc.tensor.matmul(spread[:, i % 2, a, :], sel[0:rows, d % PER_BLOCK, :], wtt[0:rows, k, blk, :], start=True, stop=True)
                mm.then_inc(spread_ready, 1)

            def sum_pair(n, i):
                k, pair = divmod(i, PAIRS)
                c = len(PE_PAIRS) * k + PE_PAIRS.index(pair)
                pe.wait_ge(multiplied, NP * n + i + 1)
                if pair == 0:
                    wait(pe, acc_read, K * n + k - 1)
                for a, d in enumerate(d for d in (2 * pair, 2 * pair + 1) if d < D):
                    mm = nc.tensor.matmul(acc[:, k % 2, :], ident[:, :], prod[:, c % PROD_BUF, a, :], start=d == 0, stop=False)
                mm.then_inc(pe_summed, 1)

            def last_sum(n, k):
                pe.wait_ge(pool_summed, pool_number(n, ADDS * (k + 1) - 1))
                for a in range(2):
                    mm = nc.tensor.matmul(acc[:, k % 2, :], ident[:, :], sums_pool[:, k % 2, a, :], start=False, stop=a == 1)
                mm.then_inc(last_summed, 1)

            def project_out(n, o, k):
                if k == 0:
                    pe.wait_ge(acc_read, K * n + K)
                    wait(pe, out_ready, K * n + o)
                mm = nc.tensor.matmul(out_ps[:, :], w[:, k, o * P:(o + 1) * P], dcn[:, k, :], start=k == 0, stop=k == K - 1)
                if k == K - 1:
                    mm.then_inc(out_filled, 1)

            def run(n, u, has_prev, has_1, has_2):
                for i in range(NP):
                    k, pair = divmod(i, PAIRS)
                    if i + 2 < NP:
                        spread_pair(n, i + 2)
                    elif has_1:
                        spread_pair(n + 1, i + 2 - NP)
                    if pair in PE_PAIRS:
                        sum_pair(n, i)
                    if pair == LAST_SUM_AT:
                        if k > 0:
                            last_sum(n, k - 1)
                        elif has_prev:
                            last_sum(n - 1, K - 1)
                    if has_prev and i in OUT_AT:
                        project_out(n - 1, *divmod(OUT_AT.index(i), K))
                    if has_1 and (pair % (PER_BLOCK // 2) == PER_BLOCK // 2 - 1 or pair == PAIRS - 1):
                        transpose_block(n + 1, k * BLOCKS + pair // (PER_BLOCK // 2))

            pe.wait_ge(consts, 64)
            pe.wait_ge(sel_ready, 2)
            for i in range(NB):
                transpose_block(0, i)
            spread_pair(0, 0)
            spread_pair(0, 1)
            units(pe, run)
            last_sum(CH - 1, K - 1)
            for o in range(K):
                for k in range(K):
                    project_out(CH - 1, o, k)


CORNERS = 4
CG = C // G
PIX = PADW * PADW


def phase_sample_any(nc, sem, x2, xproj, offsets, masks, peak, table, out, vectors, w_out, ident_mat, grid_tab):
    with ExitStack() as ctx:
        sb = lambda n, s, d: ctx.enter_context(nc.sbuf_tensor(n, s, d))
        pb = lambda n, s, d: ctx.enter_context(nc.psum_tensor(n, s, d))
        TILES = B * HW // P
        PX = 100
        GRID = 2 * PTS + G + 2 * TILES
        peaks = sb("g_peaks", [P, B * NT], F32)
        top = sb("g_top", [P, 2], F32)
        flag = sb("g_flag", [P, 1], I32)
        consts = sem("g_consts")
        peak_step = sem("g_peak_step")

        with nc.Block() as block:
            @block.sync
            def _(sp):
                sp.dma_start(peaks[:, :], peak).then_inc(consts, 16)

            @block.vector
            def _(dve):
                dve.wait_ge(consts, 16)
                nc.vector.tensor_reduce(top[:, 0:1], peaks[:, :], AX.X, ALU.max).then_inc(peak_step, 1)
                dve.wait_ge(peak_step, 2)
                nc.vector.tensor_scalar(flag[:, :], top[:, 1:2], 2.0, None, ALU.is_gt).then_inc(peak_step, 1)

            @block.gpsimd
            def _(pool):
                pool.wait_ge(peak_step, 1)
                nc.gpsimd.partition_all_reduce(top[:, 1:2], top[:, 0:1], P, bass.bass_isa.ReduceOp.max).then_inc(peak_step, 1)

        vec = sb("g_vec", [P, 1, K], F32)
        w = sb("g_w", [P, K, C], F32)
        ident = sb("g_ident", [P, P], F32)
        grid = sb("g_grid", [P, GRID], F32)
        img = sb("g_img", [P, PIX], F32)
        tr = sb("g_tr", [PX, P], F32)
        off = sb("g_off", [P, NOFF], F32)
        msk = sb("g_msk", [P, NMASK], F32)
        pos = sb("g_pos", [P, 2, NMASK], F32)
        low = sb("g_low", [P, 2, NMASK], F32)
        lowi = sb("g_lowi", [P, 2, NMASK], I32)
        over = sb("g_over", [P, 2, NMASK], F32)
        cw = sb("g_cw", [P, CORNERS, NMASK], F32)
        row = sb("g_row", [P, NMASK], F32)
        cwg = sb("g_cwg", [P, CORNERS, PTS], F32)
        rowg = sb("g_rowg", [P, CORNERS, PTS], I32)
        got = sb("g_got", [P, CORNERS * PTS, CG], F32)
        sampled = sb("g_sampled", [P, C], F32)
        dcn = sb("g_dcn", [P, K, P], F32)
        res = sb("g_res", [P, K, P], F32)
        ps = pb("g_ps", [P, T], F32)
        img_loaded = sem("g_img_loaded")
        tr_ready = sem("g_tr_ready")
        tr_copied = sem("g_tr_copied")
        table_stored = sem("g_table_stored")
        table_done = sem("g_table_done")
        tile_loaded = sem("g_tile_loaded")
        step = sem("g_step")
        rows_ready = sem("g_rows_ready")
        gathered = sem("g_gathered")
        turns = sem("g_turns")
        group_gathered = sem("g_group_gathered")
        cwg_ready = sem("g_cwg_ready")
        products = sem("g_products")
        group_done = sem("g_group_done")
        flipped = sem("g_flipped")
        flip_copied = sem("g_flip_copied")
        out_filled = sem("g_out_filled")
        out_ready = sem("g_out_ready")
        stored = sem("g_stored")
        block = ctx.enter_context(nc.Block())
        STEPS = 16
        outv = out.rearrange("b (k p) h w -> p (b k) (h w)", p=P)

        table_v = table.rearrange("(g q) c -> q g c", q=PIX)

        @block.sync
        def _(sp):
            with sp.If(sp.value_load(flag[0:1, 0:1], min_val=0, max_val=1) > 0):
                sp.sem_inc(table_done, 1)
                for dst, src in ((vec[:, :, :], vectors[:, OUT_B:OUT_B + 1, :]), (w[:, :, :], w_out), (ident[:, :], ident_mat), (grid[:, :], grid_tab)):
                    sp.dma_start(dst, src).then_inc(consts, 16)
                with sp.Fori(0, SEQ) as r:
                    sp.wait_ge(tr_ready, (PIX // PX) * r + 1)
                    sp.dma_start(img[:, :], xproj[:, bass.ds(r, 1), :].rearrange("p o t -> p (o t)")).then_inc(img_loaded, 16)
                    with sp.Fori(0, PIX // PX) as i:
                        sp.wait_ge(tr_copied, r * (PIX // PX) + i + 2)
                        sp.dma_start(table_v[bass.ds(i * PX, PX), bass.ds(r * GK, GK), :], tr[:, :].rearrange("q (g c) -> q g c", c=CG)).then_inc(table_stored, 16)
                        sp.wait_ge(table_stored, (r * (PIX // PX) + i) * 16 + 16)
                        sp.sem_inc(table_done, 1)
                with sp.Fori(0, TILES) as n:
                    slabs = sp.snap((n // (HW // P)) * K)
                    pixels = sp.snap((n % (HW // P)) * P)
                    sp.wait_ge(out_ready, K * n + 1)
                    sp.dma_start(off[:, :], offsets[:, bass.ds(n, 1), :].rearrange("p o q -> p (o q)")).then_inc(tile_loaded, 16)
                    sp.dma_start(msk[:, :], masks[:, bass.ds(n, 1), :].rearrange("p o q -> p (o q)")).then_inc(tile_loaded, 16)
                    sp.dma_start(res[:, :, :], x2[:, bass.ds(slabs, K), bass.ds(pixels, P)]).then_inc(tile_loaded, 16)
                    sp.wait_ge(out_ready, K * n + K + 1)
                    sp.dma_start(outv[:, bass.ds(slabs, K), bass.ds(pixels, P)], res[:, :, :]).then_inc(stored, 16)
                    sp.wait_ge(stored, 16 * n + 16)
                    sp.sem_inc(turns, 1)

        @block.tensor
        def _(pe):
            with pe.If(pe.value_load(flag[0:1, 0:1], min_val=0, max_val=1) > 0):
                pe.sem_inc(tr_ready, 1)
                pe.wait_ge(consts, 80)
                with pe.Fori(0, SEQ) as r:
                    pe.wait_ge(img_loaded, 16 * r + 16)
                    for i in range(PIX // PX):
                        pe.wait_ge(tr_copied, r * (PIX // PX) + i + 1)
                        nc.tensor.transpose(ps[0:PX, 0:P], img[:, i * PX:(i + 1) * PX], ident[:, :]).then_inc(tr_ready, 1)
                with pe.Fori(0, TILES) as n:
                    pe.wait_ge(group_done, G * n + G)
                    for k in range(K):
                        pe.wait_ge(flip_copied, K * n + k + 1)
                        if k == 0:
                            pe.wait_ge(out_ready, K * n + 1)
                        nc.tensor.transpose(ps[:, 0:P], sampled[:, k * P:(k + 1) * P], ident[:, :]).then_inc(flipped, 1)
                    pe.wait_ge(flip_copied, K * n + K + 1)
                    for o in range(K):
                        pe.wait_ge(out_ready, K * n + o + 1)
                        for k in range(K):
                            mm = nc.tensor.matmul(ps[:, 0:P], w[:, k, o * P:(o + 1) * P], dcn[:, k, :], start=k == 0, stop=k == K - 1)
                        mm.then_inc(out_filled, 1)

        @block.scalar
        def _(act):
            with act.If(act.value_load(flag[0:1, 0:1], min_val=0, max_val=1) > 0):
                act.sem_inc(tr_copied, 1)
                act.sem_inc(flip_copied, 1)
                with act.Fori(0, SEQ * PIX // PX) as i:
                    act.wait_ge(tr_ready, i + 2)
                    act.wait_ge(table_done, i + 1)
                    nc.scalar.activation(tr[:, :], ps[0:PX, 0:P], ACT.Copy).then_inc(tr_copied, 1)
                with act.Fori(0, TILES) as n:
                    for k in range(K):
                        act.wait_ge(flipped, K * n + k + 1)
                        nc.scalar.activation(dcn[:, k, :], ps[:, 0:P], ACT.Copy).then_inc(flip_copied, 1)

        @block.gpsimd
        def _(pool):
            with pool.If(pool.value_load(flag[0:1, 0:1], min_val=0, max_val=1) > 0):
                pool.sem_inc(group_gathered, 1)
                pool.wait_ge(table_done, SEQ * PIX // PX + 1)
                with pool.Fori(0, TILES) as n:
                    with pool.Fori(0, G) as g:
                        pool.wait_ge(rows_ready, n * G + g + 1)
                        pool.sem_inc(turns, 1)
                        for q in range(CORNERS * PTS):
                            nc.gpsimd.indirect_dma_start(
                                out=got[:, q, :], out_offset=None, in_=table,
                                in_offset=bass.IndirectOffsetOnAxis(ap=rowg[:, q // PTS, q % PTS:q % PTS + 1], axis=0),
                            ).then_inc(gathered, 16)
                        pool.wait_ge(gathered, 16 * CORNERS * PTS)
                        pool.dma_reset(range(gathered.num, gathered.num + 1))
                        pool.sem_clear(gathered)
                        pool.sem_inc(group_gathered, 1)

        @block.vector
        def _(dve):
            with dve.If(dve.value_load(flag[0:1, 0:1], min_val=0, max_val=1) > 0):
                v = nc.vector
                dve.sem_inc(out_ready, 1)
                dve.wait_ge(consts, 80)
                with dve.Fori(0, TILES) as n:
                    done = [0]

                    def link(ins):
                        done[0] += 1
                        ins.then_inc(step, 1)
                        dve.wait_ge(step, STEPS * n + done[0])

                    dve.wait_ge(tile_loaded, 48 * n + 48)
                    for c in range(2):
                        o = off[:, :].rearrange("p (g q c) -> p g q c", q=PTS, c=2)[:, :, :, c]
                        at = grid[:, c * PTS:(c + 1) * PTS].unsqueeze(1).broadcast_to([P, G, PTS])
                        link(v.tensor_tensor(pos[:, c, :].rearrange("p (g q) -> p g q", q=PTS), o, at, ALU.add))
                    tile_y = grid[:, bass.ds(2 * PTS + G + n, 1)].broadcast_to([P, NMASK])
                    link(v.tensor_tensor(pos[:, 1, :], pos[:, 1, :], tile_y, ALU.add))
                    link(v.tensor_scalar(pos[:, :, :], pos[:, :, :], float(REACH - 1), float(REACH + IMG), ALU.max, ALU.min))
                    link(v.tensor_copy(lowi[:, :, :], pos[:, :, :]))
                    link(v.tensor_copy(low[:, :, :], lowi[:, :, :]))
                    link(v.tensor_tensor(over[:, :, :], low[:, :, :], pos[:, :, :], ALU.is_gt))
                    link(v.tensor_tensor(low[:, :, :], low[:, :, :], over[:, :, :], ALU.subtract))
                    link(v.tensor_tensor(pos[:, :, :], pos[:, :, :], low[:, :, :], ALU.subtract))
                    link(v.tensor_tensor(over[:, 1, :], msk[:, :], pos[:, 1, :], ALU.mult))
                    link(v.tensor_tensor(over[:, 0, :], msk[:, :], over[:, 1, :], ALU.subtract))
                    fx = pos[:, 0, :].unsqueeze(1).broadcast_to([P, 2, NMASK])
                    link(v.tensor_tensor(cw[:, 1:4:2, :], over[:, :, :], fx, ALU.mult))
                    link(v.tensor_tensor(cw[:, 0:4:2, :], over[:, :, :], cw[:, 1:4:2, :], ALU.subtract))
                    link(v.scalar_tensor_tensor(row[:, :], low[:, 1, :], float(PADW), low[:, 0, :], ALU.mult, ALU.add))
                    link(v.tensor_tensor(row[:, :].rearrange("p (g q) -> p g q", q=PTS), row[:, :].rearrange("p (g q) -> p g q", q=PTS),
                                         grid[:, 2 * PTS:2 * PTS + G].unsqueeze(2).broadcast_to([P, G, PTS]), ALU.add))
                    tile_row = grid[:, bass.ds(2 * PTS + G + TILES + n, 1)].broadcast_to([P, NMASK])
                    v.tensor_tensor(row[:, :], row[:, :], tile_row, ALU.add).then_inc(step, 1)
                    assert done[0] + 1 == STEPS
                    with dve.Fori(0, G) as g:
                        dve.wait_ge(step, STEPS * n + STEPS)
                        dve.wait_ge(group_gathered, n * G + g + 1)
                        for c, move in enumerate((0, 1, PADW, PADW + 1)):
                            i = v.tensor_scalar(rowg[:, c, :], row[:, bass.ds(g * PTS, PTS)], float(move), None, ALU.add)
                        i.then_inc(rows_ready, 1)
                        i = v.tensor_scalar(cwg[:, :, :], cw[:, :, bass.ds(g * PTS, PTS)], 1.0, None, ALU.mult).then_inc(cwg_ready, 1)
                        dve.wait_ge(cwg_ready, n * G + g + 1)
                        dve.wait_ge(group_gathered, n * G + g + 2)
                        v.tensor_tensor(got[:, :, :], got[:, :, :], cwg[:, :, :].rearrange("p a b -> p (a b)").unsqueeze(2).broadcast_to([P, CORNERS * PTS, CG]),
                                        ALU.mult).then_inc(products, 1)
                        dve.wait_ge(products, n * G + g + 1)
                        v.tensor_reduce(sampled[:, bass.ds(g * CG, CG)], got[:, :, :].rearrange("p a b -> p b a"), AX.X, ALU.add).then_inc(group_done, 1)
                    for o in range(K):
                        dve.wait_ge(out_filled, K * n + o + 1)
                        v.scalar_tensor_tensor(res[:, o, :], ps[:, 0:P], vec[:, 0, o:o + 1], res[:, o, :], ALU.add, ALU.add).then_inc(out_ready, 1)


def build(nc, x, vectors, mvec, w_in, w_conv, w_x, w_dtr, w_dt, w_out, a_log, w_proj, l1_in_w, dw_w, w_om, b_om, l1_out_w,
          ones_mat, group_mat, ident_mat, keep_tab, bc_sel, point_sel, grid_tab, out):
    dram = lambda name, shape: nc.dram_tensor(name, shape, F32, kind="Internal").ap()
    xn = dram("xn_scratch", (P, UNITS, T))
    halo = dram("halo_scratch", (P, UNITS + 1, 3))
    ym = dram("ym_scratch", (P, UNITS, T))
    x2 = dram("x2_scratch", (P, SEQ, HW))
    stats = dram("stats_scratch", (P, SEQ, NT, 6))
    xproj = dram("xproj_scratch", (P, SEQ, PADW * PADW))
    offsets = dram("offsets_scratch", (P, B * HW // P, NOFF))
    masks = dram("masks_scratch", (P, B * HW // P, NMASK))
    peak = dram("peak_scratch", (P, B * NT))
    table = dram("table_scratch", (B * G * PADW * PADW, CG))
    with ExitStack() as ctx:
        sem = lambda name: ctx.enter_context(nc.semaphore(name))
        phase_input_norm(nc, sem, x, xn.rearrange("p (r t) c -> p r (t c)", t=NT), halo, vectors, ones_mat, group_mat)
        phase_mamba(nc, sem, xn, halo, ym, w_in, w_conv, w_x, w_dtr, w_dt, w_out, a_log, mvec, keep_tab, bc_sel, ident_mat)
        phase_project(nc, sem, ym, x, x2, stats, vectors, w_proj, ones_mat)
        phase_offsets(nc, sem, x2, stats, xproj, offsets, masks, peak, vectors, l1_in_w, dw_w, w_om, b_om, ones_mat, group_mat)
        phase_sample(nc, sem, x2, xproj, offsets, masks, out, vectors, l1_out_w, point_sel, ident_mat)
        phase_sample_any(nc, sem, x2, xproj, offsets, masks, peak, table, out, vectors, l1_out_w, ident_mat, grid_tab)


def laid_out(inputs):
    at = np.ascontiguousarray
    l0 = lambda name: np.asarray(inputs["L0_conv_" + name])
    l1 = lambda name: np.asarray(inputs["L1_conv_" + name])
    columns = lambda v: v.reshape(-1, P).T
    rows = lambda m: at(m.reshape(-1, P, m.shape[1]).transpose(1, 0, 2))
    f32 = np.float32
    x_proj = l0("x_proj_w")
    bc_sel = np.zeros((PARTS * 2 * NS, 2 * NS, P), f32)
    for r in range(2 * NS):
        for part in range(PARTS):
            bc_sel[part * 2 * NS + r, r] = 1
    point_sel = np.zeros((PER_BLOCK * ROWD, PER_BLOCK, P), f32)
    for d in range(PER_BLOCK):
        for part in range(PARTS):
            for g in range(GK):
                point_sel[d * ROWD + part * GK + g, d, g * CG:(g + 1) * CG] = 1
    keep = np.ones((P, UNITS), f32)
    keep[:, ::NT] = 0
    group = np.zeros((P, P), f32)
    per = C // 32
    for g in range(P // per):
        group[g * per:(g + 1) * per, g * per:(g + 1) * per] = 1.0 / per
    pixel, point, tile = np.arange(P), np.arange(PTS), np.arange(B * HW // P)
    per_image = HW // P
    grid = np.concatenate([
        (pixel % IMG)[:, None] + (point // 3 - 1)[None] + REACH,
        (pixel // IMG)[:, None] + (point % 3 - 1)[None] + REACH,
        np.broadcast_to(np.arange(G) * PADW * PADW, (P, G)),
        np.broadcast_to((P // IMG) * (tile % per_image), (P, tile.size)),
        np.broadcast_to((tile // per_image) * G * PADW * PADW, (P, tile.size)),
    ], 1).astype(f32)
    return {
        "x": at(np.asarray(inputs["x"])),
        "vectors": at(np.stack([columns(v) for v in (l0("norm_g"), l0("norm_b"), l0("proj_b"), l1("dw_b"), l1("ln_g"), l1("ln_b"), l1("in_b"), l1("out_b"))], 1)),
        "mvec": at(np.concatenate([columns(l0("conv_b")), columns(l0("dt_proj_b")), columns(l0("D_param")), np.broadcast_to(l0("skip_scale")[None], (P, 1))], 1)),
        "w_in": at(l0("in_proj_w").T),
        "w_conv": at(l0("conv_w").T).reshape(-1),
        "w_x": at(np.tile(rows(x_proj[RANK:].T), (1, 1, PARTS))),
        "w_dtr": rows(x_proj[:RANK].T),
        "w_dt": at(l0("dt_proj_w").T),
        "w_out": rows(l0("out_proj_w").T),
        "a_log": rows(l0("A_log")),
        "w_proj": rows(l0("proj_w").T),
        "l1_in_w": rows(l1("in_w")),
        "dw_w": rows(l1("dw_w").reshape(C, 9)),
        "w_om": rows(np.concatenate([l1("off_w"), l1("mask_w")], 1)),
        "b_om": at(np.concatenate([l1("off_b"), l1("mask_b")])),
        "l1_out_w": rows(l1("out_w")),
        "ones_mat": np.full((P, P), 1.0 / C, f32),
        "group_mat": group,
        "ident_mat": np.eye(P, dtype=f32),
        "keep_tab": keep,
        "bc_sel": bc_sel.reshape(PARTS * 2 * NS, -1),
        "point_sel": point_sel.reshape(PER_BLOCK * ROWD, -1),
        "grid_tab": grid,
    }


def kernel(**inputs):
    import concourse.bacc as _bacc
    from concourse.bass_utils import run_bass_kernel_spmd as _run

    nc = _bacc.Bacc("TRN2", target_bir_lowering=False, num_devices=1)
    arrays = laid_out(inputs)
    args = [nc.dram_tensor(f"in_{name}", a.shape, mybir.dt.from_np(a.dtype), kind="ExternalInput").ap() for name, a in arrays.items()]
    out = nc.dram_tensor("out_0_dram", (B, C, IMG, IMG), F32, kind="ExternalOutput").ap()
    build(nc, *args, out)
    r = _run(nc, [{f"in_{name}": a for name, a in arrays.items()}], core_ids=[0])
    return r.results[0]["out_0_dram"]
```
